# Optimizing a Trainium2 kernel written in Bass

```python
import numpy as np
import jax
import jax.numpy as jnp

def _softmax(x, axis=-1):
    return jax.nn.softmax(x, axis=axis)

def _gelu(x):
    return jax.nn.gelu(x, approximate=True)

def _silu(x):
    return jax.nn.silu(x)

def _sigmoid(x):
    return jax.nn.sigmoid(x)

def _layernorm(x, axis=-1, eps=1e-05):
    m = jnp.mean(x, axis=axis, keepdims=True)
    v = jnp.var(x, axis=axis, keepdims=True)
    return (x - m) / jnp.sqrt(v + eps)

def _scatter_add(tgt, idx, src, axis=0):
    return tgt.at[idx].add(src)

def _segment_sum(src, seg, n):
    return jax.ops.segment_sum(src, seg, n)
kernel_name = 'mk_adaln_d1_jaxref_r4_ee35c0'

def setup_inputs(seed: int=0):
    np.random.seed(seed)
    _w = jnp.asarray

    def _L0_attn_setup():
        import jax, jax.numpy as jnp
        import numpy as np
        NUM_HEADS = 16
        HEAD_DIM = 64
        WINDOW_SIZE = 64
        key = jax.random.key(seed)
        ks = jax.random.split(key, 5)
        B, S, D = (1, 1024, 256)
        std = 0.02
        return {'x': jax.random.normal(ks[0], (B, S, D), dtype=jnp.float32), 'Wq': jax.random.normal(ks[1], (D, NUM_HEADS * HEAD_DIM), dtype=jnp.float32) * std, 'Wk': jax.random.normal(ks[2], (D, NUM_HEADS * HEAD_DIM), dtype=jnp.float32) * std, 'Wv': jax.random.normal(ks[3], (D, NUM_HEADS * HEAD_DIM), dtype=jnp.float32) * std, 'Wo': jax.random.normal(ks[4], (NUM_HEADS * HEAD_DIM, D), dtype=jnp.float32) * std}
    _L0_attn_in = _L0_attn_setup()

    def _L0_ffn_setup():
        import jax, jax.numpy as jnp
        import numpy as np
        D_MODEL = 256
        NUM_HEADS = 4
        NUM_EXPERTS = 8
        TOP_K = 2
        D_FF = 256
        EPS = 1e-06

        def _rmsnorm(x, g):
            return x * jax.lax.rsqrt(jnp.mean(x * x, axis=-1, keepdims=True) + EPS) * g

        def _swiglu(x, w1, w2, w3):
            return jax.nn.silu(x @ w1.T) * (x @ w3.T) @ w2.T
        key = jax.random.key(seed)
        ks = jax.random.split(key, 16)
        d, e, f = (D_MODEL, NUM_EXPERTS, D_FF)
        dc = d // 4
        s = 0.02
        return {'X': jax.random.normal(ks[0], (2, 256, d), dtype=jnp.float32), 'g1': jnp.ones((d,), jnp.float32), 'g2': jnp.ones((d,), jnp.float32), 'Wq': jax.random.normal(ks[1], (d, d), jnp.float32) * s, 'Wkc': jax.random.normal(ks[2], (dc, d), jnp.float32) * s, 'Wvc': jax.random.normal(ks[3], (dc, d), jnp.float32) * s, 'Wo': jax.random.normal(ks[4], (d, d), jnp.float32) * s, 'Wr': jax.random.normal(ks[5], (e, d), jnp.float32) * s, 'expert_bias': jnp.zeros((e,), jnp.float32), 'sW1': jax.random.normal(ks[6], (f, d), jnp.float32) * s, 'sW2': jax.random.normal(ks[7], (d, f), jnp.float32) * s, 'sW3': jax.random.normal(ks[8], (f, d), jnp.float32) * s, 'eW1': jax.random.normal(ks[9], (e, f, d), jnp.float32) * s, 'eW2': jax.random.normal(ks[10], (e, d, f), jnp.float32) * s, 'eW3': jax.random.normal(ks[11], (e, f, d), jnp.float32) * s}
    _L0_ffn_in = _L0_ffn_setup()
    _L0_c = _w((lambda *s: np.random.randn(*s).astype(np.float32) * 0.05)(2, 256))
    _L0_wmod = _w((lambda *s: np.random.randn(*s).astype(np.float32) * 0.05)(256, 6 * 256) * 256 ** (-0.5))
    _d = {'L0_attn_x': _L0_attn_in['x'], 'L0_attn_Wq': _L0_attn_in['Wq'], 'L0_attn_Wk': _L0_attn_in['Wk'], 'L0_attn_Wv': _L0_attn_in['Wv'], 'L0_attn_Wo': _L0_attn_in['Wo'], 'L0_ffn_g1': _L0_ffn_in['g1'], 'L0_ffn_g2': _L0_ffn_in['g2'], 'L0_ffn_Wq': _L0_ffn_in['Wq'], 'L0_ffn_Wkc': _L0_ffn_in['Wkc'], 'L0_ffn_Wvc': _L0_ffn_in['Wvc'], 'L0_ffn_Wo': _L0_ffn_in['Wo'], 'L0_ffn_Wr': _L0_ffn_in['Wr'], 'L0_ffn_expert_bias': _L0_ffn_in['expert_bias'], 'L0_ffn_sW1': _L0_ffn_in['sW1'], 'L0_ffn_sW2': _L0_ffn_in['sW2'], 'L0_ffn_sW3': _L0_ffn_in['sW3'], 'L0_ffn_eW1': _L0_ffn_in['eW1'], 'L0_ffn_eW2': _L0_ffn_in['eW2'], 'L0_ffn_eW3': _L0_ffn_in['eW3'], 'L0_c': _L0_c, 'L0_wmod': _L0_wmod}
    _x0 = _d['L0_attn_x']
    _d['L0_attn_x'] = jax.random.normal(jax.random.fold_in(jax.random.key(seed), 1), (2, 2048, 256), dtype=_x0.dtype)
    del _x0
    return _d

def reference(L0_attn_x, L0_attn_Wq, L0_attn_Wk, L0_attn_Wv, L0_attn_Wo, L0_ffn_g1, L0_ffn_g2, L0_ffn_Wq, L0_ffn_Wkc, L0_ffn_Wvc, L0_ffn_Wo, L0_ffn_Wr, L0_ffn_expert_bias, L0_ffn_sW1, L0_ffn_sW2, L0_ffn_sW3, L0_ffn_eW1, L0_ffn_eW2, L0_ffn_eW3, L0_c, L0_wmod):

    def _L0_attn_ref(x, Wq, Wk, Wv, Wo):
        import jax, jax.numpy as jnp
        import numpy as np
        NUM_HEADS = 16
        HEAD_DIM = 64
        WINDOW_SIZE = 64
        B, S, D = x.shape
        H, Dh, W = (NUM_HEADS, HEAD_DIM, WINDOW_SIZE)
        q = (x @ Wq).reshape(B, S, H, Dh)
        k = (x @ Wk).reshape(B, S, H, Dh)
        v = (x @ Wv).reshape(B, S, H, Dh)
        scale = 1.0 / jnp.sqrt(jnp.asarray(Dh, dtype=x.dtype))
        scores = jnp.einsum('bihd,bjhd->bhij', q, k) * scale
        i = jnp.arange(S)[:, None]
        j = jnp.arange(S)[None, :]
        allowed = (j <= i) & (j >= i - W)
        scores = jnp.where(allowed[None, None, :, :], scores, jnp.finfo(scores.dtype).min)
        attn = jax.nn.softmax(scores, axis=-1)
        out = jnp.einsum('bhij,bjhd->bihd', attn, v).reshape(B, S, H * Dh)
        return out @ Wo

    def _L0_ffn_ref(X, g1, g2, Wq, Wkc, Wvc, Wo, Wr, expert_bias, sW1, sW2, sW3, eW1, eW2, eW3):
        import jax, jax.numpy as jnp
        import numpy as np
        D_MODEL = 256
        NUM_HEADS = 4
        NUM_EXPERTS = 8
        TOP_K = 2
        D_FF = 256
        EPS = 1e-06

        def _rmsnorm(x, g):
            return x * jax.lax.rsqrt(jnp.mean(x * x, axis=-1, keepdims=True) + EPS) * g

        def _swiglu(x, w1, w2, w3):
            return jax.nn.silu(x @ w1.T) * (x @ w3.T) @ w2.T
        B, S, d = X.shape
        H = NUM_HEADS
        dk = d // H
        scale = 1.0 / jnp.sqrt(jnp.float32(dk))
        nx = _rmsnorm(X, g1)
        Q = (nx @ Wq.T).reshape(B, S, H, dk).transpose(0, 2, 1, 3)
        Kc = nx @ Wkc.T
        Vc = nx @ Wvc.T
        scores = jnp.einsum('bhsd,btd->bhst', Q, Kc) * scale
        attn = jax.nn.softmax(scores, axis=-1)
        out = jnp.einsum('bhst,btd->bhsd', attn, Vc)
        out = out.transpose(0, 2, 1, 3).reshape(B, S, d) @ Wo.T
        X = X + out
        nx = _rmsnorm(X, g2)
        xf = nx.reshape(-1, d)
        logits = xf @ Wr.T + expert_bias
        rw = jax.nn.softmax(logits, axis=-1)
        topw, topi = jax.lax.top_k(rw, TOP_K)
        topw = jax.nn.softmax(topw, axis=-1)
        combine = jnp.sum(jax.nn.one_hot(topi, NUM_EXPERTS, dtype=xf.dtype) * topw[..., None], axis=1)
        shared = _swiglu(xf, sW1, sW2, sW3)
        h = jax.nn.silu(jnp.einsum('td,efd->etf', xf, eW1)) * jnp.einsum('td,efd->etf', xf, eW3)
        eo = jnp.einsum('etf,edf->etd', h, eW2)
        specialist = jnp.einsum('te,etd->td', combine, eo)
        moe_out = (shared + specialist).reshape(B, S, d)
        return X + moe_out
    x = L0_attn_x
    mod = (_silu(L0_c) @ L0_wmod).reshape(L0_c.shape[0], 6, 1, -1)
    sa, ca, ga, sb, cb, gb = (mod[:, 0], mod[:, 1], mod[:, 2], mod[:, 3], mod[:, 4], mod[:, 5])
    ga = (2 * (ga >= 0) - 1) * jnp.maximum(jnp.abs(ga), 0.25)
    gb = (2 * (gb >= 0) - 1) * jnp.maximum(jnp.abs(gb), 0.25)
    h = _layernorm(x, axis=-1) * (1 + ca) + sa
    x = x + ga * _L0_attn_ref(h, L0_attn_Wq, L0_attn_Wk, L0_attn_Wv, L0_attn_Wo)
    h = _layernorm(x, axis=-1) * (1 + cb) + sb
    x = x + gb * _L0_ffn_ref(h, L0_ffn_g1, L0_ffn_g2, L0_ffn_Wq, L0_ffn_Wkc, L0_ffn_Wvc, L0_ffn_Wo, L0_ffn_Wr, L0_ffn_expert_bias, L0_ffn_sW1, L0_ffn_sW2, L0_ffn_sW3, L0_ffn_eW1, L0_ffn_eW2, L0_ffn_eW3)
    return x

_drawn_inputs = setup_inputs


def setup_inputs(seed=0):
    import zlib

    import numpy as np

    out = dict(_drawn_inputs(seed))
    spreads = {'L0_ffn_g1': (1.0, 0.6), 'L0_ffn_g2': (1.0, 0.6), 'L0_ffn_expert_bias': (0.0, 0.8)}
    factors = {'L0_attn_Wq': 8.0,
     'L0_attn_Wk': 8.0,
     'L0_attn_Wv': 8.0,
     'L0_attn_Wo': 8.0,
     'L0_ffn_Wq': 8.0,
     'L0_ffn_Wkc': 8.0,
     'L0_ffn_Wvc': 8.0,
     'L0_ffn_Wo': 8.0,
     'L0_ffn_Wr': 8.0,
     'L0_ffn_sW1': 8.0,
     'L0_ffn_sW2': 8.0,
     'L0_ffn_sW3': 8.0,
     'L0_ffn_eW1': 8.0,
     'L0_ffn_eW2': 8.0,
     'L0_ffn_eW3': 8.0}
    for name, (base, spread) in spreads.items():
        noise = np.random.default_rng([zlib.crc32(name.encode()), seed]).standard_normal(out[name].shape)
        drawn = base * np.exp(spread * noise) if base else spread * noise
        out[name] = jnp.asarray(drawn.astype(out[name].dtype))
    for name, factor in factors.items():
        out[name] = (out[name] * factor).astype(out[name].dtype)
    return out
```

```python
from contextlib import ExitStack

import concourse.bass as bass
from concourse import mybir

ALU = mybir.AluOpType
ACT = mybir.ActivationFunctionType
AX = mybir.AxisListType
F32 = mybir.dt.float32
F32R = mybir.dt.float32r
BF16 = mybir.dt.bfloat16

P = 128
D = 256
KD = D // P
NB = 2
SEQ = 2048
TOK = NB * SEQ
CH = 512
CT = CH // P
NC = SEQ // CH
NT = SEQ // P
EPS_LN = 1e-5
EPS_RMS = 1e-6

H1 = 16
DH = 64
WIN = 64
HP = H1 // 2
KW = WIN + P
NEG = -3.0e38

H2 = 4
KT = SEQ // P

NE = 8
FF = 256
KF = FF // P


class PhaseSemaphores:

    def __init__(self, nc):
        self.nc, self.taken = nc, []

    def __enter__(self):
        return self

    def take(self, name):
        self.taken.append(self.nc.alloc_semaphore(name))
        return self.taken[-1]

    def __exit__(self, *failure):
        if failure[0] is None:
            self.nc.all_engine_barrier()
            self.nc.clear_and_free_semaphores(self.taken)
            self.nc.all_engine_barrier()


def modulation_rows(nc, sems, block_name, ctx, A, rows, bc, plus_one):
    sb = lambda n, s, d: ctx.enter_context(nc.sbuf_tensor(block_name + n, s, d))
    c_raw = sb("c_raw", [P, KD, NB], F32)
    c_silu = sb("c_silu", [P, KD, NB], F32)
    c_wide = sb("c_wide", [P, KD, NB, P], F32)
    wmod = sb("wmod", [P, KD, len(rows), D], F32)
    ps = [ctx.enter_context(nc.psum_tensor(f"{block_name}mod_ps{i}", [P, 512], F32)) for i in range(2)]
    s_in, s_silu, s_wide, s_mm, s_out = (
        sems.take(block_name + n) for n in ("mod_in", "mod_silu", "mod_wide", "mod_mm", "mod_out"))

    def load(sp):
        sp.dma_start(c_raw[:], A["cT"]).then_inc(s_in, 16)
        for j, row in enumerate(rows):
            sp.dma_start(wmod[:, :, j, :], A["wmod"][:, :, row, :]).then_inc(s_in, 16)

    def scalar(act):
        act.wait_ge(s_in, 16 * (1 + len(rows)))
        nc.scalar.activation(c_silu[:], c_raw[:], ACT.Silu).then_inc(s_silu, 1)

    def tensor(pe):
        pe.wait_ge(s_wide, 1)
        n = 0
        for j in range(len(rows)):
            for b in range(NB):
                if n >= 2:
                    pe.wait_ge(s_out, n - 1)
                for k in range(KD):
                    mm = nc.tensor.matmul(ps[n % 2][:, 0:D], c_wide[:, k, b, :], wmod[:, k, j, :],
                                          start=(k == 0), stop=(k == KD - 1))
                mm.then_inc(s_mm, 1)
                n += 1

    def vector(dve):
        dve.wait_ge(s_silu, 1)
        nc.vector.tensor_copy(c_wide[:].rearrange("p k b m -> p (k b) m"),
                              c_silu[:].rearrange("p k (b o) -> p (k b) o", o=1).to_broadcast([P, KD * NB, P])
                              ).then_inc(s_wide, 1)
        n = 0
        for j in range(len(rows)):
            for b in range(NB):
                dve.wait_ge(s_mm, n + 1)
                add = 1.0 if plus_one[j] else 0.0
                nc.vector.tensor_scalar(bc[:, j, b, :], ps[n % 2][:, 0:D], add, None, ALU.add).then_inc(s_out, 1)
                n += 1

    return load, scalar, tensor, vector, (s_out, n_of(rows))


def floor_gate(nc, dve, gate, size, s_g):
    nc.vector.tensor_scalar(size, gate, -1.0, 0.25, ALU.mult, ALU.max).then_inc(s_g, 1)
    dve.wait_ge(s_g, 1)
    nc.vector.tensor_tensor(size, size, gate, ALU.max).then_inc(s_g, 1)
    dve.wait_ge(s_g, 2)
    nc.vector.tensor_scalar(gate, gate, 0.0, 2.0, ALU.is_ge, ALU.mult).then_inc(s_g, 1)
    dve.wait_ge(s_g, 3)
    nc.vector.tensor_scalar(gate, gate, -1.0, None, ALU.add).then_inc(s_g, 1)
    dve.wait_ge(s_g, 4)
    nc.vector.tensor_tensor(gate, gate, size, ALU.mult).then_inc(s_g, 1)


def n_of(rows):
    return NB * len(rows)


def newton_rsqrt(nc, dve, root, var, scratch, wait, done):
    nc.vector.tensor_tensor(scratch, root, root, ALU.mult).then_inc(done, 1)
    wait(1)
    nc.vector.scalar_tensor_tensor(out=scratch, in0=var, scalar=-0.5, in1=scratch, op0=ALU.mult, op1=ALU.mult).then_inc(done, 1)
    wait(2)
    nc.vector.scalar_tensor_tensor(out=root, in0=scratch, scalar=1.5, in1=root, op0=ALU.add, op1=ALU.mult).then_inc(done, 1)
    wait(3)


def windowed_attention(nc, sems, A, x1):
    with ExitStack() as ctx:
        sb = lambda n, s, d: ctx.enter_context(nc.sbuf_tensor("wa_" + n, s, d))
        bank = lambda n: ctx.enter_context(nc.psum_tensor("wa_" + n, [P, 512], F32))
        wqkv = [sb(f"wqkv{s}", [P, KD, 3 * H1 * DH], F32R) for s in ("hi", "lo")]
        wo = [sb(f"wo{s}", [P, H1, D], F32R) for s in ("hi", "lo")]
        ident = sb("ident", [P, P], F32)
        mask = sb("mask", [P, NC, KW], BF16)
        mask0 = sb("mask0", [P, KW], BF16)
        bc = sb("bc", [P, 3, NB, D], F32)
        gate_abs = sb("gate_abs", [P, NB, D], F32)

        with ExitStack() as c2:
            raw = c2.enter_context(nc.sbuf_tensor("wa_raw", [P, KD * 3 * H1 * DH], F32))
            raw_o = c2.enter_context(nc.sbuf_tensor("wa_raw_o", [P, H1 * D], F32))
            sem = lambda n: sems.take("wa0_" + n)
            s_w, s_hi, s_lo, s_id, s_m, s_g = (sem(n) for n in ("w", "hi", "lo", "id", "m", "g"))
            load, mscalar, mtensor, mvector, (s_bc, n_bc) = modulation_rows(
                nc, sems, "wa0_", c2, A, (0, 1, 2), bc, (False, True, False))
            block = c2.enter_context(nc.Block())
            parts = [(raw[:, i * 1536:(i + 1) * 1536],
                      [w[:].rearrange("p k n -> p (k n)")[:, i * 1536:(i + 1) * 1536] for w in wqkv]) for i in range(4)]
            parts += [(raw_o[:, i * 2048:(i + 1) * 2048],
                       [w[:].rearrange("p h n -> p (h n)")[:, i * 2048:(i + 1) * 2048] for w in wo]) for i in range(2)]

            @block.sync
            def _(sp):
                load(sp)
                for i in range(4):
                    sp.dma_start(raw[:, i * 1536:(i + 1) * 1536],
                                 A["wqkv"].rearrange("p k n -> p (k n)")[:, i * 1536:(i + 1) * 1536]).then_inc(s_w, 16)
                    sp.wait_ge(s_w, 16 * (i + 1))
                wo_h = A["wo"].rearrange("p h n -> p (h n)")
                for i in range(2):
                    for half in range(2):
                        sp.dma_start(raw_o[64 * half:64 * half + 64, i * 2048:(i + 1) * 2048],
                                     wo_h[:, i * 2048:(i + 1) * 2048]).then_inc(s_w, 16)
                    sp.wait_ge(s_w, 16 * (6 + 2 * i))

            @block.scalar
            def _(act):
                mscalar(act)
                for i, (src, (hi, lo)) in enumerate(parts):
                    act.wait_ge(s_w, 16 * (i + 1 if i < 4 else 6 + 2 * (i - 4)))
                    nc.scalar.copy(hi, src).then_inc(s_hi, 1)

            @block.vector
            def _(dve):
                mvector(dve)
                dve.wait_ge(s_bc, n_bc)
                ga = bc[:, 2, :, :]
                floor_gate(nc, dve, ga, gate_abs[:], s_g)
                for i, (src, (hi, lo)) in enumerate(parts):
                    dve.wait_ge(s_hi, i + 1)
                    nc.vector.tensor_tensor(lo, src, hi.bitcast(F32), ALU.subtract).then_inc(s_lo, 1)

            @block.tensor
            def _(pe):
                mtensor(pe)

            @block.gpsimd
            def _(pool):
                nc.gpsimd.memset(ident[:], 0.0).then_inc(s_id, 1)
                nc.gpsimd.memset(mask[:], 0.0).then_inc(s_m, 1)
                pool.wait_ge(s_id, 1)
                nc.gpsimd.affine_select(out=ident[:], in_=ident[:], compare_op=ALU.not_equal, fill=1.0, base=0,
                                        pattern=[[-1, P]], channel_multiplier=1).then_inc(s_id, 1)
                pool.wait_ge(s_m, 1)
                nc.gpsimd.affine_select(out=mask[:], in_=mask[:], compare_op=ALU.is_ge, fill=NEG, base=0,
                                        pattern=[[0, NC], [1, KW]], channel_multiplier=-1).then_inc(s_m, 1)
                pool.wait_ge(s_m, 2)
                nc.gpsimd.affine_select(out=mask[:], in_=mask[:], compare_op=ALU.is_ge, fill=NEG, base=WIN,
                                        pattern=[[0, NC], [-1, KW]], channel_multiplier=1).then_inc(s_m, 1)
                pool.wait_ge(s_m, 3)
                nc.gpsimd.memset(mask[:, 0, 0:WIN], NEG).then_inc(s_m, 1)
                pool.wait_ge(s_m, 4)

        xa = sb("xa", [P, CT, D], F32)
        xr = sb("xr", [P, CT, D], F32)
        stats = sb("stats", [P, CT, 6], F32)
        mv = sb("mv", [P, CT, 2], F32)
        rstd = sb("rstd", [P, CT], F32)
        var = sb("var", [P, CT], F32)
        newton = sb("newton", [P, CT], F32)
        hT = [sb(f"hT{s}", [P, KD, CH], F32R) for s in ("hi", "lo")]
        v_st = sb("v_st", [P, CT + 1, H1, P], F32R)
        kk = [sb(f"k{s}", [P, 2, WIN + CH], F32R) for s in ("hi", "lo")]
        k_halo = [sb(f"k_halo{s}", [P, HP, 2, WIN], F32R) for s in ("hi", "lo")]
        q_st = sb("q_st", [P, 2, CH], F32R)
        RING = 6
        prob = sb("prob", [P, RING, 2, 2 * P], F32)
        nmax = sb("nmax", [P, RING, 2], F32)
        rsum = sb("rsum", [P, RING, 2], F32)
        rinv = sb("rinv", [P, RING, 2], F32)
        PTW = (CT + 1) * KW
        pT = [sb(f"pT{s}", [P, 2, PTW], F32R) for s in ("hi", "lo")]
        oT = [sb(f"oT{s}", [P, 2, CH], F32R) for s in ("hi", "lo")]

        b_q, b_k = bank("b_q"), bank("b_k")
        b_s = [bank("b_s0"), bank("b_s1")]
        b_t, b_o = bank("b_t"), bank("b_o")
        b_wo = [bank("b_wo0"), bank("b_wo1")]

        names = ("nwt x xr bn ag var sd rs xn hm h hT hhi hlo vp vhi vlo vhalo s ttr exp rc pn t thi tlo pv ohi olo wo "
                 "pq pk qhi qlo khi klo kdup krest ksave mask res1 res2 out init carrier").split()
        S = {n: sems.take("wa_" + n) for n in names}
        PER = dict(x=16, xr=16, bn=CT, ag=CT, nwt=3, var=1, sd=1, rs=1, xn=CT, hm=CT, h=CT, hT=KD, hhi=KD, hlo=KD,
                   vp=2 * CT, vhi=2 * CT, vlo=2 * CT, vhalo=16, s=HP * CT, ttr=HP * CT, exp=HP * CT, rc=HP * CT,
                   pn=HP * CT, t=HP * CT, thi=HP * CT, tlo=HP * CT, pv=2 * HP, ohi=2 * HP, olo=2 * HP, wo=2 * HP,
                   pq=HP, pk=HP, qhi=HP, qlo=HP, khi=HP, klo=HP, kdup=64 * HP, krest=32 * HP, ksave=32 * HP,
                   mask=1, res1=CT, res2=1, out=16)

        INIT = 8
        block = ctx.enter_context(nc.Block())

        def chunks(eng, body):
            with eng.Fori(0, NB) as b:
                with eng.Fori(0, NC) as c:
                    g = b * NC + c

                    def need(name, n, apart=False):
                        eng.wait_ge(S[name], g * PER[name] + max(n, 0))
                        if apart or eng is nc.sync:
                            eng.sem_inc(S["carrier"], 1)
                    body(need, b, c, g)

        def pt_places(t):
            halo = 0 if t == 0 else KW * t + P
            own = KW * CT + WIN if t == CT - 1 else KW * (t + 1)
            if own == halo + WIN:
                return [(0, KW, halo)]
            return [(0, WIN, halo), (WIN, KW, own)]

        BLOCK_AT = [0] + [P * j for j in range(CT - 1)] + [CH - KW]

        @block.sync
        def _(sp):
            def body(need, b, c, g):
                def restore(i):
                    for w in range(2):
                        sp.dma_start(kk[w][:, :, 0:WIN].bitcast(F32), k_halo[w][:, i, :, :].bitcast(F32)).then_inc(S["krest"], 16)

                need("hlo", 0)
                need("h", 0)
                need("hT", 0, apart=True)
                sp.dma_start(xa[:], A["x"][:, bass.ds(g * CT, CT), :]).then_inc(S["x"], 16)
                need("out", 0, apart=True)
                sp.dma_start(xr[:], A["x"][:, bass.ds(g * CT, CT), :]).then_inc(S["xr"], 16)
                need("pv", 0)
                sp.dma_start(v_st[WIN:P, 0, :, :].bitcast(F32), v_st[WIN:P, CT, :, :].bitcast(F32)).then_inc(S["vhalo"], 16)
                for i in range(HP):
                    need("s", CT * i)
                    need("ksave", 32 * i)
                    restore(i)
                    need("khi", i + 1)
                    sp.dma_start(kk[0][64:P, 0, WIN:].bitcast(F32), kk[0][0:64, 0, WIN:].bitcast(F32)).then_inc(S["kdup"], 16)
                    sp.dma_start(kk[0][0:64, 1, WIN:].bitcast(F32), kk[0][64:P, 1, WIN:].bitcast(F32)).then_inc(S["kdup"], 16)
                    need("klo", i + 1)
                    sp.dma_start(kk[1][64:P, 0, WIN:].bitcast(F32), kk[1][0:64, 0, WIN:].bitcast(F32)).then_inc(S["kdup"], 16)
                    sp.dma_start(kk[1][0:64, 1, WIN:].bitcast(F32), kk[1][64:P, 1, WIN:].bitcast(F32)).then_inc(S["kdup"], 16)
                    need("kdup", 64 * (i + 1))
                    need("krest", 32 * (i + 1))
                    for w in range(2):
                        sp.dma_start(k_halo[w][:, i, :, :].bitcast(F32), kk[w][:, :, CH:].bitcast(F32)).then_inc(S["ksave"], 16)
                need("res2", 1, apart=True)
                sp.dma_start(x1[:, bass.ds(g * CT, CT), :], xr[:]).then_inc(S["out"], 16)
            sp.wait_ge(S["init"], INIT)
            chunks(sp, body)
            sp.wait_ge(S["out"], 16 * NB * NC)
            sp.wait_ge(S["ksave"], 32 * HP * NB * NC)

        @block.gpsimd
        def _(pool):
            nc.gpsimd.memset(v_st[:, CT, :, :].bitcast(F32), 0.0).then_inc(S["init"], 1)
            nc.gpsimd.memset(v_st[0:WIN, 0, :, :].bitcast(F32), 0.0).then_inc(S["init"], 1)
            for w in range(2):
                nc.gpsimd.memset(k_halo[w][:].bitcast(F32), 0.0).then_inc(S["init"], 1)
            nc.gpsimd.memset(prob[:, :, :, 0:WIN], 0.0).then_inc(S["init"], 1)
            nc.gpsimd.memset(mask0[:], 0.0).then_inc(S["init"], 1)

            def body(need, b, c, g):
                for t in range(CT):
                    need("xn", t + 1, apart=True)
                    nc.gpsimd.tensor_tensor(xa[:, t, :], xa[:, t, :], bc[:, 1, bass.ds(b, 1), :].rearrange("p o d -> p (o d)"),
                                            ALU.mult).then_inc(S["hm"], 1)
                    need("hm", t + 1, apart=True)
                    nc.gpsimd.tensor_tensor(xa[:, t, :], xa[:, t, :], bc[:, 0, bass.ds(b, 1), :].rearrange("p o d -> p (o d)"),
                                            ALU.add).then_inc(S["h"], 1)
                for i in range(HP):
                    for t in range(CT):
                        r = (CT * i + t) % RING
                        need("rc", CT * i + t + 1, apart=True)
                        for hd in range(2):
                            p = prob[:, r, hd, WIN:]
                            x = nc.gpsimd.tensor_scalar(p, p, rinv[:, r, hd:hd + 1], 1.0, ALU.mult, ALU.mult)
                        x.then_inc(S["pn"], 1)
            pool.wait_ge(S["init"], INIT)
            chunks(pool, body)

        @block.scalar
        def _(act):
            def exp(need, i, t):
                n = CT * i + t
                need("ttr", n + 1)
                for hd in range(2):
                    p = prob[:, n % RING, hd, WIN:]
                    x = nc.scalar.activation(p, p, ACT.Exp, bias=nmax[:, n % RING, hd:hd + 1], scale=-1.0,
                                             accum_out=rsum[:, n % RING, hd:hd + 1])
                x.then_inc(S["exp"], 1)

            def t_hi(need, i, t):
                need("t", CT * i + t + 1)
                need("pv", 2 * i)
                for a, e, at in pt_places(t):
                    x = nc.scalar.copy(pT[0][:, :, at:at + e - a],
                                       b_t[:, 0:2 * KW].rearrange("p (h n) -> p h n", h=2)[:, :, a:e])
                x.then_inc(S["thi"], 1)

            def q_hi(need, i):
                need("pq", i + 1)
                need("s", CT * i)
                nc.scalar.copy(q_st[0:64, 0, :], b_q[0:64, :])
                nc.scalar.copy(q_st[0:64, 1, :], b_q[64:P, :]).then_inc(S["qhi"], 1)

            def k_hi(need, i):
                need("pk", i + 1)
                need("s", CT * i)
                need("ksave", 32 * i)
                nc.scalar.copy(kk[0][0:64, 0, WIN:], b_k[0:64, :])
                nc.scalar.copy(kk[0][64:P, 1, WIN:], b_k[64:P, :]).then_inc(S["khi"], 1)

            def o_hi(need, i, hd):
                need("pv", 2 * i + hd + 1)
                need("wo", 2 * (i - 1) + hd + 1)
                nc.scalar.copy(oT[0][:, hd, :], b_o[:]).then_inc(S["ohi"], 1)

            def body(need, b, c, g):
                need("var", 1)
                nc.scalar.activation(rstd[:], var[:], ACT.Sqrt).then_inc(S["sd"], 1)
                for k in range(KD):
                    need("hT", k + 1)
                    nc.scalar.copy(hT[0][:, k, :], (b_q, b_k)[k][:]).then_inc(S["hhi"], 1)
                for n in range(2 * CT):
                    t, half = n // 2, n % 2
                    need("vp", n + 1)
                    need("vhalo", 16)
                    nc.scalar.copy(v_st[:, t + 1, 8 * half:8 * half + 8, 0:DH],
                                   (b_q, b_k)[half][:].rearrange("p (h n) -> p h n", h=8)).then_inc(S["vhi"], 1)
                q_hi(need, 0)
                k_hi(need, 0)
                for i in range(HP + 1):
                    now, last = i < HP, i > 0
                    if now:
                        exp(need, i, 0)
                        exp(need, i, 1)
                    if last:
                        t_hi(need, i - 1, 0)
                    if now:
                        exp(need, i, 2)
                    if last:
                        t_hi(need, i - 1, 1)
                    if now:
                        exp(need, i, 3)
                    if i + 1 < HP:
                        q_hi(need, i + 1)
                        k_hi(need, i + 1)
                    if last:
                        t_hi(need, i - 1, 2)
                        t_hi(need, i - 1, 3)
                        o_hi(need, i - 1, 0)
                        o_hi(need, i - 1, 1)
            act.wait_ge(S["init"], INIT)
            chunks(act, body)

        @block.vector
        def _(dve):
            for w in range(2):
                nc.vector.memset(pT[w][:].bitcast(F32), 0.0).then_inc(S["init"], 1)
            dve.wait_ge(S["init"], INIT)

            def lo(out, psum, hi, sem=None):
                x = nc.vector.tensor_tensor(out, psum, hi.bitcast(F32), ALU.subtract)
                if sem:
                    x.then_inc(S[sem], 1)

            def ttr(need, i, t):
                n = CT * i + t
                need("s", n + 1)
                need("t", n - RING + 1, apart=True)
                m = mask0[:] if t == 0 else mask[:, 1, :]
                for hd in range(2):
                    x = nc.vector.tensor_tensor_reduce(prob[:, n % RING, hd, WIN:], b_s[t % 2][:, KW * hd:KW * hd + KW], m,
                                                       -float(DH) ** -0.5, 3.4e38, ALU.add, ALU.min,
                                                       nmax[:, n % RING, hd:hd + 1])
                x.then_inc(S["ttr"], 1)

            def recip(need, i, t):
                n = CT * i + t
                need("exp", n + 1)
                nc.vector.reciprocal(rinv[:, n % RING, :], rsum[:, n % RING, :]).then_inc(S["rc"], 1)

            def t_lo(need, i, t):
                need("thi", CT * i + t + 1)
                pl = pt_places(t)
                for a, e, at in pl:
                    lo(pT[1][:, :, at:at + e - a], b_t[:, 0:2 * KW].rearrange("p (h n) -> p h n", h=2)[:, :, a:e],
                       pT[0][:, :, at:at + e - a], "tlo" if (a, e, at) == pl[-1] else None)

            def q_lo(need, i):
                need("qhi", i + 1)
                lo(q_st[64:P, 0, :], b_q[0:64, :], q_st[0:64, 0, :])
                lo(q_st[64:P, 1, :], b_q[64:P, :], q_st[0:64, 1, :], "qlo")

            def k_lo(need, i):
                need("khi", i + 1)
                lo(kk[1][0:64, 0, WIN:], b_k[0:64, :], kk[0][0:64, 0, WIN:])
                lo(kk[1][64:P, 1, WIN:], b_k[64:P, :], kk[0][64:P, 1, WIN:], "klo")

            def o_lo(need, i, hd):
                need("ohi", 2 * i + hd + 1)
                lo(oT[1][:, hd, :], b_o[:], oT[0][:, hd, :], "olo")

            def body(need, b, c, g):
                need("x", 16)
                need("ttr", 0)
                nc.vector.tensor_copy(mask0[:], mask[:, bass.ds(c, 1), :].rearrange("p o d -> p (o d)")).then_inc(S["mask"], 1)
                for t in range(CT):
                    nc.vector.bn_stats(stats[:, t, :], xa[:, t, :]).then_inc(S["bn"], 1)
                for t in range(CT):
                    need("bn", t + 1, apart=True)
                    nc.vector.bn_aggr(mv[:, t, :], stats[:, t, :]).then_inc(S["ag"], 1)
                need("ag", CT)
                nc.vector.tensor_scalar(var[:], mv[:, :, 1], EPS_LN, None, ALU.add).then_inc(S["var"], 1)
                need("sd", 1)
                nc.vector.reciprocal(rstd[:], rstd[:]).then_inc(S["rs"], 1)
                need("rs", 1)
                newton_rsqrt(nc, dve, rstd[:], var[:], newton[:], lambda k: need("nwt", k), S["nwt"])
                for t in range(CT):
                    nc.vector.tensor_scalar(xa[:, t, :], xa[:, t, :], mv[:, t, 0:1], rstd[:, t:t + 1],
                                            ALU.subtract, ALU.mult).then_inc(S["xn"], 1)
                for k in range(KD):
                    need("hhi", k + 1)
                    lo(hT[1][:, k, :], (b_q, b_k)[k][:], hT[0][:, k, :], "hlo")
                for n in range(2 * CT):
                    t, half = n // 2, n % 2
                    need("vhi", n + 1)
                    lo(v_st[:, t + 1, 8 * half:8 * half + 8, DH:P], (b_q, b_k)[half][:].rearrange("p (h n) -> p h n", h=8),
                       v_st[:, t + 1, 8 * half:8 * half + 8, 0:DH], "vlo")
                need("mask", 1)
                q_lo(need, 0)
                k_lo(need, 0)
                for i in range(HP + 1):
                    now, last = i < HP, i > 0
                    if now:
                        ttr(need, i, 0)
                        ttr(need, i, 1)
                        recip(need, i, 0)
                        ttr(need, i, 2)
                    if last:
                        t_lo(need, i - 1, 0)
                    if now:
                        recip(need, i, 1)
                        ttr(need, i, 3)
                    if last:
                        t_lo(need, i - 1, 1)
                    if now:
                        recip(need, i, 2)
                    if i + 1 < HP:
                        q_lo(need, i + 1)
                    if now:
                        recip(need, i, 3)
                    if i + 1 < HP:
                        k_lo(need, i + 1)
                    if last:
                        t_lo(need, i - 1, 2)
                        t_lo(need, i - 1, 3)
                        o_lo(need, i - 1, 0)
                        o_lo(need, i - 1, 1)
                need("wo", 2 * HP)
                need("xr", 16)
                for t in range(CT):
                    nc.vector.tensor_tensor(xa[:, t, :], b_wo[t // 2][:, D * (t % 2):D * (t % 2) + D],
                                            bc[:, 2, bass.ds(b, 1), :].rearrange("p o d -> p (o d)"), ALU.mult).then_inc(S["res1"], 1)
                need("res1", CT)
                nc.vector.tensor_tensor(xr[:], xr[:], xa[:], ALU.add).then_inc(S["res2"], 1)
            chunks(dve, body)

        @block.tensor
        def _(pe):
            SPLIT3 = ((0, 0), (0, 1), (1, 0))

            def project(out, col0, need):
                for n, (a, e) in enumerate(SPLIT3):
                    for k in range(KD):
                        x = nc.tensor.matmul(out, wqkv[a][:, k, col0:col0 + P], hT[e][:, k, :],
                                             start=(n == 0 and k == 0), stop=(n == 2 and k == KD - 1))
                return x

            def pq(need, i):
                need("qlo", i)
                project(b_q[:], P * i, need).then_inc(S["pq"], 1)

            def pk(need, i):
                need("klo", i)
                project(b_k[:], H1 * DH + P * i, need).then_inc(S["pk"], 1)

            def scores(need, i, t):
                n = CT * i + t
                if t == 0:
                    need("qlo", i + 1)
                    need("kdup", 64 * (i + 1))
                    need("krest", 32 * (i + 1))
                    need("klo", i + 1)
                need("ttr", n - 1)
                for hd in range(2):
                    for w in range(2):
                        x = nc.tensor.matmul(b_s[t % 2][:, KW * hd:KW * hd + KW], q_st[:, hd, P * t:P * t + P],
                                             kk[w][:, hd, P * t:P * t + KW], start=(w == 0), stop=(w == 1))
                x.then_inc(S["s"], 1)

            def transposes(need, i, t):
                n = CT * i + t
                need("pn", n + 1)
                need("tlo", n, apart=True)
                for hd in range(2):
                    p = prob[:, n % RING, hd, :]
                    nc.tensor.transpose(b_t[:, KW * hd:KW * hd + WIN], p[0:WIN, 0:P], ident[0:WIN, 0:WIN])
                    x = nc.tensor.transpose(b_t[:, KW * hd + WIN:KW * hd + KW], p[:, P:], ident[:])
                x.then_inc(S["t"], 1)

            def pv(need, i, hd):
                need("tlo", CT * (i + 1))
                need("olo", 2 * i + hd)
                for j in range(CT + 1):
                    for w in range(2):
                        x = nc.tensor.matmul(b_o[:, BLOCK_AT[j]:BLOCK_AT[j] + KW], v_st[:, j, 2 * i + hd, :],
                                             pT[w][:, hd, KW * j:KW * j + KW], start=(j == 0 and w == 0),
                                             stop=(j == CT and w == 1), skip_group_check=True)
                x.then_inc(S["pv"], 1)

            def out_proj(need, i, hd, ts):
                need("olo", 2 * i + hd + 1)
                for t in ts:
                    for n, (a, e) in enumerate(SPLIT3):
                        first = i == 0 and hd == 0 and n == 0
                        x = nc.tensor.matmul(b_wo[t // 2][:, D * (t % 2):D * (t % 2) + D], oT[a][:, hd, P * t:P * t + P],
                                             wo[e][:, 2 * i + hd, :], start=(first and t % 2 == 0),
                                             stop=(i == HP - 1 and hd == 1 and n == 2), skip_group_check=True)
                if ts[-1] == CT - 1:
                    x.then_inc(S["wo"], 1)

            def body(need, b, c, g):
                for k in range(KD):
                    need("h", CT)
                    need("klo", 0)
                    need("qlo", 0)
                    for t in range(CT):
                        x = nc.tensor.transpose((b_q, b_k)[k][:, P * t:P * t + P], xa[:, t, P * k:P * k + P], ident[:])
                    x.then_inc(S["hT"], 1)
                need("hlo", KD)
                for n in range(2 * CT):
                    t, half = n // 2, n % 2
                    need("vlo", n - 1)
                    for m, (a, e) in enumerate(SPLIT3):
                        for k in range(KD):
                            x = nc.tensor.matmul((b_q, b_k)[half][:], hT[a][:, k, P * t:P * t + P],
                                                 wqkv[e][:, k, 2 * H1 * DH + 512 * half:2 * H1 * DH + 512 * half + 512],
                                                 start=(m == 0 and k == 0), stop=(m == 2 and k == KD - 1))
                    x.then_inc(S["vp"], 1)
                need("vlo", 2 * CT)
                need("res2", 0)
                pq(need, 0)
                pk(need, 0)
                for i in range(HP + 2):
                    now, last, before = i < HP, 0 < i <= HP, i > 1
                    if now:
                        scores(need, i, 0)
                        scores(need, i, 1)
                    if before:
                        out_proj(need, i - 2, 0, [0, 1, 2, 3])
                    if now:
                        scores(need, i, 2)
                    if last:
                        transposes(need, i - 1, 0)
                    if now:
                        scores(need, i, 3)
                    if last:
                        transposes(need, i - 1, 1)
                    if i + 1 < HP:
                        pq(need, i + 1)
                        pk(need, i + 1)
                    if last:
                        transposes(need, i - 1, 2)
                        transposes(need, i - 1, 3)
                    if before:
                        out_proj(need, i - 2, 1, [0, 1])
                    if last:
                        pv(need, i - 1, 0)
                    if before:
                        out_proj(need, i - 2, 1, [2, 3])
                    if last:
                        pv(need, i - 1, 1)
            pe.wait_ge(S["init"], INIT)
            chunks(pe, body)



SPLIT3 = ((0, 0), (0, 1), (1, 0))


def split_weights(nc, sems, name, sources):
    s_w, s_hi, s_lo = (sems.take(f"{name}_{n}") for n in ("raw", "hi", "lo"))
    loads = sum(len(src[0]) for src in sources)

    def load(sp):
        for drams, raw, hi, lo in sources:
            for dram, at in drams:
                sp.dma_start(at, dram).then_inc(s_w, 16)

    def scalar(act):
        act.wait_ge(s_w, 16 * loads)
        for drams, raw, hi, lo in sources:
            nc.scalar.copy(hi, raw).then_inc(s_hi, 1)

    def vector(dve):
        for i, (drams, raw, hi, lo) in enumerate(sources):
            dve.wait_ge(s_hi, i + 1)
            nc.vector.tensor_tensor(lo, raw, hi.bitcast(F32), ALU.subtract).then_inc(s_lo, 1)

    return load, scalar, vector


def make_ident(nc, pool, ident, s_id):
    nc.gpsimd.memset(ident[:], 0.0).then_inc(s_id, 1)
    pool.wait_ge(s_id, 1)
    nc.gpsimd.affine_select(out=ident[:], in_=ident[:], compare_op=ALU.not_equal, fill=1.0, base=0,
                            pattern=[[-1, P]], channel_multiplier=1).then_inc(s_id, 1)


def latent_attention(nc, sems, A, x1, x2):
    with ExitStack() as ctx:
        sb = lambda n, s, d: ctx.enter_context(nc.sbuf_tensor("la_" + n, s, d))
        wq = [sb(f"wq{s}", [P, KD, H2, P], F32R) for s in ("hi", "lo")]
        wk = [sb(f"wk{s}", [P, KD, P], F32R) for s in ("hi", "lo")]
        wv = [sb(f"wv{s}", [P, KD, D], F32R) for s in ("hi", "lo")]
        wo = [sb(f"wo{s}", [P, H2, D], F32R) for s in ("hi", "lo")]
        ident = sb("ident", [P, P], F32)
        bc = sb("bc", [P, 2, NB, D], F32)
        g1 = sb("g1", [P, D], F32)

        with ExitStack() as c2:
            raw = lambda n, s: c2.enter_context(nc.sbuf_tensor("la_raw_" + n, s, F32))
            rq, rk, rv, ro = raw("q", [P, KD * H2 * P]), raw("k", [P, KD * P]), raw("v", [P, KD * D]), raw("o", [P, H2 * D])
            s_id = sems.take("la0_id")
            s_g1 = sems.take("la0_g1")
            flat = lambda w: [x[:].rearrange("p a b -> p (a b)") for x in w]
            flat4 = lambda w: [x[:].rearrange("p a b c -> p (a b c)") for x in w]
            load, mscalar, mtensor, mvector, (s_bc, n_bc) = modulation_rows(
                nc, sems, "la0_", c2, A, (3, 4), bc, (False, True))
            wload, wscalar, wvector = split_weights(nc, sems, "la0_w", [
                ([(A["wq2"], rq[:])], rq[:], *flat4(wq)),
                ([(A["wk2"], rk[:])], rk[:], *flat(wk)),
                ([(A["wv2"], rv[:])], rv[:], *flat(wv)),
                ([(A["wo2"], ro[0:64, :]), (A["wo2"], ro[64:P, :])], ro[:], *flat(wo))])
            block = c2.enter_context(nc.Block())

            @block.sync
            def _(sp):
                load(sp)
                wload(sp)
                sp.dma_start(g1[:], A["g1"].to_broadcast([P, D])).then_inc(s_g1, 16)
                sp.wait_ge(s_g1, 16)

            @block.scalar
            def _(act):
                mscalar(act)
                wscalar(act)

            @block.vector
            def _(dve):
                mvector(dve)
                wvector(dve)

            @block.tensor
            def _(pe):
                mtensor(pe)

            @block.gpsimd
            def _(pool):
                make_ident(nc, pool, ident, s_id)
                pool.wait_ge(s_id, 2)

        xa = sb("xa", [P, CT, D], F32)
        square = sb("square", [P, D], F32)
        stats = sb("stats", [P, CT, 6], F32)
        mv = sb("mv", [P, CT, 2], F32)
        rstd = sb("rstd", [P, CT], F32)
        var = sb("var", [P, CT], F32)
        newton = sb("newton", [P, CT], F32)
        rrms = sb("rrms", [P, CT], F32)
        ms = sb("ms", [P, CT], F32)
        nxT = [sb(f"nxT{s}", [P, KD, CH], F32R) for s in ("hi", "lo")]
        q_st = sb("q_st", [P, H2, SEQ], F32R)
        kk = [sb(f"k{s}", [P, SEQ], F32R) for s in ("hi", "lo")]
        v_st = sb("v_st", [P, KT, P], F32R)
        q_now = sb("q_now", [P, H2, P], F32R)
        prob = sb("prob", [P, H2, SEQ], F32)
        HALF = SEQ // 2
        mx = sb("mx", [P, H2, 2], F32)
        nmax = sb("nmax", [P, H2], F32)
        rsum = sb("rsum", [P, H2, 2], F32)
        rtot = sb("rtot", [P, H2], F32)
        rinv = sb("rinv", [P, H2], F32)
        pT = [sb(f"pT{s}", [P, KT, 2, P], F32R) for s in ("hi", "lo")]
        oT = [sb(f"oT{s}", [P, H2, P], F32R) for s in ("hi", "lo")]

        b_s = ctx.enter_context(nc.psum_tensor("la_b_s", [P, 4, 512], F32))
        b_t = [ctx.enter_context(nc.psum_tensor(f"la_b_t{i}", [P, 512], F32)) for i in range(2)]
        b_o = ctx.enter_context(nc.psum_tensor("la_b_o", [P, 512], F32))
        b_y = ctx.enter_context(nc.psum_tensor("la_b_y", [P, 512], F32))

        PREP = dict(x=16, bn=CT, ag=CT, nwt=3, var=1, sd=1, rs=1, xn=CT, hm=CT, h=CT, keep=1, sq=CT, ms=1, sd2=1, rs2=1, nwt2=3, nr=CT,
                    nx=CT, nT=KD, nhi=KD, nlo=KD, qp=H2, qhi=H2, qlo=H2, kp=1, khi=1, klo=1, vp=2, vhi=2, vlo=2)
        TILE = dict(qn=H2, s=2 * H2, mxp=2 * H2, mxt=H2, nm=H2, exp=2 * H2, rt=H2, rc=H2, pn=H2, t=4 * H2, thi=4 * H2,
                    tlo=4 * H2, pv=2, ohi=2, olo=2, y=1, res=1)
        S = {n: sems.take("la_" + n) for n in [*PREP, *TILE, "carrier"]}
        block = ctx.enter_context(nc.Block())

        def phases(eng, prep, tile, drain):
            with eng.Fori(0, NB) as b:
                def tiles_need(name, n, apart=False):
                    if name in PREP:
                        eng.wait_ge(S[name], b * (NC * PREP[name]) + (NC * PREP[name] if n is None else max(n, 0)))
                    else:
                        eng.wait_ge(S[name], b * (NT * TILE[name]) + max(n, 0))
                    if apart or eng is nc.sync:
                        eng.sem_inc(S["carrier"], 1)

                with eng.Fori(0, NC) as c:
                    def need(name, n, apart=False):
                        g = b * NC + c
                        if name in PREP:
                            eng.wait_ge(S[name], g * PREP[name] + max(n, 0))
                        else:
                            eng.wait_ge(S[name], b * (NT * TILE[name]))
                        if apart or eng is nc.sync:
                            eng.sem_inc(S["carrier"], 1)
                    prep(need, b, c)
                tile(lambda name, n, apart=False: tiles_need(name, n, apart), b, 0, True)
                with eng.Fori(1, NT) as n:
                    def later(name, k, apart=False):
                        if name in PREP:
                            eng.wait_ge(S[name], (b + 1) * (NC * PREP[name]))
                        else:
                            eng.wait_ge(S[name], (b * NT + n) * TILE[name] + k)
                        if apart or eng is nc.sync:
                            eng.sem_inc(S["carrier"], 1)
                    tile(later, b, n, False)
                drain(lambda name, k, apart=False: tiles_need(name, NT * TILE[name] + k, apart), b)

        @block.sync
        def _(sp):
            def prep(need, b, c):
                need("nT", 0)
                sp.dma_start(xa[:], x1[:, bass.ds((b * NC + c) * CT, CT), :]).then_inc(S["x"], 16)
            phases(sp, prep, lambda *a: None, lambda *a: None)

        @block.gpsimd
        def _(pool):
            def prep(need, b, c):
                for t in range(CT):
                    for j, (was, now) in zip((1, 0), (("xn", "hm"), ("hm", "h"))):
                        need(was, t + 1, apart=True)
                        nc.gpsimd.tensor_tensor(xa[:, t, :], xa[:, t, :], bc[:, j, bass.ds(b, 1), :].rearrange("p o d -> p (o d)"),
                                                ALU.mult if j else ALU.add).then_inc(S[now], 1)
                for t in range(CT):
                    need("nr", t + 1, apart=True)
                    nc.gpsimd.tensor_tensor(xa[:, t, :], xa[:, t, :], g1[:], ALU.mult).then_inc(S["nx"], 1)

            def tile(need, b, n, first):
                for h in range(H2):
                    if first:
                        need("qlo", None, apart=True)
                    need("s", 2 * (h - H2) + 2, apart=True)
                    nc.gpsimd.tensor_copy(q_now[:, h, :], q_st[:, h, bass.ds(n * P, P)]).then_inc(S["qn"], 1)
                for h in range(H2):
                    need("rc", h + 1, apart=True)
                    p = prob[:, h, :]
                    nc.gpsimd.tensor_scalar(p, p, rinv[:, h:h + 1], 1.0, ALU.mult, ALU.mult).then_inc(S["pn"], 1)
            phases(pool, prep, tile, lambda *a: None)

        @block.scalar
        def _(act):
            def prep(need, b, c):
                need("var", 1)
                nc.scalar.activation(rstd[:], var[:], ACT.Sqrt).then_inc(S["sd"], 1)
                need("ms", 1)
                nc.scalar.activation(rrms[:], ms[:], ACT.Sqrt).then_inc(S["sd2"], 1)
                for k in range(KD):
                    need("nT", k + 1)
                    nc.scalar.copy(nxT[0][:, k, :], b_t[k][:]).then_inc(S["nhi"], 1)
                for h in range(H2):
                    need("qp", h + 1)
                    nc.scalar.activation(q_st[:, h, bass.ds(c * CH, CH)], b_s[:, h, :], ACT.Copy,
                                         scale=float(DH) ** -0.5).then_inc(S["qhi"], 1)
                need("kp", 1)
                nc.scalar.copy(kk[0][:, bass.ds(c * CH, CH)], b_t[0][:]).then_inc(S["khi"], 1)
                for j in range(2):
                    need("vp", j + 1)
                    nc.scalar.copy(v_st[:, bass.ds(c * CT + 2 * j, 2), 0:DH],
                                   (b_t[1], b_o)[j][:].rearrange("p (t n) -> p t n", t=2)[:, :, 0:DH]).then_inc(S["vhi"], 1)

            def t_hi(need, m, h):
                for j in range(4):
                    need("t", 4 * m + j + 1)
                    need("pv", m // 2)
                    nc.scalar.copy(pT[0][:, 4 * j:4 * j + 4, h % 2, :],
                                   b_t[j % 2][:].rearrange("p (k n) -> p k n", k=4)).then_inc(S["thi"], 1)

            def o_hi(need, pair, k):
                need("pv", pair + 1)
                need("y", pair // 2)
                nc.scalar.copy(oT[0][:, 2 * k:2 * k + 2, :],
                               b_o[:, 0:2 * P].rearrange("p (h n) -> p h n", h=2)).then_inc(S["ohi"], 1)

            def slot(need, m, h, run):
                if run:
                    need("pn", m - H2 + 1 if m >= H2 else m - H2 + 1)
                    need("t", 4 * (m - H2) + 4)
                    for j in range(2):
                        if j == 0:
                            need("nm", m + 1)
                        nc.scalar.activation(prob[:, h, HALF * j:HALF * j + HALF],
                                             b_s[:, 2 * j:2 * j + 2, :].rearrange("p a n -> p (a n)"), ACT.Exp,
                                             bias=nmax[:, h:h + 1], scale=1.0,
                                             accum_out=rsum[:, h, j:j + 1]).then_inc(S["exp"], 1)

            def tile(need, b, n, first):
                for m in range(H2):
                    slot(need, m, m, True)
                    if m % 2 == 0 and (m >= 4 or not first):
                        o_hi(need, (m - 4) // 2, ((m - 4) // 2) % 2)
                    if m >= 2 or not first:
                        t_hi(need, m - 2, (m - 2) % H2)

            def drain(need, b):
                for m in range(H2):
                    if m % 2 == 0:
                        o_hi(need, (m - 4) // 2, ((m - 4) // 2) % 2)
                    if m < 2:
                        t_hi(need, m - 2, (m - 2) % H2)
            phases(act, prep, tile, drain)

        @block.vector
        def _(dve):
            def lo(out, psum, hi):
                return nc.vector.tensor_tensor(out, psum, hi.bitcast(F32), ALU.subtract)

            def prep(need, b, c):
                need("x", 16)
                for t in range(CT):
                    nc.vector.bn_stats(stats[:, t, :], xa[:, t, :]).then_inc(S["bn"], 1)
                for t in range(CT):
                    need("bn", t + 1, apart=True)
                    nc.vector.bn_aggr(mv[:, t, :], stats[:, t, :]).then_inc(S["ag"], 1)
                need("ag", CT)
                nc.vector.tensor_scalar(var[:], mv[:, :, 1], EPS_LN, None, ALU.add).then_inc(S["var"], 1)
                need("sd", 1)
                nc.vector.reciprocal(rstd[:], rstd[:]).then_inc(S["rs"], 1)
                need("rs", 1)
                newton_rsqrt(nc, dve, rstd[:], var[:], newton[:], lambda k: need("nwt", k), S["nwt"])
                for t in range(CT):
                    nc.vector.tensor_scalar(xa[:, t, :], xa[:, t, :], mv[:, t, 0:1], rstd[:, t:t + 1],
                                            ALU.subtract, ALU.mult).then_inc(S["xn"], 1)
                need("h", CT)
                nc.vector.tensor_copy(x2[:, bass.ds((b * NC + c) * CT, CT), :], xa[:]).then_inc(S["keep"], 1)
                for t in range(CT):
                    need("h", t + 1, apart=True)
                    if t:
                        need("sq", t, apart=True)
                    nc.vector.tensor_tensor_reduce(square[:], xa[:, t, :], xa[:, t, :], 1.0, 0.0, ALU.mult, ALU.add,
                                                   ms[:, t:t + 1]).then_inc(S["sq"], 1)
                need("sq", CT)
                nc.vector.tensor_scalar(ms[:], ms[:], 1.0 / D, EPS_RMS, ALU.mult, ALU.add).then_inc(S["ms"], 1)
                need("sd2", 1)
                nc.vector.reciprocal(rrms[:], rrms[:]).then_inc(S["rs2"], 1)
                need("rs2", 1)
                newton_rsqrt(nc, dve, rrms[:], ms[:], newton[:], lambda k: need("nwt2", k), S["nwt2"])
                need("keep", 1)
                for t in range(CT):
                    nc.vector.tensor_scalar(xa[:, t, :], xa[:, t, :], rrms[:, t:t + 1], None,
                                            ALU.mult).then_inc(S["nr"], 1)
                for k in range(KD):
                    need("nhi", k + 1)
                    lo(nxT[1][:, k, :], b_t[k][:], nxT[0][:, k, :]).then_inc(S["nlo"], 1)
                for h in range(H2):
                    need("qhi", h + 1)
                    q = q_st[DH:P, h, bass.ds(c * CH, CH)]
                    nc.vector.scalar_tensor_tensor(out=q, in0=b_s[DH:P, h, :], scalar=float(DH) ** -0.5,
                                                   in1=q.bitcast(F32), op0=ALU.mult, op1=ALU.subtract).then_inc(S["qlo"], 1)
                need("khi", 1)
                lo(kk[1][:, bass.ds(c * CH, CH)], b_t[0][:], kk[0][:, bass.ds(c * CH, CH)]).then_inc(S["klo"], 1)
                for j in range(2):
                    need("vhi", j + 1)
                    lo(v_st[:, bass.ds(c * CT + 2 * j, 2), DH:P], (b_t[1], b_o)[j][:].rearrange("p (t n) -> p t n", t=2)[:, :, 0:DH],
                       v_st[:, bass.ds(c * CT + 2 * j, 2), 0:DH]).then_inc(S["vlo"], 1)

            def maxes(need, m, h):
                for j in range(2):
                    need("s", 2 * m + j + 1)
                    nc.vector.tensor_reduce(mx[:, h, j:j + 1], b_s[:, 2 * j:2 * j + 2, :].rearrange("p a n -> p (a n)"),
                                            AX.X, ALU.max).then_inc(S["mxp"], 1)
                need("mxp", 2 * m + 2)
                nc.vector.tensor_reduce(nmax[:, h:h + 1], mx[:, h, :], AX.X, ALU.max, negate=True).then_inc(S["nm"], 1)

            def sums(need, m, h):
                need("exp", 2 * m + 2)
                nc.vector.tensor_reduce(rtot[:, h:h + 1], rsum[:, h, :], AX.X, ALU.add).then_inc(S["rt"], 1)
                need("rt", m + 1)
                nc.vector.reciprocal(rinv[:, h:h + 1], rtot[:, h:h + 1]).then_inc(S["rc"], 1)

            def t_lo(need, m, h):
                for j in range(4):
                    need("thi", 4 * m + j + 1)
                    lo(pT[1][:, 4 * j:4 * j + 4, h % 2, :], b_t[j % 2][:].rearrange("p (k n) -> p k n", k=4),
                       pT[0][:, 4 * j:4 * j + 4, h % 2, :]).then_inc(S["tlo"], 1)

            def o_lo(need, pair, k):
                need("ohi", pair + 1)
                lo(oT[1][:, 2 * k:2 * k + 2, :], b_o[:, 0:2 * P].rearrange("p (h n) -> p h n", h=2),
                   oT[0][:, 2 * k:2 * k + 2, :]).then_inc(S["olo"], 1)

            def add_y(need, b, n):
                need("y", 0)
                at = x2[:, bass.ds(b * NT + n, 1), :].rearrange("p o d -> p (o d)")
                nc.vector.tensor_tensor(at, b_y[:, 0:D], at, ALU.add).then_inc(S["res"], 1)

            def tile(need, b, n, first):
                for m in range(H2):
                    maxes(need, m, m)
                    if m % 2 == 0 and not first:
                        o_lo(need, (m - 4) // 2, ((m - 4) // 2) % 2)
                    if m >= 2 or not first:
                        t_lo(need, m - 2, (m - 2) % H2)
                    sums(need, m, m)
                    if m == 3 and not first:
                        add_y(need, b, n - 1)

            def drain(need, b):
                for m in range(H2):
                    if m % 2 == 0:
                        o_lo(need, (m - 4) // 2, ((m - 4) // 2) % 2)
                    if m < 2:
                        t_lo(need, m - 2, (m - 2) % H2)
                add_y(need, b, NT - 1)
            phases(dve, prep, tile, drain)

        @block.tensor
        def _(pe):
            def product(out, left, right):
                for n, (a, e) in enumerate(SPLIT3):
                    for k in range(KD):
                        x = nc.tensor.matmul(out, left(a, k), right(e, k), start=(n == 0 and k == 0),
                                             stop=(n == 2 and k == KD - 1), skip_group_check=True)
                return x

            def prep(need, b, c):
                need("olo", 0)
                need("tlo", 0)
                need("vlo", 0)
                need("klo", 0)
                for k in range(KD):
                    need("nx", CT)
                    for t in range(CT):
                        x = nc.tensor.transpose(b_t[k][:, P * t:P * t + P], xa[:, t, P * k:P * k + P], ident[:])
                    x.then_inc(S["nT"], 1)
                need("nlo", KD)
                need("exp", 0)
                need("qlo", 0)
                for h in range(H2):
                    product(b_s[:, h, :], lambda a, k: wq[a][:, k, h, :], lambda e, k: nxT[e][:, k, :]).then_inc(S["qp"], 1)
                product(b_t[0][:], lambda a, k: wk[a][:, k, :], lambda e, k: nxT[e][:, k, :]).then_inc(S["kp"], 1)
                for j in range(2):
                    for i in range(2):
                        t = 2 * j + i
                        for n, (a, e) in enumerate(SPLIT3):
                            for k in range(KD):
                                x = nc.tensor.matmul((b_t[1], b_o)[j][:, D * i:D * i + D], nxT[a][:, k, P * t:P * t + P],
                                                     wv[e][:, k, :], start=(i == 0 and n == 0 and k == 0),
                                                     stop=(n == 2 and k == KD - 1), skip_group_check=True)
                    x.then_inc(S["vp"], 1)

            def scores(need, m, h, first):
                need("qn", m + 1)
                if first:
                    need("klo", None)
                    need("qlo", None)
                need("exp", 2 * m)
                for j in range(4):
                    for w in range(2):
                        x = nc.tensor.matmul(b_s[:, j, :], q_now[:, h, :], kk[w][:, 512 * j:512 * j + 512],
                                             start=(w == 0), stop=(w == 1))
                    if j % 2:
                        x.then_inc(S["s"], 1)

            def transposes(need, m, h, first):
                need("pn", m + 1)
                for j in range(4):
                    need("tlo", 4 * m + j - 1)
                    if first:
                        need("vlo", None)
                    for i in range(4):
                        k = 4 * j + i
                        x = nc.tensor.transpose(b_t[j % 2][:, P * i:P * i + P], prob[:, h, P * k:P * k + P], ident[:])
                    x.then_inc(S["t"], 1)

            def pv(need, pair):
                need("tlo", 8 * pair + 8)
                need("olo", pair)
                for k in range(KT):
                    for w in range(2):
                        x = nc.tensor.matmul(b_o[:, 0:2 * P], v_st[:, k, :], pT[w][:, k, :, :].rearrange("p h n -> p (h n)"),
                                             start=(k == 0 and w == 0), stop=(k == KT - 1 and w == 1))
                x.then_inc(S["pv"], 1)

            def out_proj(need):
                need("olo", 0)
                need("res", -1)
                for h in range(H2):
                    for n, (a, e) in enumerate(SPLIT3):
                        x = nc.tensor.matmul(b_y[:, 0:D], oT[a][:, h, :], wo[e][:, h, :], start=(h == 0 and n == 0),
                                             stop=(h == H2 - 1 and n == 2))
                x.then_inc(S["y"], 1)

            def tile(need, b, n, first):
                for m in range(H2):
                    scores(need, m, m, first and m == 0)
                    if m % 2 == 0 and not first:
                        pv(need, (m - 4) // 2)
                    if m >= 2 or not first:
                        transposes(need, m - 2, (m - 2) % H2, first and m == 2)
                    if m == 3 and not first:
                        out_proj(need)

            def drain(need, b):
                for m in range(H2):
                    if m % 2 == 0:
                        pv(need, (m - 4) // 2)
                    if m < 2:
                        transposes(need, m - 2, (m - 2) % H2, False)
                out_proj(need)
            phases(pe, prep, tile, drain)


def experts(nc, sems, A, x1, x2, out):
    NX = NE + 1
    NG = TOK // CH
    TT = TOK // P
    with ExitStack() as ctx:
        sb = lambda n, s, d: ctx.enter_context(nc.sbuf_tensor("ex_" + n, s, d))
        bc = sb("bc", [P, 1, NB, D], F32)
        gate_size = sb("gate_size", [P, NB, D], F32)
        ident = sb("ident", [P, P], F32)
        g2 = sb("g2", [P, D], F32)
        bias = sb("bias", [P, NE], F32)
        rank = sb("rank", [P, NE], F32)
        wr = [sb(f"wr{s}", [P, KD, P], F32R) for s in ("hi", "lo")]
        with ExitStack() as c2:
            raw = c2.enter_context(nc.sbuf_tensor("ex_raw", [P, KD * P], F32))
            s_id, s_in, s_g, s_rank = (sems.take("ex0_" + n) for n in ("id", "in", "g", "rank"))
            load, mscalar, mtensor, mvector, (s_bc, n_bc) = modulation_rows(nc, sems, "ex0_", c2, A, (5,), bc, (False,))
            wload, wscalar, wvector = split_weights(nc, sems, "ex0_w", [
                ([(A["wr16"], raw[:])], raw[:], *[w[:].rearrange("p k n -> p (k n)") for w in wr])])
            block = c2.enter_context(nc.Block())

            @block.sync
            def _(sp):
                load(sp)
                wload(sp)
                sp.dma_start(g2[:], A["g2"].to_broadcast([P, D])).then_inc(s_in, 16)
                sp.dma_start(bias[:], A["bias"].to_broadcast([P, NE])).then_inc(s_in, 16)
                sp.wait_ge(s_in, 32)

            @block.scalar
            def _(act):
                mscalar(act)
                wscalar(act)

            @block.vector
            def _(dve):
                mvector(dve)
                wvector(dve)
                dve.wait_ge(s_bc, n_bc)
                floor_gate(nc, dve, bc[:, 0, :, :], gate_size[:], s_g)

            @block.tensor
            def _(pe):
                mtensor(pe)

            @block.gpsimd
            def _(pool):
                make_ident(nc, pool, ident, s_id)
                for e in range(NE):
                    nc.gpsimd.memset(rank[:, e:e + 1], float(NE - e)).then_inc(s_rank, 1)
                pool.wait_ge(s_rank, NE)
                pool.wait_ge(s_id, 2)

        xfT = [sb(f"xfT{s}", [P, KD, TOK], F32R) for s in ("hi", "lo")]
        comb = sb("comb", [P, TT, NX], F32)

        with ExitStack() as c2:
            sb2 = lambda n, s, d: c2.enter_context(nc.sbuf_tensor("ro_" + n, s, d))
            xa = sb2("xa", [P, CT, D], F32)
            square = sb2("square", [P, D], F32)
            ss = sb2("ss", [P, CT], F32)
            ms = sb2("ms", [P, CT], F32)
            rrms = sb2("rrms", [P, CT], F32)
            newton = sb2("newton", [P, CT], F32)
            lgT = sb2("lgT", [P, CH], F32)
            lg = sb2("lg", [P, TT, NE], F32)
            lg2 = sb2("lg2", [P, TT, NE], F32)
            pick = [sb2(f"pick{i}", [P, TT, NE], F32) for i in range(2)]
            top = [sb2(f"top{i}", [P, TT], F32) for i in range(6)]
            b_x = [c2.enter_context(nc.psum_tensor(f"ro_b_x{i}", [P, 512], F32)) for i in range(2)]
            b_l = c2.enter_context(nc.psum_tensor("ro_b_l", [P, 512], F32))
            b_r = c2.enter_context(nc.psum_tensor("ro_b_r", [P, 512], F32))
            PER = dict(sq=CT, ms=1, sd=1, rs=1, nwt=3, nr=CT, nx=CT, xT=KD, xhi=KD, xlo=KD, lg=1, lgc=1, lt=1, lb=1)
            S = {n: sems.take("ro_" + n) for n in [*PER, "carrier", "one"]}
            s_step = sems.take("ro_step")
            s_exp = sems.take("ro_exp")
            block = c2.enter_context(nc.Block())

            def chunks(eng, body):
                with eng.Fori(0, NG) as g:
                    def need(name, n, apart=False):
                        eng.wait_ge(S[name], g * PER[name] + max(n, 0))
                        if apart:
                            eng.sem_inc(S["carrier"], 1)
                    body(need, g)

            wide = lambda a: a.rearrange("p (t o) -> p t o", o=1).to_broadcast([P, TT, NE])

            @block.scalar
            def _(act):
                def body(need, g):
                    need("ms", 0)
                    for t in range(CT):
                        if t:
                            need("sq", t)
                        at = x2[:, bass.ds(g * CT + t, 1), :].rearrange("p o d -> p (o d)")
                        nc.scalar.activation(square[:], at, ACT.Square, accum_out=ss[:, t:t + 1]).then_inc(S["sq"], 1)
                    need("ms", 1)
                    nc.scalar.activation(rrms[:], ms[:], ACT.Sqrt).then_inc(S["sd"], 1)
                    for k in range(KD):
                        need("xT", k + 1)
                        nc.scalar.copy(xfT[0][:, k, bass.ds(g * CH, CH)], b_x[k][:]).then_inc(S["xhi"], 1)
                    need("lg", 1)
                    need("lt", 0)
                    nc.scalar.copy(lgT[:], b_l[:]).then_inc(S["lgc"], 1)
                chunks(act, body)
                for j in range(2):
                    act.wait_ge(s_step, (2, 17)[j])
                    a = (lg2[:].rearrange("p t e -> p (t e)"), top[2][:])[j]
                    nc.scalar.activation(a, a, ACT.Exp).then_inc(s_exp, 1)

            @block.gpsimd
            def _(pool):
                nc.gpsimd.memset(comb[:, :, NE:NX], 1.0).then_inc(S["one"], 1)

                def body(need, g):
                    for t in range(CT):
                        need("nr", t + 1, apart=True)
                        nc.gpsimd.tensor_tensor(xa[:, t, :], xa[:, t, :], g2[:], ALU.mult).then_inc(S["nx"], 1)
                chunks(pool, body)
                pool.wait_ge(S["one"], 1)

            @block.vector
            def _(dve):
                def body(need, g):
                    need("sq", CT)
                    nc.vector.tensor_scalar(ms[:], ss[:], 1.0 / D, EPS_RMS, ALU.mult, ALU.add).then_inc(S["ms"], 1)
                    need("sd", 1)
                    nc.vector.reciprocal(rrms[:], rrms[:]).then_inc(S["rs"], 1)
                    need("rs", 1)
                    newton_rsqrt(nc, dve, rrms[:], ms[:], newton[:], lambda k: need("nwt", k), S["nwt"])
                    need("xT", 0)
                    for t in range(CT):
                        at = x2[:, bass.ds(g * CT + t, 1), :].rearrange("p o d -> p (o d)")
                        nc.vector.tensor_scalar(xa[:, t, :], at, rrms[:, t:t + 1], None, ALU.mult).then_inc(S["nr"], 1)
                    for k in range(KD):
                        need("xhi", k + 1)
                        nc.vector.tensor_tensor(xfT[1][:, k, bass.ds(g * CH, CH)], b_x[k][:],
                                                xfT[0][:, k, bass.ds(g * CH, CH)].bitcast(F32), ALU.subtract).then_inc(S["xlo"], 1)
                    need("lt", 1)
                    nc.vector.tensor_tensor(lg[:, bass.ds(g * CT, CT), :], b_r[:].rearrange("p (t n) -> p t n", t=CT)[:, :, 0:NE],
                                            bias[:].rearrange("p (o e) -> p o e", o=1).to_broadcast([P, CT, NE]),
                                            ALU.add).then_inc(S["lb"], 1)
                chunks(dve, body)

                at = [0]

                def step(x):
                    at[0] += 1
                    x.then_inc(s_step, 1)
                    dve.wait_ge(s_step, at[0])
                dve.wait_ge(S["lb"], NG)
                v = nc.vector
                step(v.tensor_reduce(top[0][:], lg[:], AX.X, ALU.max))
                step(v.tensor_tensor(lg2[:], lg[:], wide(top[0][:]), ALU.subtract))
                dve.wait_ge(s_exp, 1)
                step(v.tensor_reduce(top[0][:], lg2[:], AX.X, ALU.add))
                step(v.reciprocal(top[0][:], top[0][:]))
                step(v.tensor_tensor(lg[:], lg2[:], wide(top[0][:]), ALU.mult))
                for i in range(2):
                    step(v.tensor_reduce(top[i][:], lg[:], AX.X, ALU.max))
                    step(v.tensor_tensor(pick[i][:], lg[:], wide(top[i][:]), ALU.is_equal))
                    step(v.tensor_tensor(pick[i][:], pick[i][:],
                                         rank[:].rearrange("p (o e) -> p o e", o=1).to_broadcast([P, TT, NE]), ALU.mult))
                    step(v.tensor_reduce(top[4][:], pick[i][:], AX.X, ALU.max))
                    step(v.tensor_tensor(pick[i][:], pick[i][:], wide(top[4][:]), ALU.is_equal))
                    if i == 0:
                        step(v.scalar_tensor_tensor(out=lg[:], in0=pick[0][:], scalar=-4.0, in1=lg[:], op0=ALU.mult, op1=ALU.add))
                step(v.tensor_tensor(top[2][:], top[1][:], top[0][:], ALU.subtract))
                assert at[0] == 17, at
                dve.wait_ge(s_exp, 2)
                step(v.tensor_scalar(top[3][:], top[2][:], 1.0, None, ALU.add))
                step(v.reciprocal(top[3][:], top[3][:]))
                step(v.tensor_tensor(top[2][:], top[2][:], top[3][:], ALU.mult))
                for i in range(2):
                    step(v.tensor_tensor(pick[i][:], pick[i][:], wide(top[3 - i][:]), ALU.mult))
                step(v.tensor_tensor(comb[:, :, 0:NE], pick[0][:], pick[1][:], ALU.add))

            @block.tensor
            def _(pe):
                def body(need, g):
                    need("nx", CT)
                    need("xlo", 0)
                    for k in range(KD):
                        for t in range(CT):
                            x = nc.tensor.transpose(b_x[k][:, P * t:P * t + P], xa[:, t, P * k:P * k + P], ident[:])
                        x.then_inc(S["xT"], 1)
                    need("xlo", KD)
                    need("lgc", 0)
                    for n, (a, e) in enumerate(SPLIT3):
                        for k in range(KD):
                            x = nc.tensor.matmul(b_l[:], wr[a][:, k, :], xfT[e][:, k, bass.ds(g * CH, CH)],
                                                 start=(n == 0 and k == 0), stop=(n == 2 and k == KD - 1))
                    x.then_inc(S["lg"], 1)
                    need("lgc", 1)
                    need("lb", 0)
                    for t in range(CT):
                        x = nc.tensor.transpose(b_r[:, P * t:P * t + P], lgT[:, P * t:P * t + P], ident[:])
                    x.then_inc(S["lt"], 1)
                chunks(pe, body)

        raw = sb("raw_w", [P, 3 * KD, FF], F32)
        w13 = [[sb(f"w13_{i}{s}", [P, 2 * KD, FF], F32R) for s in ("hi", "lo")] for i in range(2)]
        w2 = [[sb(f"w2_{i}{s}", [P, KF, D], F32R) for s in ("hi", "lo")] for i in range(2)]
        act_f = sb("act_f", [P, KF, CH], F32)
        hid = sb("hid", [P, KF, CH], F32)
        hT = [[sb(f"hT_{i}{s}", [P, KF, CH], F32R) for s in ("hi", "lo")] for i in range(2)]
        x_res = sb("x_res", [P, CT, D], F32)
        b_g = [ctx.enter_context(nc.psum_tensor(f"ex_b_g{i}", [P, 512], F32)) for i in range(KF)]
        b_u = [ctx.enter_context(nc.psum_tensor(f"ex_b_u{i}", [P, 512], F32)) for i in range(KF)]
        b_y = [ctx.enter_context(nc.psum_tensor(f"ex_b_y{i}", [P, 512], F32)) for i in range(4)]

        STEP = dict(g=KF, u=KF, sil=KF, hm=KF, hhi=KF, hlo=KF, y=CT, acc=CT)
        LOAD = dict(w=16, whi=2, wlo=2)
        LAST = dict(xr=16, fg=CT, fa=1, out=16)
        S = {n: sems.take("ex_" + n) for n in [*STEP, *LOAD, *LAST, "carrier"]}
        block = ctx.enter_context(nc.Block())

        def run(eng, load, begin, step, last):
            def needs(order, s):
                def need(name, n, apart=False):
                    value = s * STEP[name] + n if name in STEP else order * LOAD[name] + n
                    if isinstance(value, int) and value <= 0:
                        return
                    eng.wait_ge(S[name], value)
                    if apart or eng is nc.sync:
                        eng.sem_inc(S["carrier"], 1)
                return need

            def expert(order, w, number, before, following):
                begin(needs(order, order * NG))
                step(needs(order, order * NG), w, number, 0, 0)
                if before is not None:
                    last(needs(order, order * NG), 1 - w, before, NG - 1, 1)
                step(needs(order, order * NG + 1), w, number, 1, 1)
                last(needs(order, order * NG + 1), w, number, 0, 0)
                load(needs(order + 1, order * NG + 2), 1 - w, following)
                with eng.Fori(1, NG // 2) as gg:
                    for par in range(2):
                        g = 2 * gg + par
                        step(needs(order, order * NG + g), w, number, g, par)
                        last(needs(order, order * NG + g), w, number, g - 1, 1 - par)

            load(needs(0, 0), 1, NE)
            expert(0, 1, NE, None, 0)
            expert(1, 0, 0, NE, 1)
            expert(2, 1, 1, 0, 2)
            with eng.Fori(1, NE // 2) as pair:
                expert(1 + 2 * pair, 0, 2 * pair, 2 * pair - 1, 2 * pair + 1)
                expert(2 + 2 * pair, 1, 2 * pair + 1, 2 * pair, 2 * pair + 2)
            last(needs(NX, NX * NG), 1, NE - 1, NG - 1, 1)

        nothing = lambda *a: None

        @block.sync
        def _(sp):
            def load(need, w, which):
                need("whi", 0)
                need("wlo", 0)
                sp.dma_start(raw[:], A["experts"][:, bass.ds(which, 1), :, :].rearrange("p o k n -> p (o k) n")).then_inc(S["w"], 16)
            run(sp, load, nothing, nothing, nothing)
            with sp.Fori(0, NG) as g:
                sp.wait_ge(S["out"], g * 16)
                sp.sem_inc(S["carrier"], 1)
                sp.dma_start(x_res[:], x1[:, bass.ds(g * CT, CT), :]).then_inc(S["xr"], 16)
                sp.wait_ge(S["fa"], g + 1)
                sp.sem_inc(S["carrier"], 1)
                sp.dma_start(out[:, bass.ds(g * CT, CT), :], x_res[:]).then_inc(S["out"], 16)
            sp.wait_ge(S["out"], NG * 16)
            sp.wait_ge(S["w"], 16 * (NX + 1))

        @block.scalar
        def _(act):
            def load(need, w, which):
                need("w", 16)
                need("y", -2 * CT)
                nc.scalar.copy(w13[w][0][:], raw[:, 0:2 * KD, :]).then_inc(S["whi"], 1)
                nc.scalar.copy(w2[w][0][:], raw[:, 2 * KD:3 * KD, :]).then_inc(S["whi"], 1)

            def step(need, w, number, g, par):
                for f in range(KF):
                    need("g", f + 1)
                    need("hm", 0)
                    nc.scalar.activation(act_f[:, f, :], b_g[f][:], ACT.Silu).then_inc(S["sil"], 1)
                need("y", -CT)
                for f in range(KF):
                    need("hm", f + 1)
                    nc.scalar.copy(hT[par][0][:, f, :], hid[:, f, :]).then_inc(S["hhi"], 1)
            run(act, load, nothing, step, nothing)

        @block.gpsimd
        def _(pool):
            def step(need, w, number, g, par):
                for f in range(KF):
                    need("hhi", f + 1, apart=True)
                    nc.gpsimd.tensor_tensor(hT[par][1][:, f, :], hid[:, f, :], hT[par][0][:, f, :].bitcast(F32),
                                            ALU.subtract).then_inc(S["hlo"], 1)
            run(pool, nothing, nothing, step, nothing)

        @block.vector
        def _(dve):
            def load(need, w, which):
                need("whi", 1)
                nc.vector.tensor_tensor(w13[w][1][:], raw[:, 0:2 * KD, :], w13[w][0][:].bitcast(F32), ALU.subtract).then_inc(S["wlo"], 1)
                need("whi", 2)
                nc.vector.tensor_tensor(w2[w][1][:], raw[:, 2 * KD:3 * KD, :], w2[w][0][:].bitcast(F32), ALU.subtract).then_inc(S["wlo"], 1)

            def step(need, w, number, g, par):
                for f in range(KF):
                    need("u", f + 1)
                    need("sil", f + 1)
                    need("hlo", 0)
                    nc.vector.tensor_tensor(hid[:, f, :], b_u[f][:], act_f[:, f, :], ALU.mult).then_inc(S["hm"], 1)

            def last(need, w, number, g, par):
                for t in range(CT):
                    need("y", t + 1 - CT)
                    at = x2[:, bass.ds(g * CT + t, 1), :].rearrange("p o d -> p (o d)")
                    c = comb[:, bass.ds(g * CT + t, 1), bass.ds(number, 1)].rearrange("p o n -> p (o n)")
                    nc.vector.scalar_tensor_tensor(out=at, in0=b_y[t][:, 0:D], scalar=c, in1=at, op0=ALU.mult,
                                                   op1=ALU.add).then_inc(S["acc"], 1)
            run(dve, load, nothing, step, last)
            with dve.Fori(0, NB) as b:
                with dve.Fori(0, NG // NB) as c:
                    g = b * (NG // NB) + c
                    dve.wait_ge(S["xr"], (g + 1) * 16)
                    dve.wait_ge(S["acc"], NX * NG * CT)
                    for t in range(CT):
                        at = x2[:, bass.ds(g * CT + t, 1), :].rearrange("p o d -> p (o d)")
                        nc.vector.tensor_tensor(at, at, bc[:, 0, bass.ds(b, 1), :].rearrange("p o d -> p (o d)"),
                                                ALU.mult).then_inc(S["fg"], 1)
                    dve.wait_ge(S["fg"], (g + 1) * CT)
                    nc.vector.tensor_tensor(x_res[:], x_res[:], x2[:, bass.ds(g * CT, CT), :], ALU.add).then_inc(S["fa"], 1)

        @block.tensor
        def _(pe):
            def begin(need):
                need("wlo", 2)

            def step(need, w, number, g, par):
                for f in range(KF):
                    for bank, m, free in ((b_g[f], 0, "sil"), (b_u[f], 1, "hm")):
                        need(free, 0)
                        for n, (a, e) in enumerate(SPLIT3):
                            for k in range(KD):
                                x = nc.tensor.matmul(bank[:], w13[w][a][:, KD * m + k, P * f:P * f + P],
                                                     xfT[e][:, k, bass.ds(g * CH, CH)],
                                                     start=(n == 0 and k == 0), stop=(n == 2 and k == KD - 1))
                        x.then_inc(S["gu"[m]], 1)

            def last(need, w, number, g, par):
                need("hlo", 0)
                for t in range(CT):
                    need("acc", -CT)
                    for n, (a, e) in enumerate(SPLIT3):
                        for k in range(KF):
                            x = nc.tensor.matmul(b_y[t][:, 0:D], hT[par][a][:, k, P * t:P * t + P], w2[w][e][:, k, :],
                                                 start=(n == 0 and k == 0), stop=(n == 2 and k == KF - 1))
                    x.then_inc(S["y"], 1)
            run(pe, nothing, begin, step, last)


def lay_out(I):
    import numpy as np
    a = lambda n: np.asarray(I["L0_" + n])
    kp = lambda w: np.ascontiguousarray(w.reshape(-1, P, w.shape[-1]).transpose(1, 0, 2))
    out = {}
    out["wqkv"] = kp(np.concatenate([a("attn_Wq"), a("attn_Wk"), a("attn_Wv")], axis=1))
    out["wo"] = np.ascontiguousarray(a("attn_Wo").reshape(H1, DH, D).transpose(1, 0, 2))
    out["cT"] = kp(np.ascontiguousarray(a("c").T))
    twice = lambda w, n=2: np.concatenate([w] * n, axis=-1)
    wq2 = np.ascontiguousarray(a("ffn_Wq").T).reshape(D, H2, DH)
    out["wq2"] = kp(np.ascontiguousarray(twice(wq2)).reshape(D, H2 * P)).reshape(P, -1)
    out["wk2"] = kp(twice(np.ascontiguousarray(a("ffn_Wkc").T))).reshape(P, -1)
    out["wv2"] = kp(twice(np.ascontiguousarray(a("ffn_Wvc").T), 4)).reshape(P, -1)
    out["wo2"] = np.ascontiguousarray(a("ffn_Wo").T.reshape(H2, DH, D).transpose(1, 0, 2)).reshape(DH, -1)
    fc = lambda w: kp(np.ascontiguousarray(w.T))
    pack = lambda w1, w3, w2: np.concatenate([fc(w1), fc(w3), fc(w2)], axis=1)
    each = [pack(a("ffn_eW1")[e], a("ffn_eW3")[e], a("ffn_eW2")[e]) for e in range(NE)]
    each.append(pack(a("ffn_sW1"), a("ffn_sW3"), a("ffn_sW2")))
    out["experts"] = np.ascontiguousarray(np.stack(each, axis=1))
    out["wr16"] = kp(twice(np.ascontiguousarray(a("ffn_Wr").T), P // NE)).reshape(P, -1)
    out["bias"] = a("ffn_expert_bias").reshape(1, NE)
    out["g1"] = a("ffn_g1").reshape(1, D)
    out["g2"] = a("ffn_g2").reshape(1, D)
    out["wmod"] = np.ascontiguousarray(kp(a("wmod")).reshape(P, KD, 6, D))
    return out


def program(nc, x, arrays, out):
    A = arrays
    x1 = nc.dram_tensor("x1_scratch", [P, TOK // P, D], F32).ap()
    by_tile = lambda a: a.rearrange("b (t p) d -> p (b t) d", p=P)
    A["x"] = by_tile(x)
    with PhaseSemaphores(nc) as sems:
        windowed_attention(nc, sems, A, x1)
    with nc.sbuf_tensor("x2_resident", [P, TOK // P, D], F32) as x2:
        with PhaseSemaphores(nc) as sems:
            latent_attention(nc, sems, A, x1, x2)
        with PhaseSemaphores(nc) as sems:
            experts(nc, sems, A, x1, x2, by_tile(out))


def kernel(**inputs):
    import numpy as np
    import concourse.bacc as bacc
    from concourse.bass_utils import run_bass_kernel_spmd

    nc = bacc.Bacc("TRN2", target_bir_lowering=False, num_devices=1)
    arrays = {f"in_{k}": v for k, v in lay_out(inputs).items()}
    arrays["in_x"] = np.ascontiguousarray(inputs["L0_attn_x"])
    aps = {k[3:]: nc.dram_tensor(k, a.shape, mybir.dt.from_np(a.dtype), kind="ExternalInput").ap()
           for k, a in arrays.items()}
    out = nc.dram_tensor("out_x", (NB, SEQ, D), F32, kind="ExternalOutput").ap()
    program(nc, aps.pop("x"), aps, out)
    return run_bass_kernel_spmd(nc, [arrays], core_ids=[0]).results[0]["out_x"]
```

```python
from contextlib import ExitStack

import concourse.bass as bass
from concourse import mybir

ALU = mybir.AluOpType
ACT = mybir.ActivationFunctionType
AX = mybir.AxisListType
F32 = mybir.dt.float32
F32R = mybir.dt.float32r
BF16 = mybir.dt.bfloat16

P = 128
D = 256
KD = D // P
NB = 2
SEQ = 2048
TOK = NB * SEQ
CH = 512
CT = CH // P
NC = SEQ // CH
NG = NB * NC
NT = SEQ // P
EPS_LN = 1e-5
EPS_RMS = 1e-6

H1 = 16
DH = 64
WIN = 64
HP = H1 // 2
KW = WIN + P
SW = 2 * P
NEG = -3.0e38

H2 = 4
KT = SEQ // P

NE = 8
FF = 256
KF = FF // P


START = 1


def begin_counts(nc, sems):
    for s in sems:
        nc.tensor.sem_inc(s, START)
    nc.all_engine_barrier()


class PhaseSemaphores:

    def __init__(self, nc):
        self.nc, self.taken = nc, []

    def __enter__(self):
        return self

    def take(self, name):
        self.taken.append(self.nc.alloc_semaphore(name))
        return self.taken[-1]

    def __exit__(self, *failure):
        if failure[0] is None:
            self.nc.all_engine_barrier()
            self.nc.clear_and_free_semaphores(self.taken)
            self.nc.all_engine_barrier()


def modulation_rows(nc, sems, block_name, ctx, A, rows, bc, plus_one):
    sb = lambda n, s, d: ctx.enter_context(nc.sbuf_tensor(block_name + n, s, d))
    c_raw = sb("c_raw", [P, KD, NB], F32)
    c_silu = sb("c_silu", [P, KD, NB], F32)
    c_wide = sb("c_wide", [P, KD, NB, P], F32)
    wmod = sb("wmod", [P, KD, len(rows), D], F32)
    ps = [ctx.enter_context(nc.psum_tensor(f"{block_name}mod_ps{i}", [P, 512], F32)) for i in range(2)]
    s_in, s_silu, s_wide, s_mm, s_out = (
        sems.take(block_name + n) for n in ("mod_in", "mod_silu", "mod_wide", "mod_mm", "mod_out"))

    def load(sp):
        sp.dma_start(c_raw[:], A["cT"]).then_inc(s_in, 16)
        for j, row in enumerate(rows):
            sp.dma_start(wmod[:, :, j, :], A["wmod"][:, :, row, :]).then_inc(s_in, 16)

    def scalar(act):
        act.wait_ge(s_in, 16 * (1 + len(rows)))
        nc.scalar.activation(c_silu[:], c_raw[:], ACT.Silu).then_inc(s_silu, 1)

    def tensor(pe):
        pe.wait_ge(s_wide, 1)
        n = 0
        for j in range(len(rows)):
            for b in range(NB):
                if n >= 2:
                    pe.wait_ge(s_out, n - 1)
                for k in range(KD):
                    mm = nc.tensor.matmul(ps[n % 2][:, 0:D], c_wide[:, k, b, :], wmod[:, k, j, :],
                                          start=(k == 0), stop=(k == KD - 1))
                mm.then_inc(s_mm, 1)
                n += 1

    def vector(dve):
        dve.wait_ge(s_silu, 1)
        nc.vector.tensor_copy(c_wide[:].rearrange("p k b m -> p (k b) m"),
                              c_silu[:].rearrange("p k (b o) -> p (k b) o", o=1).to_broadcast([P, KD * NB, P])
                              ).then_inc(s_wide, 1)
        n = 0
        for j in range(len(rows)):
            for b in range(NB):
                dve.wait_ge(s_mm, n + 1)
                add = 1.0 if plus_one[j] else 0.0
                nc.vector.tensor_scalar(bc[:, j, b, :], ps[n % 2][:, 0:D], add, None, ALU.add).then_inc(s_out, 1)
                n += 1

    return load, scalar, tensor, vector, (s_out, n_of(rows))


def floor_gate(nc, dve, gate, size, s_g):
    nc.vector.tensor_scalar(size, gate, -1.0, 0.25, ALU.mult, ALU.max).then_inc(s_g, 1)
    dve.wait_ge(s_g, 1)
    nc.vector.tensor_tensor(size, size, gate, ALU.max).then_inc(s_g, 1)
    dve.wait_ge(s_g, 2)
    nc.vector.tensor_scalar(gate, gate, 0.0, 2.0, ALU.is_ge, ALU.mult).then_inc(s_g, 1)
    dve.wait_ge(s_g, 3)
    nc.vector.tensor_scalar(gate, gate, -1.0, None, ALU.add).then_inc(s_g, 1)
    dve.wait_ge(s_g, 4)
    nc.vector.tensor_tensor(gate, gate, size, ALU.mult).then_inc(s_g, 1)


def n_of(rows):
    return NB * len(rows)


def newton_rsqrt(nc, dve, root, var, scratch, wait, done):
    nc.vector.tensor_tensor(scratch, root, root, ALU.mult).then_inc(done, 1)
    wait(1)
    nc.vector.scalar_tensor_tensor(out=scratch, in0=var, scalar=-0.5, in1=scratch, op0=ALU.mult, op1=ALU.mult).then_inc(done, 1)
    wait(2)
    nc.vector.scalar_tensor_tensor(out=root, in0=scratch, scalar=1.5, in1=root, op0=ALU.add, op1=ALU.mult).then_inc(done, 1)
    wait(3)


def windowed_attention(nc, sems, A, x1):
    with ExitStack() as ctx:
        sb = lambda n, s, d: ctx.enter_context(nc.sbuf_tensor("wa_" + n, s, d))
        bank = lambda n: ctx.enter_context(nc.psum_tensor("wa_" + n, [P, 512], F32))
        wqkv = [sb(f"wqkv{s}", [P, KD, 3 * H1 * DH], F32R) for s in ("hi", "lo")]
        wo = [sb(f"wo{s}", [P, H1, D], F32R) for s in ("hi", "lo")]
        ident = sb("ident", [P, P], F32)
        mask = sb("mask", [P, NC, KW], BF16)
        mask0 = sb("mask0", [P, KW], BF16)
        bc = sb("bc", [P, 3, NB, D], F32)

        with ExitStack() as c2:
            raw = c2.enter_context(nc.sbuf_tensor("wa_raw", [P, KD * 3 * H1 * DH], F32))
            raw_o = c2.enter_context(nc.sbuf_tensor("wa_raw_o", [P, H1 * D], F32))
            gate_abs = c2.enter_context(nc.sbuf_tensor("wa_gate_abs", [P, NB, D], F32))
            sem = lambda n: sems.take("wa0_" + n)
            s_w, s_hi, s_lo, s_id, s_m, s_g = (sem(n) for n in ("w", "hi", "lo", "id", "m", "g"))
            load, mscalar, mtensor, mvector, (s_bc, n_bc) = modulation_rows(
                nc, sems, "wa0_", c2, A, (0, 1, 2), bc, (False, True, False))
            block = c2.enter_context(nc.Block())
            parts = [(raw[:, i * 1536:(i + 1) * 1536],
                      [w[:].rearrange("p k n -> p (k n)")[:, i * 1536:(i + 1) * 1536] for w in wqkv]) for i in range(4)]
            parts += [(raw_o[:, i * 2048:(i + 1) * 2048],
                       [w[:].rearrange("p h n -> p (h n)")[:, i * 2048:(i + 1) * 2048] for w in wo]) for i in range(2)]

            @block.sync
            def _(sp):
                load(sp)
                for i in range(4):
                    sp.dma_start(raw[:, i * 1536:(i + 1) * 1536],
                                 A["wqkv"].rearrange("p k n -> p (k n)")[:, i * 1536:(i + 1) * 1536]).then_inc(s_w, 16)
                    sp.wait_ge(s_w, 16 * (i + 1))
                wo_h = A["wo"].rearrange("p h n -> p (h n)")
                for i in range(2):
                    for half in range(2):
                        sp.dma_start(raw_o[64 * half:64 * half + 64, i * 2048:(i + 1) * 2048],
                                     wo_h[:, i * 2048:(i + 1) * 2048]).then_inc(s_w, 16)
                    sp.wait_ge(s_w, 16 * (6 + 2 * i))

            @block.scalar
            def _(act):
                mscalar(act)
                for i, (src, (hi, lo)) in enumerate(parts):
                    act.wait_ge(s_w, 16 * (i + 1 if i < 4 else 6 + 2 * (i - 4)))
                    nc.scalar.copy(hi, src).then_inc(s_hi, 1)

            @block.vector
            def _(dve):
                mvector(dve)
                dve.wait_ge(s_bc, n_bc)
                ga = bc[:, 2, :, :]
                floor_gate(nc, dve, ga, gate_abs[:], s_g)
                for i, (src, (hi, lo)) in enumerate(parts):
                    dve.wait_ge(s_hi, i + 1)
                    nc.vector.tensor_tensor(lo, src, hi.bitcast(F32), ALU.subtract).then_inc(s_lo, 1)

            @block.tensor
            def _(pe):
                mtensor(pe)

            @block.gpsimd
            def _(pool):
                nc.gpsimd.memset(ident[:], 0.0).then_inc(s_id, 1)
                nc.gpsimd.memset(mask[:], 0.0).then_inc(s_m, 1)
                pool.wait_ge(s_id, 1)
                nc.gpsimd.affine_select(out=ident[:], in_=ident[:], compare_op=ALU.not_equal, fill=1.0, base=0,
                                        pattern=[[-1, P]], channel_multiplier=1).then_inc(s_id, 1)
                pool.wait_ge(s_m, 1)
                nc.gpsimd.affine_select(out=mask[:], in_=mask[:], compare_op=ALU.is_ge, fill=NEG, base=0,
                                        pattern=[[0, NC], [1, KW]], channel_multiplier=-1).then_inc(s_m, 1)
                pool.wait_ge(s_m, 2)
                nc.gpsimd.affine_select(out=mask[:], in_=mask[:], compare_op=ALU.is_ge, fill=NEG, base=WIN,
                                        pattern=[[0, NC], [-1, KW]], channel_multiplier=1).then_inc(s_m, 1)
                pool.wait_ge(s_m, 3)
                nc.gpsimd.memset(mask[:, 0, 0:WIN], NEG).then_inc(s_m, 1)
                pool.wait_ge(s_m, 4)

        xa = sb("xa", [P, CT, D], F32)
        xr = sb("xr", [P, CT, D], F32)
        stats = sb("stats", [P, CT, 6], F32)
        mv = sb("mv", [P, CT, 2], F32)
        rstd = sb("rstd", [P, CT], F32)
        var = sb("var", [P, CT], F32)
        gated = sb("gated", [P, 2, D], F32)
        newton = sb("newton", [P, CT], F32)
        hT = [sb(f"hT{s}", [P, KD, CH], F32R) for s in ("hi", "lo")]
        v_st = sb("v_st", [P, CT + 1, H1, P], F32R)
        kk = sb("kk", [P, 2, 2, CH - P + SW], F32R)
        k_halo = sb("k_halo", [P, HP, 2, 2, WIN], F32R)
        q_st = sb("q_st", [P, 2, CH], F32R)
        RING = CT
        prob = sb("prob", [P, RING, 2, 2 * P], F32)
        nmax = sb("nmax", [P, RING, 2], F32)
        rsum = sb("rsum", [P, RING, 2], F32)
        rinv = sb("rinv", [P, RING, 2], F32)
        PTW = (CT + 1) * SW
        pT = [sb(f"pT{s}", [P, 2, PTW], F32R) for s in ("hi", "lo")]
        oT = [sb(f"oT{s}", [P, 2, CH], F32R) for s in ("hi", "lo")]

        b_q, b_k = bank("b_q"), bank("b_k")
        b_s = [bank("b_s0"), bank("b_s1")]
        b_t, b_o = bank("b_t"), bank("b_o")
        b_wo = [bank("b_wo0"), bank("b_wo1")]

        names = ("nwt x xr bn ag var sd rs xn hm h hT hhi hlo vp vhi vlo vhalo s ttr exp rc pn t thi tlo pv ohi olo wo "
                 "pq pk qhi qlo khi klo kdup krest ksave mask res1 res2 out init carrier").split()
        S = {n: sems.take("wa_" + n) for n in names}
        PER = dict(x=16, xr=16, bn=CT, ag=CT, nwt=3, var=1, sd=1, rs=1, xn=CT, hm=CT, h=CT, hT=KD, hhi=KD, hlo=KD,
                   vp=2 * CT, vhi=2 * CT, vlo=2 * CT, vhalo=32, s=HP * CT, ttr=HP * CT, exp=HP * CT, rc=HP * CT,
                   pn=HP * CT, t=HP * CT, thi=HP * CT, tlo=HP * CT, pv=2 * HP, ohi=2 * HP, olo=2 * HP, wo=2 * HP,
                   pq=HP, pk=HP, qhi=HP, qlo=HP, khi=HP, klo=HP, kdup=32 * HP, krest=16 * HP, ksave=16 * HP,
                   mask=1, res1=CT, res2=CT, out=16)

        begin_counts(nc, [S[n] for n in PER])
        INIT = 8
        block = ctx.enter_context(nc.Block())

        def counts(eng, m, following):
            def need(name, n, apart=False):
                eng.wait_ge(S[name], START + m * PER[name] + (n if following else max(n, 0)))
                if apart or eng is nc.sync:
                    eng.sem_inc(S["carrier"], 1)
            return need

        def chunks(eng, first, body):
            first(counts(eng, 0, False), 0)
            with eng.Fori(0, NG) as g:
                body(counts(eng, g, False), counts(eng, g + 1, True), g, (g + 1) & (NG - 1))

        def of_batch(g, row):
            b = (g >> (NC.bit_length() - 1)) & (NB - 1)
            return bc[:, row, bass.ds(b, 1), :].rearrange("p o d -> p (o d)")

        def pt_places(t):
            halo = 0 if t == 0 else SW * t + P
            own = SW * CT + P if t == CT - 1 else SW * (t + 1)
            if own == halo + WIN:
                return [(0, KW, halo)]
            return [(0, WIN, halo), (WIN, KW, own)]

        BLOCK_AT = [0] + [P * j for j in range(CT - 1)] + [CH - SW]

        @block.sync
        def _(sp):
            def load_x(nxt, m):
                nxt("hT", 0)
                sp.dma_start(xa[:], A["x"][:, bass.ds(m * CT, CT), :]).then_inc(S["x"], 16)

            def value_halo(nxt, half):
                nxt("pv", 8 * half - 8)
                nxt("vhalo", 16 * half)
                sp.dma_start(v_st[WIN:P, 0, 8 * half:8 * half + 8, :].bitcast(F32),
                             v_st[WIN:P, CT, 8 * half:8 * half + 8, :].bitcast(F32)).then_inc(S["vhalo"], 16)

            def keys(need, i):
                need("s", CT * i)
                need("ksave", 16 * i)
                sp.dma_start(kk[:, :, :, 0:WIN].bitcast(F32), k_halo[:, i, :, :, :].bitcast(F32)).then_inc(S["krest"], 16)
                need("klo", i + 1)
                sp.dma_start(kk[64:P, :, 0, WIN:WIN + CH].bitcast(F32), kk[0:64, :, 0, WIN:WIN + CH].bitcast(F32)).then_inc(S["kdup"], 16)
                sp.dma_start(kk[0:64, :, 1, WIN:WIN + CH].bitcast(F32), kk[64:P, :, 1, WIN:WIN + CH].bitcast(F32)).then_inc(S["kdup"], 16)
                need("kdup", 32 * (i + 1))
                need("krest", 16 * (i + 1))
                sp.dma_start(k_halo[:, i, :, :, :].bitcast(F32), kk[:, :, :, CH:CH + WIN].bitcast(F32)).then_inc(S["ksave"], 16)

            def first(nxt, m):
                load_x(nxt, m)
                value_halo(nxt, 0)
                value_halo(nxt, 1)
                keys(nxt, 0)

            def body(need, nxt, g, m):
                load_x(nxt, m)
                need("out", 0)
                sp.dma_start(xr[:], A["x"][:, bass.ds(g * CT, CT), :]).then_inc(S["xr"], 16)
                for i in range(1, HP):
                    keys(need, i)
                    if i == 6:
                        value_halo(nxt, 0)
                value_halo(nxt, 1)
                keys(nxt, 0)
                need("res2", CT)
                sp.dma_start(x1[:, bass.ds(g * CT, CT), :], xr[:]).then_inc(S["out"], 16)
            sp.wait_ge(S["init"], INIT)
            chunks(sp, first, body)
            sp.wait_ge(S["out"], START + 16 * NB * NC)
            sp.wait_ge(S["ksave"], START + 16 * (HP * NB * NC + 1))

        @block.gpsimd
        def _(pool):
            nc.gpsimd.memset(v_st[:, CT, :, :].bitcast(F32), 0.0).then_inc(S["init"], 1)
            nc.gpsimd.memset(v_st[0:WIN, 0, :, :].bitcast(F32), 0.0).then_inc(S["init"], 1)
            nc.gpsimd.memset(k_halo[:].bitcast(F32), 0.0).then_inc(S["init"], 1)
            nc.gpsimd.memset(kk[:, :, :, WIN + CH:].bitcast(F32), 0.0).then_inc(S["init"], 1)
            nc.gpsimd.memset(prob[:, :, :, 0:WIN], 0.0).then_inc(S["init"], 1)
            nc.gpsimd.memset(mask0[:], 0.0).then_inc(S["init"], 1)

            def modulate(nxt, m, t):
                nxt("xn", t + 1, apart=True)
                nc.gpsimd.tensor_tensor(xa[:, t, :], xa[:, t, :], of_batch(m, 1), ALU.mult).then_inc(S["hm"], 1)
                nxt("hm", t + 1, apart=True)
                nc.gpsimd.tensor_tensor(xa[:, t, :], xa[:, t, :], of_batch(m, 0), ALU.add).then_inc(S["h"], 1)

            def first(nxt, m):
                for t in range(CT):
                    modulate(nxt, m, t)

            def body(need, nxt, g, m):
                for i in range(HP):
                    for t in range(CT):
                        r = (CT * i + t) % RING
                        need("rc", CT * i + t + 1, apart=True)
                        for hd in range(2):
                            p = prob[:, r, hd, WIN:]
                            x = nc.gpsimd.tensor_scalar(p, p, rinv[:, r, hd:hd + 1], 1.0, ALU.mult, ALU.mult)
                        x.then_inc(S["pn"], 1)
                    if i in (4, 5):
                        modulate(nxt, m, 2 * (i - 4))
                        modulate(nxt, m, 2 * (i - 4) + 1)
            pool.wait_ge(S["init"], INIT)
            chunks(pool, first, body)

        @block.scalar
        def _(act):
            def exp(need, i, t):
                n = CT * i + t
                need("ttr", n + 1)
                for hd in range(2):
                    p = prob[:, n % RING, hd, WIN:]
                    x = nc.scalar.activation(p, p, ACT.Exp, bias=nmax[:, n % RING, hd:hd + 1], scale=-1.0,
                                             accum_out=rsum[:, n % RING, hd:hd + 1])
                x.then_inc(S["exp"], 1)

            def t_hi(need, i, t):
                need("t", CT * i + t + 1)
                need("pv", 2 * i)
                for a, e, at in pt_places(t):
                    x = nc.scalar.copy(pT[0][:, :, at:at + e - a],
                                       b_t[:, 0:2 * KW].rearrange("p (h n) -> p h n", h=2)[:, :, a:e])
                x.then_inc(S["thi"], 1)

            def q_hi(need, i):
                need("pq", i + 1)
                need("s", CT * i)
                nc.scalar.copy(q_st[0:64, 0, :], b_q[0:64, :])
                nc.scalar.copy(q_st[0:64, 1, :], b_q[64:P, :]).then_inc(S["qhi"], 1)

            def k_hi(need, i):
                need("pk", i + 1)
                need("s", CT * i)
                need("ksave", 16 * i)
                nc.scalar.copy(kk[0:64, 0, 0, WIN:WIN + CH], b_k[0:64, :])
                nc.scalar.copy(kk[64:P, 0, 1, WIN:WIN + CH], b_k[64:P, :]).then_inc(S["khi"], 1)

            def o_hi(need, i, hd):
                need("pv", 2 * i + hd + 1)
                need("wo", 2 * (i - 1) + hd + 1)
                nc.scalar.copy(oT[0][:, hd, :], b_o[:]).then_inc(S["ohi"], 1)

            def root(nxt):
                nxt("var", 1)
                nc.scalar.activation(rstd[:], var[:], ACT.Sqrt).then_inc(S["sd"], 1)

            def h_hi(nxt, k):
                nxt("hT", k + 1)
                nc.scalar.copy(hT[0][:, k, :], (b_k, b_q)[k][:]).then_inc(S["hhi"], 1)

            def v_hi(nxt, n):
                half, t = n // CT, n % CT
                nxt("vp", n + 1)
                nxt("vhalo", 16 * (half + 1))
                nc.scalar.copy(v_st[:, t + 1, 8 * half:8 * half + 8, 0:DH],
                               (b_q, b_k)[n % 2][:].rearrange("p (h n) -> p h n", h=8)).then_inc(S["vhi"], 1)

            def first(nxt, m):
                root(nxt)
                for k in range(KD):
                    h_hi(nxt, k)
                for n in range(2 * CT):
                    v_hi(nxt, n)
                k_hi(nxt, 0)
                q_hi(nxt, 0)

            def body(need, nxt, g, m):
                for i in range(HP + 1):
                    now, last = i < HP, i > 0
                    if last:
                        t_hi(need, i - 1, 0)
                        t_hi(need, i - 1, 1)
                    if i == HP:
                        v_hi(nxt, 0)
                        v_hi(nxt, 1)
                    if last:
                        t_hi(need, i - 1, 2)
                    if now:
                        exp(need, i, 0)
                        exp(need, i, 1)
                    if i == HP:
                        v_hi(nxt, 2)
                    if last:
                        t_hi(need, i - 1, 3)
                    if now:
                        exp(need, i, 2)
                    if i + 1 < HP:
                        k_hi(need, i + 1)
                    if i + 1 == HP:
                        h_hi(nxt, 0)
                    if now:
                        exp(need, i, 3)
                    if last:
                        o_hi(need, i - 1, 0)
                    if i + 1 < HP:
                        q_hi(need, i + 1)
                    if i + 1 == HP:
                        h_hi(nxt, 1)
                    if i == 2:
                        root(nxt)
                    if i == HP:
                        v_hi(nxt, 3)
                    if last:
                        o_hi(need, i - 1, 1)
                for n in range(CT, 2 * CT):
                    v_hi(nxt, n)
                k_hi(nxt, 0)
                q_hi(nxt, 0)
            act.wait_ge(S["init"], INIT)
            chunks(act, first, body)

        @block.vector
        def _(dve):
            for w in range(2):
                nc.vector.memset(pT[w][:].bitcast(F32), 0.0).then_inc(S["init"], 1)
            dve.wait_ge(S["init"], INIT)

            def lo(out, psum, hi, sem=None):
                x = nc.vector.tensor_tensor(out, psum, hi.bitcast(F32), ALU.subtract)
                if sem:
                    x.then_inc(S[sem], 1)

            def ttr(need, i, t):
                n = CT * i + t
                need("s", n + 1)
                need("t", n - RING + 1, apart=True)
                m = mask0[:] if t == 0 else mask[:, 1, :]
                for hd in range(2):
                    x = nc.vector.tensor_tensor_reduce(prob[:, n % RING, hd, WIN:], b_s[t % 2][:, SW * hd:SW * hd + KW], m,
                                                       -float(DH) ** -0.5, 3.4e38, ALU.add, ALU.min,
                                                       nmax[:, n % RING, hd:hd + 1])
                x.then_inc(S["ttr"], 1)

            def recip(need, i, t):
                n = CT * i + t
                need("exp", n + 1)
                nc.vector.reciprocal(rinv[:, n % RING, :], rsum[:, n % RING, :]).then_inc(S["rc"], 1)

            def t_lo(need, i, t):
                need("thi", CT * i + t + 1)
                pl = pt_places(t)
                for a, e, at in pl:
                    lo(pT[1][:, :, at:at + e - a], b_t[:, 0:2 * KW].rearrange("p (h n) -> p h n", h=2)[:, :, a:e],
                       pT[0][:, :, at:at + e - a], "tlo" if (a, e, at) == pl[-1] else None)

            def q_lo(need, i):
                need("qhi", i + 1)
                lo(q_st[64:P, 0, :], b_q[0:64, :], q_st[0:64, 0, :])
                lo(q_st[64:P, 1, :], b_q[64:P, :], q_st[0:64, 1, :], "qlo")

            def k_lo(need, i):
                need("khi", i + 1)
                lo(kk[0:64, 1, 0, WIN:WIN + CH], b_k[0:64, :], kk[0:64, 0, 0, WIN:WIN + CH])
                lo(kk[64:P, 1, 1, WIN:WIN + CH], b_k[64:P, :], kk[64:P, 0, 1, WIN:WIN + CH], "klo")

            def o_lo(need, i, hd):
                need("ohi", 2 * i + hd + 1)
                lo(oT[1][:, hd, :], b_o[:], oT[0][:, hd, :], "olo")

            def moments(nxt):
                nxt("x", 16)
                for t in range(CT):
                    nc.vector.bn_stats(stats[:, t, :], xa[:, t, :]).then_inc(S["bn"], 1)

            def variances(nxt):
                for t in range(CT):
                    nxt("bn", t + 1, apart=True)
                    nc.vector.bn_aggr(mv[:, t, :], stats[:, t, :]).then_inc(S["ag"], 1)
                nxt("ag", CT)
                nc.vector.tensor_scalar(var[:], mv[:, :, 1], EPS_LN, None, ALU.add).then_inc(S["var"], 1)

            def inverse_roots(nxt):
                nxt("sd", 1)
                nc.vector.reciprocal(rstd[:], rstd[:]).then_inc(S["rs"], 1)
                nxt("rs", 1)
                newton_rsqrt(nc, dve, rstd[:], var[:], newton[:], lambda k: nxt("nwt", k), S["nwt"])

            def normalise(nxt):
                for t in range(CT):
                    nc.vector.tensor_scalar(xa[:, t, :], xa[:, t, :], mv[:, t, 0:1], rstd[:, t:t + 1],
                                            ALU.subtract, ALU.mult).then_inc(S["xn"], 1)

            def h_lo(nxt, k):
                nxt("hhi", k + 1)
                lo(hT[1][:, k, :], (b_k, b_q)[k][:], hT[0][:, k, :], "hlo")

            def v_lo(nxt, n):
                half, t = n // CT, n % CT
                nxt("vhi", n + 1)
                lo(v_st[:, t + 1, 8 * half:8 * half + 8, DH:P], (b_q, b_k)[n % 2][:].rearrange("p (h n) -> p h n", h=8),
                   v_st[:, t + 1, 8 * half:8 * half + 8, 0:DH], "vlo")

            def first(nxt, m):
                moments(nxt)
                variances(nxt)
                inverse_roots(nxt)
                normalise(nxt)
                for k in range(KD):
                    h_lo(nxt, k)
                for n in range(2 * CT):
                    v_lo(nxt, n)
                k_lo(nxt, 0)
                q_lo(nxt, 0)

            def body(need, nxt, g, m):
                need("ttr", 0)
                nc.vector.tensor_copy(mask0[:], mask[:, bass.ds(g & (NC - 1), 1), :].rearrange("p o d -> p (o d)")).then_inc(S["mask"], 1)
                need("mask", 1)
                for i in range(HP + 1):
                    now, last = i < HP, i > 0
                    if last:
                        t_lo(need, i - 1, 0)
                        t_lo(need, i - 1, 1)
                    if i == HP:
                        v_lo(nxt, 0)
                        v_lo(nxt, 1)
                    if now:
                        ttr(need, i, 0)
                        ttr(need, i, 1)
                    if last:
                        t_lo(need, i - 1, 2)
                    if i == HP:
                        v_lo(nxt, 2)
                    if now:
                        recip(need, i, 0)
                        ttr(need, i, 2)
                        recip(need, i, 1)
                    if last:
                        t_lo(need, i - 1, 3)
                    if now:
                        ttr(need, i, 3)
                    if i + 1 < HP:
                        k_lo(need, i + 1)
                    if i + 1 == HP:
                        h_lo(nxt, 0)
                    if now:
                        recip(need, i, 2)
                    if last:
                        o_lo(need, i - 1, 0)
                    if now:
                        recip(need, i, 3)
                    if i + 1 < HP:
                        q_lo(need, i + 1)
                    if i + 1 == HP:
                        h_lo(nxt, 1)
                    if i == HP:
                        v_lo(nxt, 3)
                    if i == 1:
                        moments(nxt)
                    if i == 2:
                        variances(nxt)
                    if i == 3:
                        inverse_roots(nxt)
                        normalise(nxt)
                    if last:
                        o_lo(need, i - 1, 1)
                for n in range(CT, 2 * CT):
                    v_lo(nxt, n)
                k_lo(nxt, 0)
                q_lo(nxt, 0)
                need("wo", 2 * HP)
                need("xr", 16)
                for t in range(CT):
                    need("res2", t - 1)
                    nc.vector.tensor_tensor(gated[:, t % 2, :], b_wo[t // 2][:, D * (t % 2):D * (t % 2) + D],
                                            of_batch(g, 2), ALU.mult).then_inc(S["res1"], 1)
                    need("res1", t + 1)
                    nc.vector.tensor_tensor(xr[:, t, :], xr[:, t, :], gated[:, t % 2, :], ALU.add).then_inc(S["res2"], 1)
            chunks(dve, first, body)

        @block.tensor
        def _(pe):
            SPLIT3 = ((0, 0), (0, 1), (1, 0))

            def project(out, col0, need):
                for n, (a, e) in enumerate(SPLIT3):
                    for k in range(KD):
                        x = nc.tensor.matmul(out, wqkv[a][:, k, col0:col0 + P], hT[e][:, k, :],
                                             start=(n == 0 and k == 0), stop=(n == 2 and k == KD - 1))
                return x

            def pq(need, i):
                need("qlo", i)
                project(b_q[:], P * i, need).then_inc(S["pq"], 1)

            def pk(need, i):
                need("klo", i)
                project(b_k[:], H1 * DH + P * i, need).then_inc(S["pk"], 1)

            def scores(need, i, t):
                n = CT * i + t
                if t == 0:
                    need("qlo", i + 1)
                    need("kdup", 32 * (i + 1))
                    need("krest", 16 * (i + 1))
                    need("klo", i + 1)
                need("ttr", n - 1)
                for hd in range(2):
                    for w in range(2):
                        x = nc.tensor.matmul(b_s[t % 2][:, SW * hd:SW * hd + SW], q_st[:, hd, P * t:P * t + P],
                                             kk[:, w, hd, P * t:P * t + SW], start=(w == 0), stop=(w == 1))
                x.then_inc(S["s"], 1)

            def transposes(need, i, t):
                n = CT * i + t
                need("pn", n + 1)
                need("tlo", n, apart=True)
                for hd in range(2):
                    p = prob[:, n % RING, hd, :]
                    nc.tensor.transpose(b_t[:, KW * hd:KW * hd + WIN], p[0:WIN, 0:P], ident[0:WIN, 0:WIN])
                    x = nc.tensor.transpose(b_t[:, KW * hd + WIN:KW * hd + KW], p[:, P:], ident[:])
                x.then_inc(S["t"], 1)

            def pv(need, i, hd):
                need("tlo", CT * (i + 1))
                need("olo", 2 * i + hd)
                for j in range(CT + 1):
                    for w in range(2):
                        x = nc.tensor.matmul(b_o[:, BLOCK_AT[j]:BLOCK_AT[j] + SW], v_st[:, j, 2 * i + hd, :],
                                             pT[w][:, hd, SW * j:SW * j + SW], start=(j == 0 and w == 0),
                                             stop=(j == CT and w == 1), skip_group_check=True)
                x.then_inc(S["pv"], 1)

            def out_proj(need, i, hd, ts):
                need("olo", 2 * i + hd + 1)
                if i == 0 and hd == 0:
                    need("res2", 0)
                for t in ts:
                    for n, (a, e) in enumerate(SPLIT3):
                        first = i == 0 and hd == 0 and n == 0
                        x = nc.tensor.matmul(b_wo[t // 2][:, D * (t % 2):D * (t % 2) + D], oT[a][:, hd, P * t:P * t + P],
                                             wo[e][:, 2 * i + hd, :], start=(first and t % 2 == 0),
                                             stop=(i == HP - 1 and hd == 1 and n == 2), skip_group_check=True)
                if ts[-1] == CT - 1:
                    x.then_inc(S["wo"], 1)

            def h_transposes(nxt, k):
                nxt("h", CT)
                nxt("klo", 0)
                nxt("qlo", 0)
                for t in range(CT):
                    x = nc.tensor.transpose((b_k, b_q)[k][:, P * t:P * t + P], xa[:, t, P * k:P * k + P], ident[:])
                x.then_inc(S["hT"], 1)

            def values(nxt, n):
                half, t = n // CT, n % CT
                nxt("hlo", KD)
                nxt("vlo", n - 1)
                for x_part, (a, e) in enumerate(SPLIT3):
                    for k in range(KD):
                        x = nc.tensor.matmul((b_q, b_k)[n % 2][:], hT[a][:, k, P * t:P * t + P],
                                             wqkv[e][:, k, 2 * H1 * DH + 512 * half:2 * H1 * DH + 512 * half + 512],
                                             start=(x_part == 0 and k == 0), stop=(x_part == 2 and k == KD - 1))
                x.then_inc(S["vp"], 1)

            def first(nxt, m):
                for k in range(KD):
                    h_transposes(nxt, k)
                for n in range(2 * CT):
                    values(nxt, n)
                nxt("vlo", 2 * CT)
                pk(nxt, 0)
                pq(nxt, 0)

            def body(need, nxt, g, m):
                for i in range(HP + 1):
                    now, last, before = i < HP, i > 0, i > 1
                    if last:
                        transposes(need, i - 1, 0)
                    if before:
                        out_proj(need, i - 2, 0, [0, 1, 2, 3])
                    if last:
                        transposes(need, i - 1, 1)
                    if now:
                        scores(need, i, 0)
                        scores(need, i, 1)
                    if i == HP:
                        values(nxt, 0)
                        values(nxt, 1)
                    if before:
                        out_proj(need, i - 2, 1, [0, 1])
                    if last:
                        transposes(need, i - 1, 2)
                    if now:
                        scores(need, i, 2)
                    if before:
                        out_proj(need, i - 2, 1, [2, 3])
                    if i == HP:
                        values(nxt, 2)
                    if last:
                        transposes(need, i - 1, 3)
                    if now:
                        scores(need, i, 3)
                    if i + 1 < HP:
                        pk(need, i + 1)
                    if i + 1 == HP:
                        h_transposes(nxt, 0)
                    if last:
                        pv(need, i - 1, 0)
                    if i + 1 < HP:
                        pq(need, i + 1)
                    if i + 1 == HP:
                        h_transposes(nxt, 1)
                    if i == HP:
                        values(nxt, 3)
                    if last:
                        pv(need, i - 1, 1)
                values(nxt, CT)
                values(nxt, CT + 1)
                out_proj(need, HP - 1, 0, [0, 1, 2, 3])
                values(nxt, CT + 2)
                out_proj(need, HP - 1, 1, [0, 1, 2, 3])
                values(nxt, CT + 3)
                nxt("vlo", 2 * CT)
                pk(nxt, 0)
                pq(nxt, 0)
            pe.wait_ge(S["init"], INIT)
            chunks(pe, first, body)



SPLIT3 = ((0, 0), (0, 1), (1, 0))


def split_weights(nc, sems, name, sources):
    s_w, s_hi, s_lo = (sems.take(f"{name}_{n}") for n in ("raw", "hi", "lo"))
    loads = sum(len(src[0]) for src in sources)

    def load(sp):
        for drams, raw, hi, lo in sources:
            for dram, at in drams:
                sp.dma_start(at, dram).then_inc(s_w, 16)

    def scalar(act):
        act.wait_ge(s_w, 16 * loads)
        for drams, raw, hi, lo in sources:
            nc.scalar.copy(hi, raw).then_inc(s_hi, 1)

    def vector(dve):
        for i, (drams, raw, hi, lo) in enumerate(sources):
            dve.wait_ge(s_hi, i + 1)
            nc.vector.tensor_tensor(lo, raw, hi.bitcast(F32), ALU.subtract).then_inc(s_lo, 1)

    return load, scalar, vector


def make_ident(nc, pool, ident, s_id):
    nc.gpsimd.memset(ident[:], 0.0).then_inc(s_id, 1)
    pool.wait_ge(s_id, 1)
    nc.gpsimd.affine_select(out=ident[:], in_=ident[:], compare_op=ALU.not_equal, fill=1.0, base=0,
                            pattern=[[-1, P]], channel_multiplier=1).then_inc(s_id, 1)


def latent_attention(nc, sems, A, x1, x2):
    with ExitStack() as ctx:
        sb = lambda n, s, d: ctx.enter_context(nc.sbuf_tensor("la_" + n, s, d))
        wq = [sb(f"wq{s}", [P, KD, H2, P], F32R) for s in ("hi", "lo")]
        wk = [sb(f"wk{s}", [P, KD, P], F32R) for s in ("hi", "lo")]
        wv = [sb(f"wv{s}", [P, KD, D], F32R) for s in ("hi", "lo")]
        wo = [sb(f"wo{s}", [P, H2, D], F32R) for s in ("hi", "lo")]
        ident = sb("ident", [P, P], F32)
        bc = sb("bc", [P, 2, NB, D], F32)
        g1 = sb("g1", [P, D], F32)

        with ExitStack() as c2:
            raw = lambda n, s: c2.enter_context(nc.sbuf_tensor("la_raw_" + n, s, F32))
            rq, rk, rv, ro = raw("q", [P, KD * H2 * P]), raw("k", [P, KD * P]), raw("v", [P, KD * D]), raw("o", [P, H2 * D])
            s_id = sems.take("la0_id")
            s_g1 = sems.take("la0_g1")
            flat = lambda w: [x[:].rearrange("p a b -> p (a b)") for x in w]
            flat4 = lambda w: [x[:].rearrange("p a b c -> p (a b c)") for x in w]
            load, mscalar, mtensor, mvector, (s_bc, n_bc) = modulation_rows(
                nc, sems, "la0_", c2, A, (3, 4), bc, (False, True))
            wload, wscalar, wvector = split_weights(nc, sems, "la0_w", [
                ([(A["wq2"], rq[:])], rq[:], *flat4(wq)),
                ([(A["wk2"], rk[:])], rk[:], *flat(wk)),
                ([(A["wv2"], rv[:])], rv[:], *flat(wv)),
                ([(A["wo2"], ro[0:64, :]), (A["wo2"], ro[64:P, :])], ro[:], *flat(wo))])
            block = c2.enter_context(nc.Block())

            @block.sync
            def _(sp):
                load(sp)
                wload(sp)
                sp.dma_start(g1[:], A["g1"].to_broadcast([P, D])).then_inc(s_g1, 16)
                sp.wait_ge(s_g1, 16)

            @block.scalar
            def _(act):
                mscalar(act)
                wscalar(act)

            @block.vector
            def _(dve):
                mvector(dve)
                wvector(dve)

            @block.tensor
            def _(pe):
                mtensor(pe)

            @block.gpsimd
            def _(pool):
                make_ident(nc, pool, ident, s_id)
                pool.wait_ge(s_id, 2)

        xa = sb("xa", [P, CT, D], F32)
        square = sb("square", [P, D], F32)
        stats = sb("stats", [P, CT, 6], F32)
        mv = sb("mv", [P, CT, 2], F32)
        rstd = sb("rstd", [P, CT], F32)
        var = sb("var", [P, CT], F32)
        newton = sb("newton", [P, CT], F32)
        rrms = sb("rrms", [P, CT], F32)
        ms = sb("ms", [P, CT], F32)
        nxT = [sb(f"nxT{s}", [P, KD, CH], F32R) for s in ("hi", "lo")]
        q_st = sb("q_st", [P, H2, SEQ], F32R)
        kk = [sb(f"k{s}", [P, SEQ], F32R) for s in ("hi", "lo")]
        v_st = sb("v_st", [P, KT, P], F32R)
        q_now = sb("q_now", [P, H2, P], F32R)
        prob = sb("prob", [P, H2, SEQ], F32)
        HALF = SEQ // 2
        mx = sb("mx", [P, H2, 2], F32)
        nmax = sb("nmax", [P, H2], F32)
        rsum = sb("rsum", [P, H2, 2], F32)
        rtot = sb("rtot", [P, H2], F32)
        rinv = sb("rinv", [P, H2], F32)
        pT = [sb(f"pT{s}", [P, KT, 2, P], F32R) for s in ("hi", "lo")]
        oT = [sb(f"oT{s}", [P, H2, P], F32R) for s in ("hi", "lo")]

        b_s = ctx.enter_context(nc.psum_tensor("la_b_s", [P, 4, 512], F32))
        b_t = [ctx.enter_context(nc.psum_tensor(f"la_b_t{i}", [P, 512], F32)) for i in range(2)]
        b_o = ctx.enter_context(nc.psum_tensor("la_b_o", [P, 512], F32))
        b_y = ctx.enter_context(nc.psum_tensor("la_b_y", [P, 512], F32))

        PREP = dict(x=16, bn=CT, ag=CT, nwt=3, var=1, sd=1, rs=1, xn=CT, hm=CT, h=CT, keep=1, sq=CT, ms=1, sd2=1, rs2=1, nwt2=3, nr=CT,
                    nx=CT, nT=KD, nhi=KD, nlo=KD, qp=H2, qhi=H2, qlo=H2, kp=1, khi=1, klo=1, vp=2, vhi=2, vlo=2)
        TILE = dict(qn=H2, s=2 * H2, mxp=2 * H2, mxt=H2, nm=H2, exp=2 * H2, rt=H2, rc=H2, pn=H2, t=4 * H2, thi=4 * H2,
                    tlo=4 * H2, pv=2, ohi=2, olo=2, y=1, res=1)
        S = {n: sems.take("la_" + n) for n in [*PREP, *TILE, "carrier"]}
        begin_counts(nc, [S[n] for n in (*PREP, *TILE)])
        block = ctx.enter_context(nc.Block())

        def phases(eng, prep, tile, drain):
            with eng.Fori(0, NB) as b:
                def tiles_need(name, n, apart=False):
                    if name in PREP:
                        eng.wait_ge(S[name], START + b * (NC * PREP[name]) + (NC * PREP[name] if n is None else max(n, 0)))
                    else:
                        eng.wait_ge(S[name], START + b * (NT * TILE[name]) + max(n, 0))
                    if apart or eng is nc.sync:
                        eng.sem_inc(S["carrier"], 1)

                with eng.Fori(0, NC) as c:
                    def need(name, n, apart=False):
                        g = b * NC + c
                        if name in PREP:
                            eng.wait_ge(S[name], START + g * PREP[name] + max(n, 0))
                        else:
                            eng.wait_ge(S[name], START + b * (NT * TILE[name]))
                        if apart or eng is nc.sync:
                            eng.sem_inc(S["carrier"], 1)
                    prep(need, b, c)
                tile(lambda name, n, apart=False: tiles_need(name, n, apart), b, 0, True)
                with eng.Fori(1, NT) as n:
                    def later(name, k, apart=False):
                        if name in PREP:
                            eng.wait_ge(S[name], START + (b + 1) * (NC * PREP[name]))
                        else:
                            eng.wait_ge(S[name], START + (b * NT + n) * TILE[name] + k)
                        if apart or eng is nc.sync:
                            eng.sem_inc(S["carrier"], 1)
                    tile(later, b, n, False)
                drain(lambda name, k, apart=False: tiles_need(name, NT * TILE[name] + k, apart), b)

        @block.sync
        def _(sp):
            def prep(need, b, c):
                need("nT", 0)
                sp.dma_start(xa[:], x1[:, bass.ds((b * NC + c) * CT, CT), :]).then_inc(S["x"], 16)
            phases(sp, prep, lambda *a: None, lambda *a: None)

        @block.gpsimd
        def _(pool):
            def prep(need, b, c):
                for t in range(CT):
                    for j, (was, now) in zip((1, 0), (("xn", "hm"), ("hm", "h"))):
                        need(was, t + 1, apart=True)
                        nc.gpsimd.tensor_tensor(xa[:, t, :], xa[:, t, :], bc[:, j, bass.ds(b, 1), :].rearrange("p o d -> p (o d)"),
                                                ALU.mult if j else ALU.add).then_inc(S[now], 1)
                for t in range(CT):
                    need("nr", t + 1, apart=True)
                    nc.gpsimd.tensor_tensor(xa[:, t, :], xa[:, t, :], g1[:], ALU.mult).then_inc(S["nx"], 1)

            def tile(need, b, n, first):
                for h in range(H2):
                    if first:
                        need("qlo", None, apart=True)
                    need("s", 2 * (h - H2) + 2, apart=True)
                    nc.gpsimd.tensor_copy(q_now[:, h, :], q_st[:, h, bass.ds(n * P, P)]).then_inc(S["qn"], 1)
                for h in range(H2):
                    need("rc", h + 1, apart=True)
                    p = prob[:, h, :]
                    nc.gpsimd.tensor_scalar(p, p, rinv[:, h:h + 1], 1.0, ALU.mult, ALU.mult).then_inc(S["pn"], 1)
            phases(pool, prep, tile, lambda *a: None)

        @block.scalar
        def _(act):
            def prep(need, b, c):
                need("var", 1)
                nc.scalar.activation(rstd[:], var[:], ACT.Sqrt).then_inc(S["sd"], 1)
                need("ms", 1)
                nc.scalar.activation(rrms[:], ms[:], ACT.Sqrt).then_inc(S["sd2"], 1)
                for k in range(KD):
                    need("nT", k + 1)
                    nc.scalar.copy(nxT[0][:, k, :], b_t[k][:]).then_inc(S["nhi"], 1)
                for h in range(H2):
                    need("qp", h + 1)
                    nc.scalar.activation(q_st[:, h, bass.ds(c * CH, CH)], b_s[:, h, :], ACT.Copy,
                                         scale=float(DH) ** -0.5).then_inc(S["qhi"], 1)
                need("kp", 1)
                nc.scalar.copy(kk[0][:, bass.ds(c * CH, CH)], b_t[0][:]).then_inc(S["khi"], 1)
                for j in range(2):
                    need("vp", j + 1)
                    nc.scalar.copy(v_st[:, bass.ds(c * CT + 2 * j, 2), 0:DH],
                                   (b_t[1], b_o)[j][:].rearrange("p (t n) -> p t n", t=2)[:, :, 0:DH]).then_inc(S["vhi"], 1)

            def t_hi(need, m, h):
                for j in range(4):
                    need("t", 4 * m + j + 1)
                    need("pv", m // 2)
                    nc.scalar.copy(pT[0][:, 4 * j:4 * j + 4, h % 2, :],
                                   b_t[j % 2][:].rearrange("p (k n) -> p k n", k=4)).then_inc(S["thi"], 1)

            def o_hi(need, pair, k):
                need("pv", pair + 1)
                need("y", pair // 2)
                nc.scalar.copy(oT[0][:, 2 * k:2 * k + 2, :],
                               b_o[:, 0:2 * P].rearrange("p (h n) -> p h n", h=2)).then_inc(S["ohi"], 1)

            def slot(need, m, h, run):
                if run:
                    need("pn", m - H2 + 1 if m >= H2 else m - H2 + 1)
                    need("t", 4 * (m - H2) + 4)
                    for j in range(2):
                        if j == 0:
                            need("nm", m + 1)
                        nc.scalar.activation(prob[:, h, HALF * j:HALF * j + HALF],
                                             b_s[:, 2 * j:2 * j + 2, :].rearrange("p a n -> p (a n)"), ACT.Exp,
                                             bias=nmax[:, h:h + 1], scale=1.0,
                                             accum_out=rsum[:, h, j:j + 1]).then_inc(S["exp"], 1)

            def tile(need, b, n, first):
                for m in range(H2):
                    slot(need, m, m, True)
                    if m % 2 == 0 and (m >= 4 or not first):
                        o_hi(need, (m - 4) // 2, ((m - 4) // 2) % 2)
                    if m >= 2 or not first:
                        t_hi(need, m - 2, (m - 2) % H2)

            def drain(need, b):
                for m in range(H2):
                    if m % 2 == 0:
                        o_hi(need, (m - 4) // 2, ((m - 4) // 2) % 2)
                    if m < 2:
                        t_hi(need, m - 2, (m - 2) % H2)
            phases(act, prep, tile, drain)

        @block.vector
        def _(dve):
            def lo(out, psum, hi):
                return nc.vector.tensor_tensor(out, psum, hi.bitcast(F32), ALU.subtract)

            def prep(need, b, c):
                need("x", 16)
                for t in range(CT):
                    nc.vector.bn_stats(stats[:, t, :], xa[:, t, :]).then_inc(S["bn"], 1)
                for t in range(CT):
                    need("bn", t + 1, apart=True)
                    nc.vector.bn_aggr(mv[:, t, :], stats[:, t, :]).then_inc(S["ag"], 1)
                need("ag", CT)
                nc.vector.tensor_scalar(var[:], mv[:, :, 1], EPS_LN, None, ALU.add).then_inc(S["var"], 1)
                need("sd", 1)
                nc.vector.reciprocal(rstd[:], rstd[:]).then_inc(S["rs"], 1)
                need("rs", 1)
                newton_rsqrt(nc, dve, rstd[:], var[:], newton[:], lambda k: need("nwt", k), S["nwt"])
                for t in range(CT):
                    nc.vector.tensor_scalar(xa[:, t, :], xa[:, t, :], mv[:, t, 0:1], rstd[:, t:t + 1],
                                            ALU.subtract, ALU.mult).then_inc(S["xn"], 1)
                need("h", CT)
                nc.vector.tensor_copy(x2[:, bass.ds((b * NC + c) * CT, CT), :], xa[:]).then_inc(S["keep"], 1)
                for t in range(CT):
                    need("h", t + 1, apart=True)
                    if t:
                        need("sq", t, apart=True)
                    nc.vector.tensor_tensor_reduce(square[:], xa[:, t, :], xa[:, t, :], 1.0, 0.0, ALU.mult, ALU.add,
                                                   ms[:, t:t + 1]).then_inc(S["sq"], 1)
                need("sq", CT)
                nc.vector.tensor_scalar(ms[:], ms[:], 1.0 / D, EPS_RMS, ALU.mult, ALU.add).then_inc(S["ms"], 1)
                need("sd2", 1)
                nc.vector.reciprocal(rrms[:], rrms[:]).then_inc(S["rs2"], 1)
                need("rs2", 1)
                newton_rsqrt(nc, dve, rrms[:], ms[:], newton[:], lambda k: need("nwt2", k), S["nwt2"])
                need("keep", 1)
                for t in range(CT):
                    nc.vector.tensor_scalar(xa[:, t, :], xa[:, t, :], rrms[:, t:t + 1], None,
                                            ALU.mult).then_inc(S["nr"], 1)
                for k in range(KD):
                    need("nhi", k + 1)
                    lo(nxT[1][:, k, :], b_t[k][:], nxT[0][:, k, :]).then_inc(S["nlo"], 1)
                for h in range(H2):
                    need("qhi", h + 1)
                    q = q_st[DH:P, h, bass.ds(c * CH, CH)]
                    nc.vector.scalar_tensor_tensor(out=q, in0=b_s[DH:P, h, :], scalar=float(DH) ** -0.5,
                                                   in1=q.bitcast(F32), op0=ALU.mult, op1=ALU.subtract).then_inc(S["qlo"], 1)
                need("khi", 1)
                lo(kk[1][:, bass.ds(c * CH, CH)], b_t[0][:], kk[0][:, bass.ds(c * CH, CH)]).then_inc(S["klo"], 1)
                for j in range(2):
                    need("vhi", j + 1)
                    lo(v_st[:, bass.ds(c * CT + 2 * j, 2), DH:P], (b_t[1], b_o)[j][:].rearrange("p (t n) -> p t n", t=2)[:, :, 0:DH],
                       v_st[:, bass.ds(c * CT + 2 * j, 2), 0:DH]).then_inc(S["vlo"], 1)

            def maxes(need, m, h):
                for j in range(2):
                    need("s", 2 * m + j + 1)
                    nc.vector.tensor_reduce(mx[:, h, j:j + 1], b_s[:, 2 * j:2 * j + 2, :].rearrange("p a n -> p (a n)"),
                                            AX.X, ALU.max).then_inc(S["mxp"], 1)
                need("mxp", 2 * m + 2)
                nc.vector.tensor_reduce(nmax[:, h:h + 1], mx[:, h, :], AX.X, ALU.max, negate=True).then_inc(S["nm"], 1)

            def sums(need, m, h):
                need("exp", 2 * m + 2)
                nc.vector.tensor_reduce(rtot[:, h:h + 1], rsum[:, h, :], AX.X, ALU.add).then_inc(S["rt"], 1)
                need("rt", m + 1)
                nc.vector.reciprocal(rinv[:, h:h + 1], rtot[:, h:h + 1]).then_inc(S["rc"], 1)

            def t_lo(need, m, h):
                for j in range(4):
                    need("thi", 4 * m + j + 1)
                    lo(pT[1][:, 4 * j:4 * j + 4, h % 2, :], b_t[j % 2][:].rearrange("p (k n) -> p k n", k=4),
                       pT[0][:, 4 * j:4 * j + 4, h % 2, :]).then_inc(S["tlo"], 1)

            def o_lo(need, pair, k):
                need("ohi", pair + 1)
                lo(oT[1][:, 2 * k:2 * k + 2, :], b_o[:, 0:2 * P].rearrange("p (h n) -> p h n", h=2),
                   oT[0][:, 2 * k:2 * k + 2, :]).then_inc(S["olo"], 1)

            def add_y(need, b, n):
                need("y", 0)
                at = x2[:, bass.ds(b * NT + n, 1), :].rearrange("p o d -> p (o d)")
                nc.vector.tensor_tensor(at, b_y[:, 0:D], at, ALU.add).then_inc(S["res"], 1)

            def tile(need, b, n, first):
                for m in range(H2):
                    maxes(need, m, m)
                    if m % 2 == 0 and not first:
                        o_lo(need, (m - 4) // 2, ((m - 4) // 2) % 2)
                    if m >= 2 or not first:
                        t_lo(need, m - 2, (m - 2) % H2)
                    sums(need, m, m)
                    if m == 3 and not first:
                        add_y(need, b, n - 1)

            def drain(need, b):
                for m in range(H2):
                    if m % 2 == 0:
                        o_lo(need, (m - 4) // 2, ((m - 4) // 2) % 2)
                    if m < 2:
                        t_lo(need, m - 2, (m - 2) % H2)
                add_y(need, b, NT - 1)
            phases(dve, prep, tile, drain)

        @block.tensor
        def _(pe):

            def product(out, left, right):
                for n, (a, e) in enumerate(SPLIT3):
                    for k in range(KD):
                        x = nc.tensor.matmul(out, left(a, k), right(e, k), start=(n == 0 and k == 0),
                                             stop=(n == 2 and k == KD - 1), skip_group_check=True)
                return x

            def prep(need, b, c):
                need("olo", 0)
                need("tlo", 0)
                need("vlo", 0)
                need("klo", 0)
                for k in range(KD):
                    need("nx", CT)
                    for t in range(CT):
                        x = nc.tensor.transpose(b_t[k][:, P * t:P * t + P], xa[:, t, P * k:P * k + P], ident[:])
                    x.then_inc(S["nT"], 1)
                need("nlo", KD)
                need("exp", 0)
                need("qlo", 0)
                for h in range(H2):
                    product(b_s[:, h, :], lambda a, k: wq[a][:, k, h, :], lambda e, k: nxT[e][:, k, :]).then_inc(S["qp"], 1)
                product(b_t[0][:], lambda a, k: wk[a][:, k, :], lambda e, k: nxT[e][:, k, :]).then_inc(S["kp"], 1)
                for j in range(2):
                    for i in range(2):
                        t = 2 * j + i
                        for n, (a, e) in enumerate(SPLIT3):
                            for k in range(KD):
                                x = nc.tensor.matmul((b_t[1], b_o)[j][:, D * i:D * i + D], nxT[a][:, k, P * t:P * t + P],
                                                     wv[e][:, k, :], start=(i == 0 and n == 0 and k == 0),
                                                     stop=(n == 2 and k == KD - 1), skip_group_check=True)
                    x.then_inc(S["vp"], 1)

            def scores(need, m, h, first):
                need("qn", m + 1)
                if first:
                    need("klo", None)
                    need("qlo", None)
                need("exp", 2 * m)
                for j in range(4):
                    for w in range(2):
                        x = nc.tensor.matmul(b_s[:, j, :], q_now[:, h, :], kk[w][:, 512 * j:512 * j + 512],
                                             start=(w == 0), stop=(w == 1))
                    if j % 2:
                        x.then_inc(S["s"], 1)

            def transposes(need, m, h, first):
                need("pn", m + 1)
                for j in range(4):
                    need("tlo", 4 * m + j - 1)
                    if first:
                        need("vlo", None)
                    for i in range(4):
                        k = 4 * j + i
                        x = nc.tensor.transpose(b_t[j % 2][:, P * i:P * i + P], prob[:, h, P * k:P * k + P], ident[:])
                    x.then_inc(S["t"], 1)

            def pv(need, pair):
                need("tlo", 8 * pair + 8)
                need("olo", pair)
                for k in range(KT):
                    for w in range(2):
                        x = nc.tensor.matmul(b_o[:, 0:2 * P], v_st[:, k, :], pT[w][:, k, :, :].rearrange("p h n -> p (h n)"),
                                             start=(k == 0 and w == 0), stop=(k == KT - 1 and w == 1))
                x.then_inc(S["pv"], 1)

            def out_proj(need):
                need("olo", 0)
                need("res", -1)
                for h in range(H2):
                    for n, (a, e) in enumerate(SPLIT3):
                        x = nc.tensor.matmul(b_y[:, 0:D], oT[a][:, h, :], wo[e][:, h, :], start=(h == 0 and n == 0),
                                             stop=(h == H2 - 1 and n == 2))
                x.then_inc(S["y"], 1)

            def tile(need, b, n, first):
                for m in range(H2):
                    scores(need, m, m, first and m == 0)
                    if m % 2 == 0 and not first:
                        pv(need, (m - 4) // 2)
                    if m >= 2 or not first:
                        transposes(need, m - 2, (m - 2) % H2, first and m == 2)
                    if m == 3 and not first:
                        out_proj(need)

            def drain(need, b):
                for m in range(H2):
                    if m % 2 == 0:
                        pv(need, (m - 4) // 2)
                    if m < 2:
                        transposes(need, m - 2, (m - 2) % H2, False)
                out_proj(need)
            phases(pe, prep, tile, drain)


def experts(nc, sems, A, x1, x2, out):
    NX = NE + 1
    TT = TOK // P
    with ExitStack() as ctx:
        sb = lambda n, s, d: ctx.enter_context(nc.sbuf_tensor("ex_" + n, s, d))
        bc = sb("bc", [P, 1, NB, D], F32)
        gate_size = sb("gate_size", [P, NB, D], F32)
        ident = sb("ident", [P, P], F32)
        g2 = sb("g2", [P, D], F32)
        bias = sb("bias", [P, NE], F32)
        rank = sb("rank", [P, NE], F32)
        wr = [sb(f"wr{s}", [P, KD, P], F32R) for s in ("hi", "lo")]
        with ExitStack() as c2:
            raw = c2.enter_context(nc.sbuf_tensor("ex_raw", [P, KD * P], F32))
            s_id, s_in, s_g, s_rank = (sems.take("ex0_" + n) for n in ("id", "in", "g", "rank"))
            load, mscalar, mtensor, mvector, (s_bc, n_bc) = modulation_rows(nc, sems, "ex0_", c2, A, (5,), bc, (False,))
            wload, wscalar, wvector = split_weights(nc, sems, "ex0_w", [
                ([(A["wr16"], raw[:])], raw[:], *[w[:].rearrange("p k n -> p (k n)") for w in wr])])
            block = c2.enter_context(nc.Block())

            @block.sync
            def _(sp):
                load(sp)
                wload(sp)
                sp.dma_start(g2[:], A["g2"].to_broadcast([P, D])).then_inc(s_in, 16)
                sp.dma_start(bias[:], A["bias"].to_broadcast([P, NE])).then_inc(s_in, 16)
                sp.wait_ge(s_in, 32)

            @block.scalar
            def _(act):
                mscalar(act)
                wscalar(act)

            @block.vector
            def _(dve):
                mvector(dve)
                wvector(dve)
                dve.wait_ge(s_bc, n_bc)
                floor_gate(nc, dve, bc[:, 0, :, :], gate_size[:], s_g)

            @block.tensor
            def _(pe):
                mtensor(pe)

            @block.gpsimd
            def _(pool):
                make_ident(nc, pool, ident, s_id)
                for e in range(NE):
                    nc.gpsimd.memset(rank[:, e:e + 1], float(NE - e)).then_inc(s_rank, 1)
                pool.wait_ge(s_rank, NE)
                pool.wait_ge(s_id, 2)

        xfT = [sb(f"xfT{s}", [P, KD, TOK], F32R) for s in ("hi", "lo")]
        comb = sb("comb", [P, TT, NX], F32)

        with ExitStack() as c2:
            sb2 = lambda n, s, d: c2.enter_context(nc.sbuf_tensor("ro_" + n, s, d))
            xa = sb2("xa", [P, CT, D], F32)
            square = sb2("square", [P, D], F32)
            ss = sb2("ss", [P, CT], F32)
            ms = sb2("ms", [P, CT], F32)
            rrms = sb2("rrms", [P, CT], F32)
            newton = sb2("newton", [P, CT], F32)
            lgT = sb2("lgT", [P, CH], F32)
            lg = sb2("lg", [P, TT, NE], F32)
            lg2 = sb2("lg2", [P, TT, NE], F32)
            pick = [sb2(f"pick{i}", [P, TT, NE], F32) for i in range(2)]
            top = [sb2(f"top{i}", [P, TT], F32) for i in range(6)]
            b_x = [c2.enter_context(nc.psum_tensor(f"ro_b_x{i}", [P, 512], F32)) for i in range(2)]
            b_l = c2.enter_context(nc.psum_tensor("ro_b_l", [P, 512], F32))
            b_r = c2.enter_context(nc.psum_tensor("ro_b_r", [P, 512], F32))
            PER = dict(sq=CT, ms=1, sd=1, rs=1, nwt=3, nr=CT, nx=CT, xT=KD, xhi=KD, xlo=KD, lg=1, lgc=1, lt=1, lb=1)
            S = {n: sems.take("ro_" + n) for n in [*PER, "carrier", "one"]}
            s_step = sems.take("ro_step")
            s_exp = sems.take("ro_exp")
            begin_counts(nc, [S[n] for n in PER])
            block = c2.enter_context(nc.Block())

            def chunks(eng, body):
                with eng.Fori(0, NG) as g:
                    def need(name, n, apart=False):
                        eng.wait_ge(S[name], START + g * PER[name] + max(n, 0))
                        if apart:
                            eng.sem_inc(S["carrier"], 1)
                    body(need, g)

            wide = lambda a: a.rearrange("p (t o) -> p t o", o=1).to_broadcast([P, TT, NE])

            @block.scalar
            def _(act):
                def body(need, g):
                    need("ms", 0)
                    for t in range(CT):
                        if t:
                            need("sq", t)
                        at = x2[:, bass.ds(g * CT + t, 1), :].rearrange("p o d -> p (o d)")
                        nc.scalar.activation(square[:], at, ACT.Square, accum_out=ss[:, t:t + 1]).then_inc(S["sq"], 1)
                    need("ms", 1)
                    nc.scalar.activation(rrms[:], ms[:], ACT.Sqrt).then_inc(S["sd"], 1)
                    for k in range(KD):
                        need("xT", k + 1)
                        nc.scalar.copy(xfT[0][:, k, bass.ds(g * CH, CH)], b_x[k][:]).then_inc(S["xhi"], 1)
                    need("lg", 1)
                    need("lt", 0)
                    nc.scalar.copy(lgT[:], b_l[:]).then_inc(S["lgc"], 1)
                chunks(act, body)
                for j in range(2):
                    act.wait_ge(s_step, (2, 17)[j])
                    a = (lg2[:].rearrange("p t e -> p (t e)"), top[2][:])[j]
                    nc.scalar.activation(a, a, ACT.Exp).then_inc(s_exp, 1)

            @block.gpsimd
            def _(pool):
                nc.gpsimd.memset(comb[:, :, NE:NX], 1.0).then_inc(S["one"], 1)

                def body(need, g):
                    for t in range(CT):
                        need("nr", t + 1, apart=True)
                        nc.gpsimd.tensor_tensor(xa[:, t, :], xa[:, t, :], g2[:], ALU.mult).then_inc(S["nx"], 1)
                chunks(pool, body)
                pool.wait_ge(S["one"], 1)

            @block.vector
            def _(dve):
                def body(need, g):
                    need("sq", CT)
                    nc.vector.tensor_scalar(ms[:], ss[:], 1.0 / D, EPS_RMS, ALU.mult, ALU.add).then_inc(S["ms"], 1)
                    need("sd", 1)
                    nc.vector.reciprocal(rrms[:], rrms[:]).then_inc(S["rs"], 1)
                    need("rs", 1)
                    newton_rsqrt(nc, dve, rrms[:], ms[:], newton[:], lambda k: need("nwt", k), S["nwt"])
                    need("xT", 0)
                    for t in range(CT):
                        at = x2[:, bass.ds(g * CT + t, 1), :].rearrange("p o d -> p (o d)")
                        nc.vector.tensor_scalar(xa[:, t, :], at, rrms[:, t:t + 1], None, ALU.mult).then_inc(S["nr"], 1)
                    for k in range(KD):
                        need("xhi", k + 1)
                        nc.vector.tensor_tensor(xfT[1][:, k, bass.ds(g * CH, CH)], b_x[k][:],
                                                xfT[0][:, k, bass.ds(g * CH, CH)].bitcast(F32), ALU.subtract).then_inc(S["xlo"], 1)
                    need("lt", 1)
                    nc.vector.tensor_tensor(lg[:, bass.ds(g * CT, CT), :], b_r[:].rearrange("p (t n) -> p t n", t=CT)[:, :, 0:NE],
                                            bias[:].rearrange("p (o e) -> p o e", o=1).to_broadcast([P, CT, NE]),
                                            ALU.add).then_inc(S["lb"], 1)
                chunks(dve, body)

                at = [0]

                def step(x):
                    at[0] += 1
                    x.then_inc(s_step, 1)
                    dve.wait_ge(s_step, at[0])
                dve.wait_ge(S["lb"], START + NG)
                v = nc.vector
                step(v.tensor_reduce(top[0][:], lg[:], AX.X, ALU.max))
                step(v.tensor_tensor(lg2[:], lg[:], wide(top[0][:]), ALU.subtract))
                dve.wait_ge(s_exp, 1)
                step(v.tensor_reduce(top[0][:], lg2[:], AX.X, ALU.add))
                step(v.reciprocal(top[0][:], top[0][:]))
                step(v.tensor_tensor(lg[:], lg2[:], wide(top[0][:]), ALU.mult))
                for i in range(2):
                    step(v.tensor_reduce(top[i][:], lg[:], AX.X, ALU.max))
                    step(v.tensor_tensor(pick[i][:], lg[:], wide(top[i][:]), ALU.is_equal))
                    step(v.tensor_tensor(pick[i][:], pick[i][:],
                                         rank[:].rearrange("p (o e) -> p o e", o=1).to_broadcast([P, TT, NE]), ALU.mult))
                    step(v.tensor_reduce(top[4][:], pick[i][:], AX.X, ALU.max))
                    step(v.tensor_tensor(pick[i][:], pick[i][:], wide(top[4][:]), ALU.is_equal))
                    if i == 0:
                        step(v.scalar_tensor_tensor(out=lg[:], in0=pick[0][:], scalar=-4.0, in1=lg[:], op0=ALU.mult, op1=ALU.add))
                step(v.tensor_tensor(top[2][:], top[1][:], top[0][:], ALU.subtract))
                assert at[0] == 17, at
                dve.wait_ge(s_exp, 2)
                step(v.tensor_scalar(top[3][:], top[2][:], 1.0, None, ALU.add))
                step(v.reciprocal(top[3][:], top[3][:]))
                step(v.tensor_tensor(top[2][:], top[2][:], top[3][:], ALU.mult))
                for i in range(2):
                    step(v.tensor_tensor(pick[i][:], pick[i][:], wide(top[3 - i][:]), ALU.mult))
                step(v.tensor_tensor(comb[:, :, 0:NE], pick[0][:], pick[1][:], ALU.add))

            @block.tensor
            def _(pe):

                def body(need, g):
                    need("nx", CT)
                    need("xlo", 0)
                    for k in range(KD):
                        for t in range(CT):
                            x = nc.tensor.transpose(b_x[k][:, P * t:P * t + P], xa[:, t, P * k:P * k + P], ident[:])
                        x.then_inc(S["xT"], 1)
                    need("xlo", KD)
                    need("lgc", 0)
                    for n, (a, e) in enumerate(SPLIT3):
                        for k in range(KD):
                            x = nc.tensor.matmul(b_l[:], wr[a][:, k, :], xfT[e][:, k, bass.ds(g * CH, CH)],
                                                 start=(n == 0 and k == 0), stop=(n == 2 and k == KD - 1))
                    x.then_inc(S["lg"], 1)
                    need("lgc", 1)
                    need("lb", 0)
                    for t in range(CT):
                        x = nc.tensor.transpose(b_r[:, P * t:P * t + P], lgT[:, P * t:P * t + P], ident[:])
                    x.then_inc(S["lt"], 1)
                chunks(pe, body)

        raw = sb("raw_w", [P, 3 * KD, FF], F32)
        w13 = [[sb(f"w13_{i}{s}", [P, 2 * KD, FF], F32R) for s in ("hi", "lo")] for i in range(2)]
        w2 = [[sb(f"w2_{i}{s}", [P, KF, D], F32R) for s in ("hi", "lo")] for i in range(2)]
        act_f = sb("act_f", [P, KF, CH], F32)
        hid = sb("hid", [P, KF, CH], F32)
        hT = [[sb(f"hT_{i}{s}", [P, KF, CH], F32R) for s in ("hi", "lo")] for i in range(2)]
        x_res = sb("x_res", [P, CT, D], F32)
        b_g = [ctx.enter_context(nc.psum_tensor(f"ex_b_g{i}", [P, 512], F32)) for i in range(KF)]
        b_u = [ctx.enter_context(nc.psum_tensor(f"ex_b_u{i}", [P, 512], F32)) for i in range(KF)]
        b_y = [ctx.enter_context(nc.psum_tensor(f"ex_b_y{i}", [P, 512], F32)) for i in range(4)]

        STEP = dict(g=KF, u=KF, sil=KF, hm=KF, hhi=KF, hlo=KF, y=CT, acc=CT)
        LOAD = dict(w=16, whi=2, wlo=2)
        LAST = dict(xr=16, fg=CT, fa=1, out=16)
        S = {n: sems.take("ex_" + n) for n in [*STEP, *LOAD, *LAST, "carrier"]}
        begin_counts(nc, [S[n] for n in (*STEP, *LOAD, *LAST)])
        block = ctx.enter_context(nc.Block())

        def run(eng, load, begin, step, last):
            def needs(order, s):
                def need(name, n, apart=False):
                    value = s * STEP[name] + n if name in STEP else order * LOAD[name] + n
                    if isinstance(value, int) and value <= 0:
                        return
                    eng.wait_ge(S[name], START + value)
                    if apart or eng is nc.sync:
                        eng.sem_inc(S["carrier"], 1)
                return need

            def expert(order, w, number, before, following):
                begin(needs(order, order * NG))
                step(needs(order, order * NG), w, number, 0, 0)
                if before is not None:
                    last(needs(order, order * NG), 1 - w, before, NG - 1, 1)
                step(needs(order, order * NG + 1), w, number, 1, 1)
                last(needs(order, order * NG + 1), w, number, 0, 0)
                load(needs(order + 1, order * NG + 2), 1 - w, following)
                with eng.Fori(1, NG // 2) as gg:
                    for par in range(2):
                        g = 2 * gg + par
                        step(needs(order, order * NG + g), w, number, g, par)
                        last(needs(order, order * NG + g), w, number, g - 1, 1 - par)

            load(needs(0, 0), 1, NE)
            expert(0, 1, NE, None, 0)
            expert(1, 0, 0, NE, 1)
            expert(2, 1, 1, 0, 2)
            with eng.Fori(1, NE // 2) as pair:
                expert(1 + 2 * pair, 0, 2 * pair, 2 * pair - 1, 2 * pair + 1)
                expert(2 + 2 * pair, 1, 2 * pair + 1, 2 * pair, 2 * pair + 2)
            last(needs(NX, NX * NG), 1, NE - 1, NG - 1, 1)

        nothing = lambda *a: None

        @block.sync
        def _(sp):
            def load(need, w, which):
                need("whi", 0)
                need("wlo", 0)
                sp.dma_start(raw[:], A["experts"][:, bass.ds(which, 1), :, :].rearrange("p o k n -> p (o k) n")).then_inc(S["w"], 16)
            run(sp, load, nothing, nothing, nothing)
            with sp.Fori(0, NG) as g:
                sp.wait_ge(S["out"], START + g * 16)
                sp.sem_inc(S["carrier"], 1)
                sp.dma_start(x_res[:], x1[:, bass.ds(g * CT, CT), :]).then_inc(S["xr"], 16)
                sp.wait_ge(S["fa"], START + g + 1)
                sp.sem_inc(S["carrier"], 1)
                sp.dma_start(out[:, bass.ds(g * CT, CT), :], x_res[:]).then_inc(S["out"], 16)
            sp.wait_ge(S["out"], START + NG * 16)
            sp.wait_ge(S["w"], START + 16 * (NX + 1))

        @block.scalar
        def _(act):
            def load(need, w, which):
                need("w", 16)
                need("y", -2 * CT)
                nc.scalar.copy(w13[w][0][:], raw[:, 0:2 * KD, :]).then_inc(S["whi"], 1)
                nc.scalar.copy(w2[w][0][:], raw[:, 2 * KD:3 * KD, :]).then_inc(S["whi"], 1)

            def step(need, w, number, g, par):
                for f in range(KF):
                    need("g", f + 1)
                    need("hm", 0)
                    nc.scalar.activation(act_f[:, f, :], b_g[f][:], ACT.Silu).then_inc(S["sil"], 1)
                need("y", -CT)
                for f in range(KF):
                    need("hm", f + 1)
                    nc.scalar.copy(hT[par][0][:, f, :], hid[:, f, :]).then_inc(S["hhi"], 1)
            run(act, load, nothing, step, nothing)

        @block.gpsimd
        def _(pool):
            def step(need, w, number, g, par):
                for f in range(KF):
                    need("hhi", f + 1, apart=True)
                    nc.gpsimd.tensor_tensor(hT[par][1][:, f, :], hid[:, f, :], hT[par][0][:, f, :].bitcast(F32),
                                            ALU.subtract).then_inc(S["hlo"], 1)
            run(pool, nothing, nothing, step, nothing)

        @block.vector
        def _(dve):
            def load(need, w, which):
                need("whi", 1)
                nc.vector.tensor_tensor(w13[w][1][:], raw[:, 0:2 * KD, :], w13[w][0][:].bitcast(F32), ALU.subtract).then_inc(S["wlo"], 1)
                need("whi", 2)
                nc.vector.tensor_tensor(w2[w][1][:], raw[:, 2 * KD:3 * KD, :], w2[w][0][:].bitcast(F32), ALU.subtract).then_inc(S["wlo"], 1)

            def step(need, w, number, g, par):
                for f in range(KF):
                    need("u", f + 1)
                    need("sil", f + 1)
                    need("hlo", 0)
                    nc.vector.tensor_tensor(hid[:, f, :], b_u[f][:], act_f[:, f, :], ALU.mult).then_inc(S["hm"], 1)

            def last(need, w, number, g, par):
                for t in range(CT):
                    need("y", t + 1 - CT)
                    at = x2[:, bass.ds(g * CT + t, 1), :].rearrange("p o d -> p (o d)")
                    c = comb[:, bass.ds(g * CT + t, 1), bass.ds(number, 1)].rearrange("p o n -> p (o n)")
                    nc.vector.scalar_tensor_tensor(out=at, in0=b_y[t][:, 0:D], scalar=c, in1=at, op0=ALU.mult,
                                                   op1=ALU.add).then_inc(S["acc"], 1)
            run(dve, load, nothing, step, last)
            with dve.Fori(0, NB) as b:
                with dve.Fori(0, NG // NB) as c:
                    g = b * (NG // NB) + c
                    dve.wait_ge(S["xr"], START + (g + 1) * 16)
                    dve.wait_ge(S["acc"], START + NX * NG * CT)
                    for t in range(CT):
                        at = x2[:, bass.ds(g * CT + t, 1), :].rearrange("p o d -> p (o d)")
                        nc.vector.tensor_tensor(at, at, bc[:, 0, bass.ds(b, 1), :].rearrange("p o d -> p (o d)"),
                                                ALU.mult).then_inc(S["fg"], 1)
                    dve.wait_ge(S["fg"], START + (g + 1) * CT)
                    nc.vector.tensor_tensor(x_res[:], x_res[:], x2[:, bass.ds(g * CT, CT), :], ALU.add).then_inc(S["fa"], 1)

        @block.tensor
        def _(pe):

            def begin(need):
                need("wlo", 2)

            def step(need, w, number, g, par):
                for f in range(KF):
                    for bank, m, free in ((b_g[f], 0, "sil"), (b_u[f], 1, "hm")):
                        need(free, 0)
                        for n, (a, e) in enumerate(SPLIT3):
                            for k in range(KD):
                                x = nc.tensor.matmul(bank[:], w13[w][a][:, KD * m + k, P * f:P * f + P],
                                                     xfT[e][:, k, bass.ds(g * CH, CH)],
                                                     start=(n == 0 and k == 0), stop=(n == 2 and k == KD - 1))
                        x.then_inc(S["gu"[m]], 1)

            def last(need, w, number, g, par):
                need("hlo", 0)
                for t in range(CT):
                    need("acc", -CT)
                    for n, (a, e) in enumerate(SPLIT3):
                        for k in range(KF):
                            x = nc.tensor.matmul(b_y[t][:, 0:D], hT[par][a][:, k, P * t:P * t + P], w2[w][e][:, k, :],
                                                 start=(n == 0 and k == 0), stop=(n == 2 and k == KF - 1))
                    x.then_inc(S["y"], 1)
            run(pe, nothing, begin, step, last)


def lay_out(I):
    import numpy as np
    a = lambda n: np.asarray(I["L0_" + n])
    kp = lambda w: np.ascontiguousarray(w.reshape(-1, P, w.shape[-1]).transpose(1, 0, 2))
    out = {}
    out["wqkv"] = kp(np.concatenate([a("attn_Wq"), a("attn_Wk"), a("attn_Wv")], axis=1))
    out["wo"] = np.ascontiguousarray(a("attn_Wo").reshape(H1, DH, D).transpose(1, 0, 2))
    out["cT"] = kp(np.ascontiguousarray(a("c").T))
    twice = lambda w, n=2: np.concatenate([w] * n, axis=-1)
    wq2 = np.ascontiguousarray(a("ffn_Wq").T).reshape(D, H2, DH)
    out["wq2"] = kp(np.ascontiguousarray(twice(wq2)).reshape(D, H2 * P)).reshape(P, -1)
    out["wk2"] = kp(twice(np.ascontiguousarray(a("ffn_Wkc").T))).reshape(P, -1)
    out["wv2"] = kp(twice(np.ascontiguousarray(a("ffn_Wvc").T), 4)).reshape(P, -1)
    out["wo2"] = np.ascontiguousarray(a("ffn_Wo").T.reshape(H2, DH, D).transpose(1, 0, 2)).reshape(DH, -1)
    fc = lambda w: kp(np.ascontiguousarray(w.T))
    pack = lambda w1, w3, w2: np.concatenate([fc(w1), fc(w3), fc(w2)], axis=1)
    each = [pack(a("ffn_eW1")[e], a("ffn_eW3")[e], a("ffn_eW2")[e]) for e in range(NE)]
    each.append(pack(a("ffn_sW1"), a("ffn_sW3"), a("ffn_sW2")))
    out["experts"] = np.ascontiguousarray(np.stack(each, axis=1))
    out["wr16"] = kp(twice(np.ascontiguousarray(a("ffn_Wr").T), P // NE)).reshape(P, -1)
    out["bias"] = a("ffn_expert_bias").reshape(1, NE)
    out["g1"] = a("ffn_g1").reshape(1, D)
    out["g2"] = a("ffn_g2").reshape(1, D)
    out["wmod"] = np.ascontiguousarray(kp(a("wmod")).reshape(P, KD, 6, D))
    return out


def program(nc, x, arrays, out):
    A = arrays
    x1 = nc.dram_tensor("x1_scratch", [P, TOK // P, D], F32).ap()
    by_tile = lambda a: a.rearrange("b (t p) d -> p (b t) d", p=P)
    A["x"] = by_tile(x)
    with PhaseSemaphores(nc) as sems:
        windowed_attention(nc, sems, A, x1)
    with nc.sbuf_tensor("x2_resident", [P, TOK // P, D], F32) as x2:
        with PhaseSemaphores(nc) as sems:
            latent_attention(nc, sems, A, x1, x2)
        with PhaseSemaphores(nc) as sems:
            experts(nc, sems, A, x1, x2, by_tile(out))


def kernel(**inputs):
    import numpy as np
    import concourse.bacc as bacc
    from concourse.bass_utils import run_bass_kernel_spmd

    nc = bacc.Bacc("TRN2", target_bir_lowering=False, num_devices=1)
    arrays = {f"in_{k}": v for k, v in lay_out(inputs).items()}
    arrays["in_x"] = np.ascontiguousarray(inputs["L0_attn_x"])
    aps = {k[3:]: nc.dram_tensor(k, a.shape, mybir.dt.from_np(a.dtype), kind="ExternalInput").ap()
           for k, a in arrays.items()}
    out = nc.dram_tensor("out_x", (NB, SEQ, D), F32, kind="ExternalOutput").ap()
    program(nc, aps.pop("x"), aps, out)
    return run_bass_kernel_spmd(nc, [arrays], core_ids=[0]).results[0]["out_x"]
```

```python
from contextlib import ExitStack

import concourse.bass as bass
from concourse import mybir

ALU = mybir.AluOpType
ACT = mybir.ActivationFunctionType
AX = mybir.AxisListType
F32 = mybir.dt.float32
F32R = mybir.dt.float32r
BF16 = mybir.dt.bfloat16

P = 128
D = 256
KD = D // P
NB = 2
SEQ = 2048
TOK = NB * SEQ
CH = 512
CT = CH // P
NC = SEQ // CH
NG = NB * NC
NT = SEQ // P
EPS_LN = 1e-5
EPS_RMS = 1e-6

H1 = 16
DH = 64
WIN = 64
HP = H1 // 2
KW = WIN + P
SW = 2 * P
NEG = -3.0e38

H2 = 4
KT = SEQ // P

NE = 8
FF = 256
KF = FF // P


START = 1


def begin_counts(nc, sems):
    for s in sems:
        nc.tensor.sem_inc(s, START)
    nc.all_engine_barrier()


class PhaseSemaphores:

    def __init__(self, nc):
        self.nc, self.taken = nc, []

    def __enter__(self):
        return self

    def take(self, name):
        self.taken.append(self.nc.alloc_semaphore(name))
        return self.taken[-1]

    def __exit__(self, *failure):
        if failure[0] is None:
            self.nc.all_engine_barrier()
            self.nc.clear_and_free_semaphores(self.taken)
            self.nc.all_engine_barrier()


def modulation_rows(nc, sems, block_name, ctx, A, rows, bc, plus_one):
    sb = lambda n, s, d: ctx.enter_context(nc.sbuf_tensor(block_name + n, s, d))
    c_raw = sb("c_raw", [P, KD, NB], F32)
    c_silu = sb("c_silu", [P, KD, NB], F32)
    c_wide = sb("c_wide", [P, KD, NB, P], F32)
    wmod = sb("wmod", [P, KD, len(rows), D], F32)
    ps = [ctx.enter_context(nc.psum_tensor(f"{block_name}mod_ps{i}", [P, 512], F32)) for i in range(2)]
    s_in, s_silu, s_wide, s_mm, s_out = (
        sems.take(block_name + n) for n in ("mod_in", "mod_silu", "mod_wide", "mod_mm", "mod_out"))

    def load(sp):
        sp.dma_start(c_raw[:], A["cT"]).then_inc(s_in, 16)
        for j, row in enumerate(rows):
            sp.dma_start(wmod[:, :, j, :], A["wmod"][:, :, row, :]).then_inc(s_in, 16)

    def scalar(act):
        act.wait_ge(s_in, 16 * (1 + len(rows)))
        nc.scalar.activation(c_silu[:], c_raw[:], ACT.Silu).then_inc(s_silu, 1)

    def tensor(pe):
        pe.wait_ge(s_wide, 1)
        n = 0
        for j in range(len(rows)):
            for b in range(NB):
                if n >= 2:
                    pe.wait_ge(s_out, n - 1)
                for k in range(KD):
                    mm = nc.tensor.matmul(ps[n % 2][:, 0:D], c_wide[:, k, b, :], wmod[:, k, j, :],
                                          start=(k == 0), stop=(k == KD - 1))
                mm.then_inc(s_mm, 1)
                n += 1

    def vector(dve):
        dve.wait_ge(s_silu, 1)
        nc.vector.tensor_copy(c_wide[:].rearrange("p k b m -> p (k b) m"),
                              c_silu[:].rearrange("p k (b o) -> p (k b) o", o=1).to_broadcast([P, KD * NB, P])
                              ).then_inc(s_wide, 1)
        n = 0
        for j in range(len(rows)):
            for b in range(NB):
                dve.wait_ge(s_mm, n + 1)
                add = 1.0 if plus_one[j] else 0.0
                nc.vector.tensor_scalar(bc[:, j, b, :], ps[n % 2][:, 0:D], add, None, ALU.add).then_inc(s_out, 1)
                n += 1

    return load, scalar, tensor, vector, (s_out, n_of(rows))


def floor_gate(nc, dve, gate, size, s_g):
    nc.vector.tensor_scalar(size, gate, -1.0, 0.25, ALU.mult, ALU.max).then_inc(s_g, 1)
    dve.wait_ge(s_g, 1)
    nc.vector.tensor_tensor(size, size, gate, ALU.max).then_inc(s_g, 1)
    dve.wait_ge(s_g, 2)
    nc.vector.tensor_scalar(gate, gate, 0.0, 2.0, ALU.is_ge, ALU.mult).then_inc(s_g, 1)
    dve.wait_ge(s_g, 3)
    nc.vector.tensor_scalar(gate, gate, -1.0, None, ALU.add).then_inc(s_g, 1)
    dve.wait_ge(s_g, 4)
    nc.vector.tensor_tensor(gate, gate, size, ALU.mult).then_inc(s_g, 1)


def n_of(rows):
    return NB * len(rows)


def newton_rsqrt(nc, dve, root, var, scratch, wait, done):
    nc.vector.tensor_tensor(scratch, root, root, ALU.mult).then_inc(done, 1)
    wait(1)
    nc.vector.scalar_tensor_tensor(out=scratch, in0=var, scalar=-0.5, in1=scratch, op0=ALU.mult, op1=ALU.mult).then_inc(done, 1)
    wait(2)
    nc.vector.scalar_tensor_tensor(out=root, in0=scratch, scalar=1.5, in1=root, op0=ALU.add, op1=ALU.mult).then_inc(done, 1)
    wait(3)


def windowed_attention(nc, sems, A, x1):
    with ExitStack() as ctx:
        sb = lambda n, s, d: ctx.enter_context(nc.sbuf_tensor("wa_" + n, s, d))
        bank = lambda n: ctx.enter_context(nc.psum_tensor("wa_" + n, [P, 512], F32))
        wqkv = [sb(f"wqkv{s}", [P, KD, 3 * H1 * DH], F32R) for s in ("hi", "lo")]
        wo = [sb(f"wo{s}", [P, H1, D], F32R) for s in ("hi", "lo")]
        ident = sb("ident", [P, P], F32)
        mask = sb("mask", [P, NC, KW], BF16)
        mask0 = sb("mask0", [P, KW], BF16)
        bc = sb("bc", [P, 3, NB, D], F32)

        with ExitStack() as c2:
            raw = c2.enter_context(nc.sbuf_tensor("wa_raw", [P, KD * 3 * H1 * DH], F32))
            raw_o = c2.enter_context(nc.sbuf_tensor("wa_raw_o", [P, H1 * D], F32))
            gate_abs = c2.enter_context(nc.sbuf_tensor("wa_gate_abs", [P, NB, D], F32))
            sem = lambda n: sems.take("wa0_" + n)
            s_hi, s_lo, s_id, s_m, s_g = (sem(n) for n in ("hi", "lo", "id", "m", "g"))
            s_w = [sem(f"w{i}") for i in range(6)]
            load, mscalar, mtensor, mvector, (s_bc, n_bc) = modulation_rows(
                nc, sems, "wa0_", c2, A, (0, 1, 2), bc, (False, True, False))
            block = c2.enter_context(nc.Block())
            parts = [(raw[:, i * 1536:(i + 1) * 1536],
                      [w[:].rearrange("p k n -> p (k n)")[:, i * 1536:(i + 1) * 1536] for w in wqkv]) for i in range(4)]
            parts += [(raw_o[:, i * 2048:(i + 1) * 2048],
                       [w[:].rearrange("p h n -> p (h n)")[:, i * 2048:(i + 1) * 2048] for w in wo]) for i in range(2)]

            @block.sync
            def _(sp):
                load(sp)
                for i in range(4):
                    sp.dma_start(raw[:, i * 1536:(i + 1) * 1536],
                                 A["wqkv"].rearrange("p k n -> p (k n)")[:, i * 1536:(i + 1) * 1536]).then_inc(s_w[i], 16)
                wo_h = A["wo"].rearrange("p h n -> p (h n)")
                for i in range(2):
                    for half in range(2):
                        sp.dma_start(raw_o[64 * half:64 * half + 64, i * 2048:(i + 1) * 2048],
                                     wo_h[:, i * 2048:(i + 1) * 2048]).then_inc(s_w[4 + i], 16)

            @block.scalar
            def _(act):
                mscalar(act)
                for i, (src, (hi, lo)) in enumerate(parts):
                    act.wait_ge(s_w[i], 16 if i < 4 else 32)
                    nc.scalar.copy(hi, src).then_inc(s_hi, 1)

            @block.vector
            def _(dve):
                mvector(dve)
                dve.wait_ge(s_bc, n_bc)
                ga = bc[:, 2, :, :]
                floor_gate(nc, dve, ga, gate_abs[:], s_g)
                for i, (src, (hi, lo)) in enumerate(parts):
                    dve.wait_ge(s_hi, i + 1)
                    nc.vector.tensor_tensor(lo, src, hi.bitcast(F32), ALU.subtract).then_inc(s_lo, 1)

            @block.tensor
            def _(pe):
                mtensor(pe)

            @block.gpsimd
            def _(pool):
                nc.gpsimd.memset(ident[:], 0.0).then_inc(s_id, 1)
                nc.gpsimd.memset(mask[:], 0.0).then_inc(s_m, 1)
                pool.wait_ge(s_id, 1)
                nc.gpsimd.affine_select(out=ident[:], in_=ident[:], compare_op=ALU.not_equal, fill=1.0, base=0,
                                        pattern=[[-1, P]], channel_multiplier=1).then_inc(s_id, 1)
                pool.wait_ge(s_m, 1)
                nc.gpsimd.affine_select(out=mask[:], in_=mask[:], compare_op=ALU.is_ge, fill=NEG, base=0,
                                        pattern=[[0, NC], [1, KW]], channel_multiplier=-1).then_inc(s_m, 1)
                pool.wait_ge(s_m, 2)
                nc.gpsimd.affine_select(out=mask[:], in_=mask[:], compare_op=ALU.is_ge, fill=NEG, base=WIN,
                                        pattern=[[0, NC], [-1, KW]], channel_multiplier=1).then_inc(s_m, 1)
                pool.wait_ge(s_m, 3)
                nc.gpsimd.memset(mask[:, 0, 0:WIN], NEG).then_inc(s_m, 1)
                pool.wait_ge(s_m, 4)

        xa = sb("xa", [P, CT, D], F32)
        xr = sb("xr", [P, CT, D], F32)
        stats = sb("stats", [P, CT, 6], F32)
        mv = sb("mv", [P, CT, 2], F32)
        rstd = sb("rstd", [P, CT], F32)
        var = sb("var", [P, CT], F32)
        gated = sb("gated", [P, 2, D], F32)
        newton = sb("newton", [P, CT], F32)
        hT = [sb(f"hT{s}", [P, KD, CH], F32R) for s in ("hi", "lo")]
        v_st = sb("v_st", [P, CT + 1, H1, P], F32R)
        kk = sb("kk", [P, 2, 2, CH - P + SW], F32R)
        k_halo = sb("k_halo", [P, HP, 2, 2, WIN], F32R)
        q_st = sb("q_st", [P, 2, CH], F32R)
        RING = CT
        prob = sb("prob", [P, RING, 2, 2 * P], F32)
        nmax = sb("nmax", [P, RING, 2], F32)
        rsum = sb("rsum", [P, RING, 2], F32)
        rinv = sb("rinv", [P, RING, 2], F32)
        PTW = (CT + 1) * SW
        pT = [sb(f"pT{s}", [P, 2, PTW], F32R) for s in ("hi", "lo")]
        oT = [sb(f"oT{s}", [P, 2, CH], F32R) for s in ("hi", "lo")]

        b_q, b_k = bank("b_q"), bank("b_k")
        b_s = [bank("b_s0"), bank("b_s1")]
        b_t, b_o = bank("b_t"), bank("b_o")
        b_wo = [bank("b_wo0"), bank("b_wo1")]

        names = ("nwt x xr bn ag var sd rs xn hm h hT hhi hlo vp vhi vlo vhalo s ttr exp rc pn t thi tlo pv ohi olo wo "
                 "pq pk qhi qlo khi klo kdup krest ksave mask res1 res2 out init carrier").split()
        S = {n: sems.take("wa_" + n) for n in names}
        PER = dict(x=16, xr=16, bn=CT, ag=CT, nwt=3, var=1, sd=1, rs=1, xn=CT, hm=CT, h=CT, hT=KD, hhi=KD, hlo=KD,
                   vp=2 * CT, vhi=2 * CT, vlo=2 * CT, vhalo=32, s=HP * CT, ttr=HP * CT, exp=HP * CT, rc=HP * CT,
                   pn=HP * CT, t=HP * CT, thi=HP * CT, tlo=HP * CT, pv=2 * HP, ohi=2 * HP, olo=2 * HP, wo=2 * HP,
                   pq=HP, pk=HP, qhi=HP, qlo=HP, khi=HP, klo=HP, kdup=32 * HP, krest=16 * HP, ksave=16 * HP,
                   mask=1, res1=CT, res2=CT, out=16)

        begin_counts(nc, [S[n] for n in PER])
        INIT = 8
        block = ctx.enter_context(nc.Block())

        def counts(eng, m, following):
            def need(name, n, apart=False):
                eng.wait_ge(S[name], START + m * PER[name] + (n if following else max(n, 0)))
                if apart or eng is nc.sync:
                    eng.sem_inc(S["carrier"], 1)
            return need

        def chunks(eng, first, body):
            first(counts(eng, 0, False), 0)
            with eng.Fori(0, NG) as g:
                body(counts(eng, g, False), counts(eng, g + 1, True), g, (g + 1) & (NG - 1))

        value_bank = [(b_q, b_k)[n % 2] for n in range(2 * CT - 1)] + [b_o]

        def of_batch(g, row):
            b = (g >> (NC.bit_length() - 1)) & (NB - 1)
            return bc[:, row, bass.ds(b, 1), :].rearrange("p o d -> p (o d)")

        def pt_places(t):
            halo = 0 if t == 0 else SW * t + P
            own = SW * CT + P if t == CT - 1 else SW * (t + 1)
            if own == halo + WIN:
                return [(0, KW, halo)]
            return [(0, WIN, halo), (WIN, KW, own)]

        BLOCK_AT = [0] + [P * j for j in range(CT - 1)] + [CH - SW]

        @block.sync
        def _(sp):
            def load_x(nxt, m):
                nxt("hT", 0)
                sp.dma_start(xa[:], A["x"][:, bass.ds(m * CT, CT), :]).then_inc(S["x"], 16)

            def value_halo(nxt, half):
                nxt("pv", 8 * half - 8)
                nxt("vhalo", 16 * half)
                sp.dma_start(v_st[WIN:P, 0, 8 * half:8 * half + 8, :].bitcast(F32),
                             v_st[WIN:P, CT, 8 * half:8 * half + 8, :].bitcast(F32)).then_inc(S["vhalo"], 16)

            def keys(need, i):
                need("s", CT * i)
                need("ksave", 16 * i)
                sp.dma_start(kk[:, :, :, 0:WIN].bitcast(F32), k_halo[:, i, :, :, :].bitcast(F32)).then_inc(S["krest"], 16)
                need("klo", i + 1)
                sp.dma_start(kk[64:P, :, 0, WIN:WIN + CH].bitcast(F32), kk[0:64, :, 0, WIN:WIN + CH].bitcast(F32)).then_inc(S["kdup"], 16)
                sp.dma_start(kk[0:64, :, 1, WIN:WIN + CH].bitcast(F32), kk[64:P, :, 1, WIN:WIN + CH].bitcast(F32)).then_inc(S["kdup"], 16)
                need("kdup", 32 * (i + 1))
                need("krest", 16 * (i + 1))
                sp.dma_start(k_halo[:, i, :, :, :].bitcast(F32), kk[:, :, :, CH:CH + WIN].bitcast(F32)).then_inc(S["ksave"], 16)

            def first(nxt, m):
                load_x(nxt, m)
                sp.wait_ge(S["init"], INIT)
                value_halo(nxt, 0)
                value_halo(nxt, 1)
                keys(nxt, 0)

            def body(need, nxt, g, m):
                load_x(nxt, m)
                need("out", 0)
                sp.dma_start(xr[:], A["x"][:, bass.ds(g * CT, CT), :]).then_inc(S["xr"], 16)
                for i in range(1, HP):
                    keys(need, i)
                    if i == 6:
                        value_halo(nxt, 0)
                value_halo(nxt, 1)
                keys(nxt, 0)
                need("res2", CT)
                sp.dma_start(x1[:, bass.ds(g * CT, CT), :], xr[:]).then_inc(S["out"], 16)
            chunks(sp, first, body)
            sp.wait_ge(S["out"], START + 16 * NB * NC)
            sp.wait_ge(S["ksave"], START + 16 * (HP * NB * NC + 1))

        @block.gpsimd
        def _(pool):
            nc.gpsimd.memset(v_st[:, CT, :, :].bitcast(F32), 0.0).then_inc(S["init"], 1)
            nc.gpsimd.memset(v_st[0:WIN, 0, :, :].bitcast(F32), 0.0).then_inc(S["init"], 1)
            nc.gpsimd.memset(k_halo[:].bitcast(F32), 0.0).then_inc(S["init"], 1)
            nc.gpsimd.memset(kk[:, :, :, WIN + CH:].bitcast(F32), 0.0).then_inc(S["init"], 1)
            nc.gpsimd.memset(prob[:, :, :, 0:WIN], 0.0).then_inc(S["init"], 1)
            nc.gpsimd.memset(mask0[:], 0.0).then_inc(S["init"], 1)

            def modulate(nxt, m, t):
                nxt("xn", t + 1, apart=True)
                nc.gpsimd.tensor_tensor(xa[:, t, :], xa[:, t, :], of_batch(m, 1), ALU.mult).then_inc(S["hm"], 1)
                nxt("hm", t + 1, apart=True)
                nc.gpsimd.tensor_tensor(xa[:, t, :], xa[:, t, :], of_batch(m, 0), ALU.add).then_inc(S["h"], 1)

            def first(nxt, m):
                for t in range(CT):
                    modulate(nxt, m, t)

            def body(need, nxt, g, m):
                for i in range(HP):
                    for t in range(CT):
                        r = (CT * i + t) % RING
                        need("rc", CT * i + t + 1, apart=True)
                        for hd in range(2):
                            p = prob[:, r, hd, WIN:]
                            x = nc.gpsimd.tensor_scalar(p, p, rinv[:, r, hd:hd + 1], 1.0, ALU.mult, ALU.mult)
                        x.then_inc(S["pn"], 1)
                    if i in (4, 5):
                        modulate(nxt, m, 2 * (i - 4))
                        modulate(nxt, m, 2 * (i - 4) + 1)
            pool.wait_ge(S["init"], INIT)
            chunks(pool, first, body)

        @block.scalar
        def _(act):
            def exp(need, i, t):
                n = CT * i + t
                need("ttr", n + 1)
                for hd in range(2):
                    p = prob[:, n % RING, hd, WIN:]
                    x = nc.scalar.activation(p, p, ACT.Exp, bias=nmax[:, n % RING, hd:hd + 1], scale=-1.0,
                                             accum_out=rsum[:, n % RING, hd:hd + 1])
                x.then_inc(S["exp"], 1)

            def t_hi(need, i, t):
                need("t", CT * i + t + 1)
                need("pv", 2 * i)
                for a, e, at in pt_places(t):
                    x = nc.scalar.copy(pT[0][:, :, at:at + e - a],
                                       b_t[:, 0:2 * KW].rearrange("p (h n) -> p h n", h=2)[:, :, a:e])
                x.then_inc(S["thi"], 1)

            def q_hi(need, i):
                need("pq", i + 1)
                need("s", CT * i)
                nc.scalar.copy(q_st[0:64, 0, :], b_q[0:64, :])
                nc.scalar.copy(q_st[0:64, 1, :], b_q[64:P, :]).then_inc(S["qhi"], 1)

            def k_hi(need, i):
                need("pk", i + 1)
                need("s", CT * i)
                need("ksave", 16 * i)
                nc.scalar.copy(kk[0:64, 0, 0, WIN:WIN + CH], b_k[0:64, :])
                nc.scalar.copy(kk[64:P, 0, 1, WIN:WIN + CH], b_k[64:P, :]).then_inc(S["khi"], 1)

            def o_hi(need, i, hd):
                need("pv", 2 * i + hd + 1)
                need("wo", 2 * (i - 1) + hd + 1)
                nc.scalar.copy(oT[0][:, hd, :], b_o[:]).then_inc(S["ohi"], 1)

            def root(nxt):
                nxt("var", 1)
                nc.scalar.activation(rstd[:], var[:], ACT.Sqrt).then_inc(S["sd"], 1)

            def h_hi(nxt, k):
                nxt("hT", k + 1)
                nc.scalar.copy(hT[0][:, k, :], (b_k, b_q)[k][:]).then_inc(S["hhi"], 1)

            def v_hi(nxt, n):
                half, t = n // CT, n % CT
                nxt("vp", n + 1)
                nxt("vhalo", 16 * (half + 1))
                nc.scalar.copy(v_st[:, t + 1, 8 * half:8 * half + 8, 0:DH],
                               value_bank[n][:].rearrange("p (h n) -> p h n", h=8)).then_inc(S["vhi"], 1)

            def first(nxt, m):
                root(nxt)
                act.wait_ge(S["init"], INIT)
                for k in range(KD):
                    h_hi(nxt, k)
                for n in range(2 * CT):
                    v_hi(nxt, n)
                    if n == 2 * CT - 2:
                        k_hi(nxt, 0)
                q_hi(nxt, 0)

            def body(need, nxt, g, m):
                for i in range(HP + 1):
                    if i > 0:
                        t_hi(need, i - 1, 0)
                    if i > 1:
                        o_hi(need, i - 2, 1)
                    if i > 0:
                        t_hi(need, i - 1, 1)
                    if i == HP:
                        v_hi(nxt, 0)
                    if i < HP:
                        exp(need, i, 0)
                    if i > 0:
                        t_hi(need, i - 1, 2)
                    if i < HP:
                        exp(need, i, 1)
                    if i == HP:
                        v_hi(nxt, 1)
                    if i > 0:
                        t_hi(need, i - 1, 3)
                    if i < HP:
                        exp(need, i, 2)
                    if i == HP:
                        v_hi(nxt, 2)
                    if i + 1 < HP:
                        k_hi(need, i + 1)
                    if i + 1 == HP:
                        h_hi(nxt, 0)
                    if i > 0:
                        o_hi(need, i - 1, 0)
                    if i < HP:
                        exp(need, i, 3)
                    if i + 1 < HP:
                        q_hi(need, i + 1)
                    if i + 1 == HP:
                        h_hi(nxt, 1)
                    if i == 2:
                        root(nxt)
                    if i == HP:
                        v_hi(nxt, 3)
                        o_hi(need, i - 1, 1)
                for n in range(CT, 2 * CT):
                    v_hi(nxt, n)
                    if n == 2 * CT - 2:
                        k_hi(nxt, 0)
                q_hi(nxt, 0)
            chunks(act, first, body)

        @block.vector
        def _(dve):
            def lo(out, psum, hi, sem=None):
                x = nc.vector.tensor_tensor(out, psum, hi.bitcast(F32), ALU.subtract)
                if sem:
                    x.then_inc(S[sem], 1)

            def ttr(need, i, t):
                n = CT * i + t
                need("s", n + 1)
                need("t", n - RING + 1, apart=True)
                m = mask0[:] if t == 0 else mask[:, 1, :]
                for hd in range(2):
                    x = nc.vector.tensor_tensor_reduce(prob[:, n % RING, hd, WIN:], b_s[t % 2][:, SW * hd:SW * hd + KW], m,
                                                       -float(DH) ** -0.5, 3.4e38, ALU.add, ALU.min,
                                                       nmax[:, n % RING, hd:hd + 1])
                x.then_inc(S["ttr"], 1)

            def recip(need, i, t):
                n = CT * i + t
                need("exp", n + 1)
                nc.vector.reciprocal(rinv[:, n % RING, :], rsum[:, n % RING, :]).then_inc(S["rc"], 1)

            def t_lo(need, i, t):
                need("thi", CT * i + t + 1)
                pl = pt_places(t)
                for a, e, at in pl:
                    lo(pT[1][:, :, at:at + e - a], b_t[:, 0:2 * KW].rearrange("p (h n) -> p h n", h=2)[:, :, a:e],
                       pT[0][:, :, at:at + e - a], "tlo" if (a, e, at) == pl[-1] else None)

            def q_lo(need, i):
                need("qhi", i + 1)
                lo(q_st[64:P, 0, :], b_q[0:64, :], q_st[0:64, 0, :])
                lo(q_st[64:P, 1, :], b_q[64:P, :], q_st[0:64, 1, :], "qlo")

            def k_lo(need, i):
                need("khi", i + 1)
                lo(kk[0:64, 1, 0, WIN:WIN + CH], b_k[0:64, :], kk[0:64, 0, 0, WIN:WIN + CH])
                lo(kk[64:P, 1, 1, WIN:WIN + CH], b_k[64:P, :], kk[64:P, 0, 1, WIN:WIN + CH], "klo")

            def o_lo(need, i, hd):
                need("ohi", 2 * i + hd + 1)
                lo(oT[1][:, hd, :], b_o[:], oT[0][:, hd, :], "olo")

            def moments(nxt):
                nxt("x", 16)
                for t in range(CT):
                    nc.vector.bn_stats(stats[:, t, :], xa[:, t, :]).then_inc(S["bn"], 1)

            def variances(nxt):
                for t in range(CT):
                    nxt("bn", t + 1, apart=True)
                    nc.vector.bn_aggr(mv[:, t, :], stats[:, t, :]).then_inc(S["ag"], 1)
                nxt("ag", CT)
                nc.vector.tensor_scalar(var[:], mv[:, :, 1], EPS_LN, None, ALU.add).then_inc(S["var"], 1)

            def inverse_roots(nxt):
                nxt("sd", 1)
                nc.vector.reciprocal(rstd[:], rstd[:]).then_inc(S["rs"], 1)
                nxt("rs", 1)
                newton_rsqrt(nc, dve, rstd[:], var[:], newton[:], lambda k: nxt("nwt", k), S["nwt"])

            def normalise(nxt):
                for t in range(CT):
                    nc.vector.tensor_scalar(xa[:, t, :], xa[:, t, :], mv[:, t, 0:1], rstd[:, t:t + 1],
                                            ALU.subtract, ALU.mult).then_inc(S["xn"], 1)

            def h_lo(nxt, k):
                nxt("hhi", k + 1)
                lo(hT[1][:, k, :], (b_k, b_q)[k][:], hT[0][:, k, :], "hlo")

            def v_lo(nxt, n):
                half, t = n // CT, n % CT
                nxt("vhi", n + 1)
                lo(v_st[:, t + 1, 8 * half:8 * half + 8, DH:P], value_bank[n][:].rearrange("p (h n) -> p h n", h=8),
                   v_st[:, t + 1, 8 * half:8 * half + 8, 0:DH], "vlo")

            def first(nxt, m):
                moments(nxt)
                variances(nxt)
                inverse_roots(nxt)
                normalise(nxt)
                for w in range(2):
                    nc.vector.memset(pT[w][:].bitcast(F32), 0.0).then_inc(S["init"], 1)
                dve.wait_ge(S["init"], INIT)
                for k in range(KD):
                    h_lo(nxt, k)
                for n in range(2 * CT):
                    v_lo(nxt, n)
                    if n == 2 * CT - 2:
                        k_lo(nxt, 0)
                q_lo(nxt, 0)

            def body(need, nxt, g, m):
                need("ttr", 0)
                nc.vector.tensor_copy(mask0[:], mask[:, bass.ds(g & (NC - 1), 1), :].rearrange("p o d -> p (o d)")).then_inc(S["mask"], 1)
                need("mask", 1)
                for i in range(HP + 1):
                    if i > 0:
                        t_lo(need, i - 1, 0)
                    if i > 1:
                        o_lo(need, i - 2, 1)
                    if i < HP:
                        ttr(need, i, 0)
                    if i > 0:
                        t_lo(need, i - 1, 1)
                    if i == HP:
                        v_lo(nxt, 0)
                    if i < HP:
                        ttr(need, i, 1)
                    if i > 0:
                        t_lo(need, i - 1, 2)
                    if i == HP:
                        v_lo(nxt, 1)
                    if i < HP:
                        recip(need, i, 0)
                        ttr(need, i, 2)
                        recip(need, i, 1)
                    if i > 0:
                        t_lo(need, i - 1, 3)
                    if i < HP:
                        ttr(need, i, 3)
                    if i == HP:
                        v_lo(nxt, 2)
                    if i + 1 < HP:
                        k_lo(need, i + 1)
                    if i + 1 == HP:
                        h_lo(nxt, 0)
                    if i > 0:
                        o_lo(need, i - 1, 0)
                    if i < HP:
                        recip(need, i, 2)
                    if i + 1 < HP:
                        q_lo(need, i + 1)
                    if i + 1 == HP:
                        h_lo(nxt, 1)
                    if i < HP:
                        recip(need, i, 3)
                    if i == HP:
                        v_lo(nxt, 3)
                    if i == 1:
                        moments(nxt)
                    if i == 2:
                        variances(nxt)
                    if i == 3:
                        inverse_roots(nxt)
                        normalise(nxt)
                    if i == HP:
                        o_lo(need, i - 1, 1)
                for n in range(CT, 2 * CT):
                    v_lo(nxt, n)
                    if n == 2 * CT - 2:
                        k_lo(nxt, 0)
                q_lo(nxt, 0)
                need("wo", 2 * HP)
                need("xr", 16)
                for t in range(CT):
                    need("res2", t - 1)
                    nc.vector.tensor_tensor(gated[:, t % 2, :], b_wo[t // 2][:, D * (t % 2):D * (t % 2) + D],
                                            of_batch(g, 2), ALU.mult).then_inc(S["res1"], 1)
                    need("res1", t + 1)
                    nc.vector.tensor_tensor(xr[:, t, :], xr[:, t, :], gated[:, t % 2, :], ALU.add).then_inc(S["res2"], 1)
            chunks(dve, first, body)

        @block.tensor
        def _(pe):
            SPLIT3 = ((0, 0), (0, 1), (1, 0))

            def project(out, col0):
                for n, (a, e) in enumerate(SPLIT3):
                    for k in range(KD):
                        x = nc.tensor.matmul(out, wqkv[a][:, k, col0:col0 + P], hT[e][:, k, :],
                                             start=(n == 0 and k == 0), stop=(n == 2 and k == KD - 1))
                return x

            def pq(need, i):
                need("qlo", i)
                project(b_q[:], P * i).then_inc(S["pq"], 1)

            def pk(need, i):
                need("klo", i)
                project(b_k[:], H1 * DH + P * i).then_inc(S["pk"], 1)

            def scores(need, i, t):
                n = CT * i + t
                if t == 0:
                    need("qlo", i + 1)
                    need("kdup", 32 * (i + 1))
                    need("krest", 16 * (i + 1))
                    need("klo", i + 1)
                need("ttr", n - 1)
                for hd in range(2):
                    for w in range(2):
                        x = nc.tensor.matmul(b_s[t % 2][:, SW * hd:SW * hd + SW], q_st[:, hd, P * t:P * t + P],
                                             kk[:, w, hd, P * t:P * t + SW], start=(w == 0), stop=(w == 1))
                x.then_inc(S["s"], 1)

            def transposes(need, i, t):
                n = CT * i + t
                need("pn", n + 1)
                need("tlo", n, apart=True)
                for hd in range(2):
                    p = prob[:, n % RING, hd, :]
                    nc.tensor.transpose(b_t[:, KW * hd:KW * hd + WIN], p[0:WIN, 0:P], ident[0:WIN, 0:WIN])
                    x = nc.tensor.transpose(b_t[:, KW * hd + WIN:KW * hd + KW], p[:, P:], ident[:])
                x.then_inc(S["t"], 1)

            def pv(need, i, hd):
                need("tlo", CT * (i + 1))
                need("olo", 2 * i + hd)
                if i == 0 and hd == 0:
                    need("vlo", 2 * CT)
                for j in range(CT + 1):
                    for w in range(2):
                        x = nc.tensor.matmul(b_o[:, BLOCK_AT[j]:BLOCK_AT[j] + SW], v_st[:, j, 2 * i + hd, :],
                                             pT[w][:, hd, SW * j:SW * j + SW], start=(j == 0 and w == 0),
                                             stop=(j == CT and w == 1), skip_group_check=True)
                x.then_inc(S["pv"], 1)

            def out_proj(need, i, hd, ts):
                need("olo", 2 * i + hd + 1)
                if i == 0 and hd == 0:
                    need("res2", 0)
                for t in ts:
                    for n, (a, e) in enumerate(SPLIT3):
                        first = i == 0 and hd == 0 and n == 0
                        x = nc.tensor.matmul(b_wo[t // 2][:, D * (t % 2):D * (t % 2) + D], oT[a][:, hd, P * t:P * t + P],
                                             wo[e][:, 2 * i + hd, :], start=(first and t % 2 == 0),
                                             stop=(i == HP - 1 and hd == 1 and n == 2), skip_group_check=True)
                if ts[-1] == CT - 1:
                    x.then_inc(S["wo"], 1)

            def h_transposes(nxt, k):
                nxt("h", CT)
                nxt("klo", 0)
                nxt("qlo", 0)
                for t in range(CT):
                    x = nc.tensor.transpose((b_k, b_q)[k][:, P * t:P * t + P], xa[:, t, P * k:P * k + P], ident[:])
                x.then_inc(S["hT"], 1)

            def values(nxt, n):
                half, t = n // CT, n % CT
                nxt("hlo", KD)
                if n == 2 * CT - 1:
                    nxt("olo", 0)
                else:
                    nxt("vlo", n - 1)
                for x_part, (a, e) in enumerate(SPLIT3):
                    for k in range(KD):
                        x = nc.tensor.matmul(value_bank[n][:], hT[a][:, k, P * t:P * t + P],
                                             wqkv[e][:, k, 2 * H1 * DH + 512 * half:2 * H1 * DH + 512 * half + 512],
                                             start=(x_part == 0 and k == 0), stop=(x_part == 2 and k == KD - 1))
                x.then_inc(S["vp"], 1)

            def first(nxt, m):
                for k in range(KD):
                    h_transposes(nxt, k)
                for n in range(2 * CT - 1):
                    values(nxt, n)
                nxt("vlo", 2 * CT - 2)
                pk(nxt, 0)
                values(nxt, 2 * CT - 1)
                nxt("vlo", 2 * CT - 1)
                pq(nxt, 0)

            def body(need, nxt, g, m):
                scores(need, 0, 0)
                scores(need, 0, 1)
                pk(need, 1)
                scores(need, 0, 2)
                pq(need, 1)
                scores(need, 0, 3)
                for i in range(1, HP + 1):
                    transposes(need, i - 1, 0)
                    if i > 1:
                        out_proj(need, i - 2, 0, [0, 1, 2, 3])
                    if i < HP:
                        scores(need, i, 0)
                    transposes(need, i - 1, 1)
                    if i < HP:
                        scores(need, i, 1)
                    if i > 1:
                        out_proj(need, i - 2, 1, [0, 1])
                    if i == HP:
                        values(nxt, 0)
                    transposes(need, i - 1, 2)
                    if i < HP:
                        scores(need, i, 2)
                    if i + 1 < HP:
                        pk(need, i + 1)
                    if i + 1 == HP:
                        h_transposes(nxt, 0)
                    if i == HP:
                        values(nxt, 1)
                    transposes(need, i - 1, 3)
                    if i < HP:
                        scores(need, i, 3)
                    if i == HP:
                        values(nxt, 2)
                    pv(need, i - 1, 0)
                    if i + 1 < HP:
                        pq(need, i + 1)
                    if i + 1 == HP:
                        h_transposes(nxt, 1)
                    if i > 1:
                        out_proj(need, i - 2, 1, [2, 3])
                    if i == HP:
                        values(nxt, 3)
                    pv(need, i - 1, 1)
                values(nxt, CT)
                values(nxt, CT + 1)
                out_proj(need, HP - 1, 0, [0, 1, 2, 3])
                values(nxt, CT + 2)
                nxt("vlo", 2 * CT - 2)
                pk(nxt, 0)
                values(nxt, CT + 3)
                nxt("vlo", 2 * CT - 1)
                pq(nxt, 0)
                out_proj(need, HP - 1, 1, [0, 1, 2, 3])
            pe.wait_ge(S["init"], INIT)
            chunks(pe, first, body)



SPLIT3 = ((0, 0), (0, 1), (1, 0))


def split_weights(nc, sems, name, sources):
    s_w, s_hi, s_lo = (sems.take(f"{name}_{n}") for n in ("raw", "hi", "lo"))
    loads = sum(len(src[0]) for src in sources)

    def load(sp):
        for drams, raw, hi, lo in sources:
            for dram, at in drams:
                sp.dma_start(at, dram).then_inc(s_w, 16)

    def scalar(act):
        act.wait_ge(s_w, 16 * loads)
        for drams, raw, hi, lo in sources:
            nc.scalar.copy(hi, raw).then_inc(s_hi, 1)

    def vector(dve):
        for i, (drams, raw, hi, lo) in enumerate(sources):
            dve.wait_ge(s_hi, i + 1)
            nc.vector.tensor_tensor(lo, raw, hi.bitcast(F32), ALU.subtract).then_inc(s_lo, 1)

    return load, scalar, vector


def make_ident(nc, pool, ident, s_id):
    nc.gpsimd.memset(ident[:], 0.0).then_inc(s_id, 1)
    pool.wait_ge(s_id, 1)
    nc.gpsimd.affine_select(out=ident[:], in_=ident[:], compare_op=ALU.not_equal, fill=1.0, base=0,
                            pattern=[[-1, P]], channel_multiplier=1).then_inc(s_id, 1)


def latent_attention(nc, sems, A, x1, x2):
    with ExitStack() as ctx:
        sb = lambda n, s, d: ctx.enter_context(nc.sbuf_tensor("la_" + n, s, d))
        wq = [sb(f"wq{s}", [P, KD, H2, P], F32R) for s in ("hi", "lo")]
        wk = [sb(f"wk{s}", [P, KD, P], F32R) for s in ("hi", "lo")]
        wv = [sb(f"wv{s}", [P, KD, D], F32R) for s in ("hi", "lo")]
        wo = [sb(f"wo{s}", [P, H2, D], F32R) for s in ("hi", "lo")]
        ident = sb("ident", [P, P], F32)
        bc = sb("bc", [P, 2, NB, D], F32)
        g1 = sb("g1", [P, D], F32)
        TT = TOK // P
        rrms = sb("rrms", [P, TT], F32)

        with ExitStack() as c2:
            raw = lambda n, s: c2.enter_context(nc.sbuf_tensor("la_raw_" + n, s, F32))
            rq, rk, rv, ro = raw("q", [P, KD * H2 * P]), raw("k", [P, KD * P]), raw("v", [P, KD * D]), raw("o", [P, H2 * D])
            s_id = sems.take("la0_id")
            s_g1 = sems.take("la0_g1")
            s_x, s_bn, s_ag, s_var, s_root, s_rs, s_nwt, s_scaled, s_h, s_sq = (
                sems.take("la0_" + n) for n in "x bn ag var root rs nwt scaled h sq".split())
            s_carrier = sems.take("la0_carrier")
            sb2 = lambda n, s: c2.enter_context(nc.sbuf_tensor("la0_" + n, s, F32))
            stats, mv, square = sb2("stats", [P, TT, 6]), sb2("mv", [P, TT, 2]), sb2("square", [P, D])
            rstd, var, newton, ms = (sb2(n, [P, TT]) for n in ("rstd", "var", "newton", "ms"))
            flat = lambda w: [x[:].rearrange("p a b -> p (a b)") for x in w]
            flat4 = lambda w: [x[:].rearrange("p a b c -> p (a b c)") for x in w]
            load, mscalar, mtensor, mvector, (s_bc, n_bc) = modulation_rows(
                nc, sems, "la0_", c2, A, (3, 4), bc, (False, True))
            wload, wscalar, wvector = split_weights(nc, sems, "la0_w", [
                ([(A["wq2"], rq[:])], rq[:], *flat4(wq)),
                ([(A["wk2"], rk[:])], rk[:], *flat(wk)),
                ([(A["wv2"], rv[:])], rv[:], *flat(wv)),
                ([(A["wo2"], ro[0:64, :]), (A["wo2"], ro[64:P, :])], ro[:], *flat(wo))])
            block = c2.enter_context(nc.Block())

            tile_at = lambda k: x2[:, bass.ds(k, 1), :].rearrange("p o d -> p (o d)")

            def tiles(eng, body):
                for b in range(NB):
                    with eng.Fori(0, NT // 4) as n:
                        body(b, b * NT + 4 * n)

            @block.sync
            def _(sp):
                for g in range(NG):
                    sp.dma_start(x2[:, g * CT:(g + 1) * CT, :], x1[:, g * CT:(g + 1) * CT, :]).then_inc(s_x, 16)
                load(sp)
                wload(sp)
                sp.dma_start(g1[:], A["g1"].to_broadcast([P, D])).then_inc(s_g1, 16)
                sp.wait_ge(s_g1, 16)

            @block.scalar
            def _(act):
                mscalar(act)
                wscalar(act)
                act.wait_ge(s_var, 1)
                nc.scalar.activation(rstd[:], var[:], ACT.Sqrt).then_inc(s_root, 1)

                def squares(b, first):
                    for k in range(4):
                        act.wait_ge(s_h, first + k + 1)
                        nc.scalar.activation(square[:], tile_at(first + k), ACT.Square,
                                             accum_out=ms[:, bass.ds(first + k, 1)]).then_inc(s_sq, 1)
                        act.wait_ge(s_sq, first + k + 1)
                tiles(act, squares)
                act.wait_ge(s_var, 2)
                nc.scalar.activation(rrms[:], ms[:], ACT.Sqrt).then_inc(s_root, 1)

            @block.vector
            def _(dve):
                mvector(dve)
                dve.wait_ge(s_x, 16 * NG)
                for k in range(TT):
                    nc.vector.bn_stats(stats[:, k, :], x2[:, k, :]).then_inc(s_bn, 1)
                dve.wait_ge(s_bn, TT)
                for k in range(TT):
                    nc.vector.bn_aggr(mv[:, k, :], stats[:, k, :]).then_inc(s_ag, 1)
                dve.wait_ge(s_ag, TT)
                nc.vector.tensor_scalar(var[:], mv[:, :, 1], EPS_LN, None, ALU.add).then_inc(s_var, 1)
                dve.wait_ge(s_root, 1)
                nc.vector.reciprocal(rstd[:], rstd[:]).then_inc(s_rs, 1)
                dve.wait_ge(s_rs, 1)
                newton_rsqrt(nc, dve, rstd[:], var[:], newton[:], lambda k: dve.wait_ge(s_nwt, k), s_nwt)

                def scale(b, first):
                    for k in range(4):
                        at = tile_at(first + k)
                        nc.vector.scalar_tensor_tensor(out=at, in0=at, scalar=mv[:, bass.ds(first + k, 1), 0], in1=bc[:, 1, b, :],
                                                       op0=ALU.subtract, op1=ALU.mult).then_inc(s_scaled, 1)
                    for k in range(4):
                        at = tile_at(first + k)
                        dve.wait_ge(s_scaled, first + k + 1)
                        dve.sem_inc(s_carrier, 1)
                        nc.vector.scalar_tensor_tensor(out=at, in0=at, scalar=rstd[:, bass.ds(first + k, 1)], in1=bc[:, 0, b, :],
                                                       op0=ALU.mult, op1=ALU.add).then_inc(s_h, 1)
                tiles(dve, scale)
                wvector(dve)
                dve.wait_ge(s_sq, TT)
                nc.vector.tensor_scalar(ms[:], ms[:], 1.0 / D, EPS_RMS, ALU.mult, ALU.add).then_inc(s_var, 1)
                dve.wait_ge(s_root, 2)
                nc.vector.reciprocal(rrms[:], rrms[:]).then_inc(s_rs, 1)
                dve.wait_ge(s_rs, 2)
                newton_rsqrt(nc, dve, rrms[:], ms[:], newton[:], lambda k: dve.wait_ge(s_nwt, 3 + k), s_nwt)

            @block.tensor
            def _(pe):
                mtensor(pe)

            @block.gpsimd
            def _(pool):
                make_ident(nc, pool, ident, s_id)
                pool.wait_ge(s_id, 2)

        xa = sb("xa", [P, CT, D], F32)
        nxT = [sb(f"nxT{s}", [P, KD, CH], F32R) for s in ("hi", "lo")]
        q_st = sb("q_st", [P, H2, SEQ], F32R)
        kk = [sb(f"k{s}", [P, SEQ], F32R) for s in ("hi", "lo")]
        v_st = sb("v_st", [P, KT, P], F32R)
        q_now = sb("q_now", [P, H2, P], F32R)
        prob = sb("prob", [P, H2, SEQ], F32)
        HALF = SEQ // 2
        mx = sb("mx", [P, H2, 2], F32)
        nmax = sb("nmax", [P, H2], F32)
        rsum = sb("rsum", [P, H2, 2], F32)
        rtot = sb("rtot", [P, H2], F32)
        rinv = sb("rinv", [P, H2], F32)
        pT = [sb(f"pT{s}", [P, KT, 2, P], F32R) for s in ("hi", "lo")]
        oT = [sb(f"oT{s}", [P, H2, P], F32R) for s in ("hi", "lo")]

        b_s = ctx.enter_context(nc.psum_tensor("la_b_s", [P, 4, 512], F32))
        b_t = [ctx.enter_context(nc.psum_tensor(f"la_b_t{i}", [P, 512], F32)) for i in range(2)]
        b_o = ctx.enter_context(nc.psum_tensor("la_b_o", [P, 512], F32))
        b_y = ctx.enter_context(nc.psum_tensor("la_b_y", [P, 512], F32))

        PREP = dict(nx=CT, nT=KD, nhi=KD, nlo=KD, qp=H2, qhi=H2, qlo=H2, kp=1, khi=1, klo=1, vp=2, vhi=2, vlo=2)
        TILE = dict(qn=H2, s=2 * H2, mxp=2 * H2, mxt=H2, nm=H2, exp=2 * H2, rt=H2, rc=H2, pn=H2, t=4 * H2, thi=4 * H2,
                    tlo=4 * H2, pv=8, ohi=2, olo=2, y=1, res=1)
        S = {n: sems.take("la_" + n) for n in [*PREP, *TILE, "carrier"]}
        begin_counts(nc, [S[n] for n in (*PREP, *TILE)])
        block = ctx.enter_context(nc.Block())

        nothing = lambda *a: None

        def phases(eng, prep, tile, drain):
            with eng.Fori(0, NB) as b:
                def tiles_need(name, n, apart=False):
                    if name in PREP:
                        eng.wait_ge(S[name], START + b * (NC * PREP[name]) + (NC * PREP[name] if n is None else max(n, 0)))
                    else:
                        eng.wait_ge(S[name], START + b * (NT * TILE[name]) + max(n, 0))
                    if apart or eng is nc.sync:
                        eng.sem_inc(S["carrier"], 1)

                with eng.Fori(0, NC) as c:
                    def need(name, n, apart=False):
                        g = b * NC + c
                        if name in PREP:
                            eng.wait_ge(S[name], START + g * PREP[name] + max(n, 0))
                        else:
                            eng.wait_ge(S[name], START + b * (NT * TILE[name]))
                        if apart or eng is nc.sync:
                            eng.sem_inc(S["carrier"], 1)
                    prep(need, b, c)
                tile(lambda name, n, apart=False: tiles_need(name, n, apart), b, 0, True)
                with eng.Fori(1, NT) as n:
                    def later(name, k, apart=False):
                        if name in PREP:
                            eng.wait_ge(S[name], START + (b + 1) * (NC * PREP[name]))
                        else:
                            eng.wait_ge(S[name], START + (b * NT + n) * TILE[name] + k)
                        if apart or eng is nc.sync:
                            eng.sem_inc(S["carrier"], 1)
                    tile(later, b, n, False)
                drain(lambda name, k, apart=False: tiles_need(name, NT * TILE[name] + k, apart), b)

        @block.gpsimd
        def _(pool):
            def tile(need, b, n, first):
                for h in range(H2):
                    if first:
                        need("qlo", None, apart=True)
                    need("s", 2 * (h - H2) + 2, apart=True)
                    nc.gpsimd.tensor_copy(q_now[:, h, :], q_st[:, h, bass.ds(n * P, P)]).then_inc(S["qn"], 1)
                for m in range(0 if first else -1, H2 - 1):
                    normalise(need, m, m % H2)

            def normalise(need, m, h):
                need("exp", 2 * m + 2, apart=True)
                nc.gpsimd.tensor_tensor(rtot[:, h:h + 1], rsum[:, h, 0:1], rsum[:, h, 1:2], ALU.add).then_inc(S["rt"], 1)
                need("rc", m + 1, apart=True)
                p = prob[:, h, :]
                nc.gpsimd.tensor_scalar(p, p, rinv[:, h:h + 1], 1.0, ALU.mult, ALU.mult).then_inc(S["pn"], 1)
            phases(pool, nothing, tile, lambda need, b: normalise(need, -1, H2 - 1))

        @block.scalar
        def _(act):
            def prep(need, b, c):
                for k in range(KD):
                    need("nT", k + 1)
                    nc.scalar.copy(nxT[0][:, k, :], b_t[k][:]).then_inc(S["nhi"], 1)
                for h in range(H2):
                    need("qp", h + 1)
                    nc.scalar.activation(q_st[:, h, bass.ds(c * CH, CH)], b_s[:, h, :], ACT.Copy,
                                         scale=float(DH) ** -0.5).then_inc(S["qhi"], 1)
                need("kp", 1)
                nc.scalar.copy(kk[0][:, bass.ds(c * CH, CH)], b_t[0][:]).then_inc(S["khi"], 1)
                for j in range(2):
                    need("vp", j + 1)
                    nc.scalar.copy(v_st[:, bass.ds(c * CT + 2 * j, 2), 0:DH],
                                   (b_t[1], b_o)[j][:].rearrange("p (t n) -> p t n", t=2)[:, :, 0:DH]).then_inc(S["vhi"], 1)

            def t_hi(need, m, h, j):
                need("t", 4 * m + j + 1)
                need("pv", 4 * (m // 2 - 1) + j + 1)
                nc.scalar.copy(pT[0][:, 4 * j:4 * j + 4, h % 2, :],
                               b_t[j % 2][:].rearrange("p (k n) -> p k n", k=4)).then_inc(S["thi"], 1)

            def o_hi(need, pair, k):
                need("pv", 4 * pair + 4)
                need("y", pair // 2)
                nc.scalar.copy(oT[0][:, 2 * k:2 * k + 2, :],
                               b_o[:, 0:2 * P].rearrange("p (h n) -> p h n", h=2)).then_inc(S["ohi"], 1)

            def exp(need, m, h, j):
                if j == 0:
                    need("t", 4 * (m - H2) + 4)
                    need("nm", m + 1)
                nc.scalar.activation(prob[:, h, HALF * j:HALF * j + HALF],
                                     b_s[:, 2 * j:2 * j + 2, :].rearrange("p a n -> p (a n)"), ACT.Exp,
                                     bias=nmax[:, h:h + 1], scale=1.0, accum_out=rsum[:, h, j:j + 1]).then_inc(S["exp"], 1)

            def tile(need, b, n, first):
                for m in range(H2):
                    evacuate = m >= 2 or not first
                    h = (m - 2) % H2
                    if evacuate:
                        t_hi(need, m - 2, h, 0)
                    if evacuate:
                        t_hi(need, m - 2, h, 1)
                    if evacuate:
                        t_hi(need, m - 2, h, 2)
                    exp(need, m, m, 0)
                    if m % 2 == 0 and not first:
                        o_hi(need, (m - 4) // 2, ((m - 4) // 2) % 2)
                    if evacuate:
                        t_hi(need, m - 2, h, 3)
                    exp(need, m, m, 1)

            def drain(need, b):
                for m in range(0, H2):
                    if m < 2:
                        for j in range(4):
                            t_hi(need, m - 2, (m - 2) % H2, j)
                    if m % 2 == 0:
                        o_hi(need, (m - 4) // 2, ((m - 4) // 2) % 2)
            phases(act, prep, tile, drain)

        @block.vector
        def _(dve):
            def lo(out, psum, hi):
                return nc.vector.tensor_tensor(out, psum, hi.bitcast(F32), ALU.subtract)

            def tokens(g):
                for t in range(CT):
                    at = x2[:, bass.ds(g * CT + t, 1), :].rearrange("p o d -> p (o d)")
                    nc.vector.scalar_tensor_tensor(out=xa[:, t, :], in0=at, scalar=rrms[:, bass.ds(g * CT + t, 1)], in1=g1[:],
                                                   op0=ALU.mult, op1=ALU.mult).then_inc(S["nx"], 1)

            def prep(need, b, c):
                for k in range(KD):
                    need("nhi", k + 1)
                    lo(nxT[1][:, k, :], b_t[k][:], nxT[0][:, k, :]).then_inc(S["nlo"], 1)
                for h in range(H2):
                    if h == 2:
                        need("nT", KD, apart=True)
                        tokens((b * NC + c + 1) & (NG - 1))
                    need("qhi", h + 1)
                    q = q_st[DH:P, h, bass.ds(c * CH, CH)]
                    nc.vector.scalar_tensor_tensor(out=q, in0=b_s[DH:P, h, :], scalar=float(DH) ** -0.5,
                                                   in1=q.bitcast(F32), op0=ALU.mult, op1=ALU.subtract).then_inc(S["qlo"], 1)
                need("khi", 1)
                lo(kk[1][:, bass.ds(c * CH, CH)], b_t[0][:], kk[0][:, bass.ds(c * CH, CH)]).then_inc(S["klo"], 1)
                for j in range(2):
                    need("vhi", j + 1)
                    lo(v_st[:, bass.ds(c * CT + 2 * j, 2), DH:P], (b_t[1], b_o)[j][:].rearrange("p (t n) -> p t n", t=2)[:, :, 0:DH],
                       v_st[:, bass.ds(c * CT + 2 * j, 2), 0:DH]).then_inc(S["vlo"], 1)

            def half_max(need, m, h, j):
                need("s", 2 * m + j + 1)
                nc.vector.tensor_reduce(mx[:, h, j:j + 1], b_s[:, 2 * j:2 * j + 2, :].rearrange("p a n -> p (a n)"),
                                        AX.X, ALU.max).then_inc(S["mxp"], 1)

            def full_max(need, m, h):
                need("mxp", 2 * m + 2)
                nc.vector.tensor_reduce(nmax[:, h:h + 1], mx[:, h, :], AX.X, ALU.max, negate=True).then_inc(S["nm"], 1)

            def sums(need, m, h):
                need("rt", m + 1)
                nc.vector.reciprocal(rinv[:, h:h + 1], rtot[:, h:h + 1]).then_inc(S["rc"], 1)

            def t_lo(need, m, h, j):
                need("thi", 4 * m + j + 1)
                lo(pT[1][:, 4 * j:4 * j + 4, h % 2, :], b_t[j % 2][:].rearrange("p (k n) -> p k n", k=4),
                   pT[0][:, 4 * j:4 * j + 4, h % 2, :]).then_inc(S["tlo"], 1)

            def o_lo(need, pair, k):
                need("ohi", pair + 1)
                lo(oT[1][:, 2 * k:2 * k + 2, :], b_o[:, 0:2 * P].rearrange("p (h n) -> p h n", h=2),
                   oT[0][:, 2 * k:2 * k + 2, :]).then_inc(S["olo"], 1)

            def add_y(need, b, n):
                need("y", 0)
                at = x2[:, bass.ds(b * NT + n, 1), :].rearrange("p o d -> p (o d)")
                nc.vector.tensor_tensor(at, b_y[:, 0:D], at, ALU.add).then_inc(S["res"], 1)

            def tile(need, b, n, first):
                for m in range(H2):
                    evacuate = m >= 2 or not first
                    h = (m - 2) % H2
                    half_max(need, m, m, 0)
                    if evacuate:
                        t_lo(need, m - 2, h, 0)
                    half_max(need, m, m, 1)
                    full_max(need, m, m)
                    if evacuate:
                        t_lo(need, m - 2, h, 1)
                    if m >= 1 or not first:
                        sums(need, m - 1, (m - 1) % H2)
                    if evacuate:
                        t_lo(need, m - 2, h, 2)
                    if m % 2 == 0 and not first:
                        o_lo(need, (m - 4) // 2, ((m - 4) // 2) % 2)
                    if evacuate:
                        t_lo(need, m - 2, h, 3)
                    if m == 3 and not first:
                        add_y(need, b, n - 1)

            def drain(need, b):
                sums(need, -1, H2 - 1)
                for m in range(H2):
                    if m < 2:
                        for j in range(4):
                            t_lo(need, m - 2, (m - 2) % H2, j)
                    if m % 2 == 0:
                        o_lo(need, (m - 4) // 2, ((m - 4) // 2) % 2)
                add_y(need, b, NT - 1)
            tokens(0)
            phases(dve, prep, tile, drain)

        @block.tensor
        def _(pe):

            def product(out, left, right):
                for n, (a, e) in enumerate(SPLIT3):
                    for k in range(KD):
                        x = nc.tensor.matmul(out, left(a, k), right(e, k), start=(n == 0 and k == 0),
                                             stop=(n == 2 and k == KD - 1), skip_group_check=True)
                return x

            def prep(need, b, c):
                need("olo", 0)
                need("tlo", 0)
                need("vlo", 0)
                need("klo", 0)
                for k in range(KD):
                    need("nx", CT)
                    for t in range(CT):
                        x = nc.tensor.transpose(b_t[k][:, P * t:P * t + P], xa[:, t, P * k:P * k + P], ident[:])
                    x.then_inc(S["nT"], 1)
                need("nlo", KD)
                need("exp", 0)
                need("qlo", 0)
                for h in range(H2):
                    product(b_s[:, h, :], lambda a, k: wq[a][:, k, h, :], lambda e, k: nxT[e][:, k, :]).then_inc(S["qp"], 1)
                product(b_t[0][:], lambda a, k: wk[a][:, k, :], lambda e, k: nxT[e][:, k, :]).then_inc(S["kp"], 1)
                for j in range(2):
                    for i in range(2):
                        t = 2 * j + i
                        for n, (a, e) in enumerate(SPLIT3):
                            for k in range(KD):
                                x = nc.tensor.matmul((b_t[1], b_o)[j][:, D * i:D * i + D], nxT[a][:, k, P * t:P * t + P],
                                                     wv[e][:, k, :], start=(i == 0 and n == 0 and k == 0),
                                                     stop=(n == 2 and k == KD - 1), skip_group_check=True)
                    x.then_inc(S["vp"], 1)

            def scores(need, m, h, half, first):
                if half == 0:
                    need("qn", m + 1)
                    if first:
                        need("klo", None)
                        need("qlo", None)
                need("exp", 2 * m - 1 + half)
                for j in (2 * half, 2 * half + 1):
                    for w in range(2):
                        x = nc.tensor.matmul(b_s[:, j, :], q_now[:, h, :], kk[w][:, 512 * j:512 * j + 512],
                                             start=(w == 0), stop=(w == 1))
                x.then_inc(S["s"], 1)

            def transposes(need, m, h, j, first):
                if j == 0:
                    need("pn", m + 1)
                need("tlo", 4 * m + j - 1)
                if first:
                    need("vlo", None)
                for k in range(4 * j, 4 * j + 4):
                    x = nc.tensor.transpose(b_t[j % 2][:, P * (k % 4):P * (k % 4) + P], prob[:, h, P * k:P * k + P], ident[:])
                x.then_inc(S["t"], 1)

            def pv(need, pair, j):
                need("tlo", 8 * pair + 4 + j + 1)
                if j == 0:
                    need("olo", pair)
                for k in range(4 * j, 4 * j + 4):
                    for w in range(2):
                        x = nc.tensor.matmul(b_o[:, 0:2 * P], v_st[:, k, :], pT[w][:, k, :, :].rearrange("p h n -> p (h n)"),
                                             start=(k == 0 and w == 0), stop=(k == KT - 1 and w == 1))
                x.then_inc(S["pv"], 1)

            def out_proj(need):
                need("olo", 0)
                need("res", -1)
                for h in range(H2):
                    for n, (a, e) in enumerate(SPLIT3):
                        x = nc.tensor.matmul(b_y[:, 0:D], oT[a][:, h, :], wo[e][:, h, :], start=(h == 0 and n == 0),
                                             stop=(h == H2 - 1 and n == 2))
                x.then_inc(S["y"], 1)

            def tile(need, b, n, first):
                for m in range(H2):
                    turn = m >= 2 or not first
                    h = (m - 2) % H2
                    even = m % 2 == 0
                    scores(need, m, m, 0, first and m == 0)
                    if turn:
                        transposes(need, m - 2, h, 0, first and m == 2)
                    if even and not first:
                        pv(need, (m - 4) // 2, 2)
                    scores(need, m, m, 1, False)
                    if turn:
                        transposes(need, m - 2, h, 1, False)
                    if even and not first:
                        pv(need, (m - 4) // 2, 3)
                    if turn and not even:
                        pv(need, (m - 3) // 2, 0)
                    if m == 3 and not first:
                        out_proj(need)
                    if turn:
                        transposes(need, m - 2, h, 2, False)
                    if turn and not even:
                        pv(need, (m - 3) // 2, 1)
                    if turn:
                        transposes(need, m - 2, h, 3, False)

            def drain(need, b):
                for m in range(3):
                    if m % 2 == 0:
                        pv(need, (m - 4) // 2, 2)
                        pv(need, (m - 4) // 2, 3)
                    if m < 2:
                        for j in range(4):
                            transposes(need, m - 2, m - 2 + H2, j, False)
                    if m == 1:
                        pv(need, -1, 0)
                        pv(need, -1, 1)
                out_proj(need)
            phases(pe, prep, tile, drain)


def experts(nc, sems, A, x1, x2, out):
    NX = NE + 1
    TT = TOK // P
    with ExitStack() as ctx:
        sb = lambda n, s, d: ctx.enter_context(nc.sbuf_tensor("ex_" + n, s, d))
        bc = sb("bc", [P, 1, NB, D], F32)
        gate_size = sb("gate_size", [P, NB, D], F32)
        ident = sb("ident", [P, P], F32)
        g2 = sb("g2", [P, D], F32)
        bias = sb("bias", [P, NE], F32)
        rank = sb("rank", [P, NE], F32)
        wr = [sb(f"wr{s}", [P, KD, P], F32R) for s in ("hi", "lo")]
        rrms = sb("rrms", [P, TT], F32)
        with ExitStack() as c2:
            raw = c2.enter_context(nc.sbuf_tensor("ex_raw", [P, KD * P], F32))
            s_id, s_in, s_g, s_rank = (sems.take("ex0_" + n) for n in ("id", "in", "g", "rank"))
            load, mscalar, mtensor, mvector, (s_bc, n_bc) = modulation_rows(nc, sems, "ex0_", c2, A, (5,), bc, (False,))
            wload, wscalar, wvector = split_weights(nc, sems, "ex0_w", [
                ([(A["wr16"], raw[:])], raw[:], *[w[:].rearrange("p k n -> p (k n)") for w in wr])])
            s_sq, s_sq2, s_ms, s_root, s_rs, s_nwt = (sems.take("ex0_" + n) for n in ("sq", "sq2", "ms", "root", "rs", "nwt"))
            square = c2.enter_context(nc.sbuf_tensor("ex0_square", [P, 2, D], F32))
            ms, newton = (c2.enter_context(nc.sbuf_tensor("ex0_" + n, [P, TT], F32)) for n in ("ms", "newton"))
            block = c2.enter_context(nc.Block())

            @block.sync
            def _(sp):
                load(sp)
                wload(sp)
                sp.dma_start(g2[:], A["g2"].to_broadcast([P, D])).then_inc(s_in, 16)
                sp.dma_start(bias[:], A["bias"].to_broadcast([P, NE])).then_inc(s_in, 16)
                sp.wait_ge(s_in, 32)

            @block.scalar
            def _(act):
                for k in range(TT // 2):
                    if k:
                        act.wait_ge(s_sq, k)
                    nc.scalar.activation(square[:, 0, :], x2[:, k, :], ACT.Square, accum_out=ms[:, k:k + 1]).then_inc(s_sq, 1)
                act.wait_ge(s_ms, 1)
                nc.scalar.activation(rrms[:], ms[:], ACT.Sqrt).then_inc(s_root, 1)
                mscalar(act)
                wscalar(act)

            @block.vector
            def _(dve):
                for k in range(TT // 2, TT):
                    if k > TT // 2:
                        dve.wait_ge(s_sq2, k - TT // 2)
                    nc.vector.tensor_tensor_reduce(square[:, 1, :], x2[:, k, :], x2[:, k, :], 1.0, 0.0, ALU.mult, ALU.add,
                                                   ms[:, k:k + 1]).then_inc(s_sq2, 1)
                dve.wait_ge(s_sq, TT // 2)
                dve.wait_ge(s_sq2, TT // 2)
                nc.vector.tensor_scalar(ms[:], ms[:], 1.0 / D, EPS_RMS, ALU.mult, ALU.add).then_inc(s_ms, 1)
                dve.wait_ge(s_root, 1)
                nc.vector.reciprocal(rrms[:], rrms[:]).then_inc(s_rs, 1)
                dve.wait_ge(s_rs, 1)
                newton_rsqrt(nc, dve, rrms[:], ms[:], newton[:], lambda k: dve.wait_ge(s_nwt, k), s_nwt)
                mvector(dve)
                wvector(dve)
                dve.wait_ge(s_bc, n_bc)
                floor_gate(nc, dve, bc[:, 0, :, :], gate_size[:], s_g)

            @block.tensor
            def _(pe):
                mtensor(pe)

            @block.gpsimd
            def _(pool):
                make_ident(nc, pool, ident, s_id)
                for e in range(NE):
                    nc.gpsimd.memset(rank[:, e:e + 1], float(NE - e)).then_inc(s_rank, 1)
                pool.wait_ge(s_rank, NE)
                pool.wait_ge(s_id, 2)

        xfT = [sb(f"xfT{s}", [P, KD, TOK], F32R) for s in ("hi", "lo")]
        comb = sb("comb", [P, TT, NX], F32)

        with ExitStack() as c2:
            sb2 = lambda n, s, d: c2.enter_context(nc.sbuf_tensor("ro_" + n, s, d))
            xa = sb2("xa", [P, CT, D], F32)
            lgT = sb2("lgT", [P, CH], F32)
            lg = sb2("lg", [P, TT, NE], F32)
            lg2 = sb2("lg2", [P, TT, NE], F32)
            pick = [sb2(f"pick{i}", [P, TT, NE], F32) for i in range(2)]
            top = [sb2(f"top{i}", [P, TT], F32) for i in range(6)]
            b_x = [c2.enter_context(nc.psum_tensor(f"ro_b_x{i}", [P, 512], F32)) for i in range(2)]
            b_l = c2.enter_context(nc.psum_tensor("ro_b_l", [P, 512], F32))
            b_r = c2.enter_context(nc.psum_tensor("ro_b_r", [P, 512], F32))
            PER = dict(nx=CT, xT=KD, xhi=KD, xlo=KD, lg=1, lgc=1, lt=1, lb=1)
            S = {n: sems.take("ro_" + n) for n in [*PER, "carrier", "one"]}
            s_step = sems.take("ro_step")
            s_exp = sems.take("ro_exp")
            begin_counts(nc, [S[n] for n in PER])
            block = c2.enter_context(nc.Block())

            def chunks(eng, body):
                with eng.Fori(0, NG) as g:
                    def need(name, n, apart=False):
                        eng.wait_ge(S[name], START + g * PER[name] + max(n, 0))
                        if apart:
                            eng.sem_inc(S["carrier"], 1)
                    body(need, g)

            wide = lambda a: a.rearrange("p (t o) -> p t o", o=1).to_broadcast([P, TT, NE])

            @block.scalar
            def _(act):
                def body(need, g):
                    for k in range(KD):
                        need("xT", k + 1)
                        nc.scalar.copy(xfT[0][:, k, bass.ds(g * CH, CH)], b_x[k][:]).then_inc(S["xhi"], 1)
                    need("lg", 1)
                    need("lt", 0)
                    nc.scalar.copy(lgT[:], b_l[:]).then_inc(S["lgc"], 1)
                chunks(act, body)
                for j in range(2):
                    act.wait_ge(s_step, (2, 17)[j])
                    a = (lg2[:].rearrange("p t e -> p (t e)"), top[2][:])[j]
                    nc.scalar.activation(a, a, ACT.Exp).then_inc(s_exp, 1)

            @block.gpsimd
            def _(pool):
                nc.gpsimd.memset(comb[:, :, NE:NX], 1.0).then_inc(S["one"], 1)
                pool.wait_ge(S["one"], 1)

            @block.vector
            def _(dve):
                def tokens(g):
                    for t in range(CT):
                        at = x2[:, bass.ds(g * CT + t, 1), :].rearrange("p o d -> p (o d)")
                        nc.vector.scalar_tensor_tensor(out=xa[:, t, :], in0=at, scalar=rrms[:, bass.ds(g * CT + t, 1)],
                                                       in1=g2[:], op0=ALU.mult, op1=ALU.mult).then_inc(S["nx"], 1)

                def body(need, g):
                    for k in range(KD):
                        need("xhi", k + 1)
                        nc.vector.tensor_tensor(xfT[1][:, k, bass.ds(g * CH, CH)], b_x[k][:],
                                                xfT[0][:, k, bass.ds(g * CH, CH)].bitcast(F32), ALU.subtract).then_inc(S["xlo"], 1)
                    need("xT", KD, apart=True)
                    tokens((g + 1) & (NG - 1))
                    need("lt", 1)
                    nc.vector.tensor_tensor(lg[:, bass.ds(g * CT, CT), :], b_r[:].rearrange("p (t n) -> p t n", t=CT)[:, :, 0:NE],
                                            bias[:].rearrange("p (o e) -> p o e", o=1).to_broadcast([P, CT, NE]),
                                            ALU.add).then_inc(S["lb"], 1)
                tokens(0)
                chunks(dve, body)

                at = [0]

                def step(x):
                    at[0] += 1
                    x.then_inc(s_step, 1)
                    dve.wait_ge(s_step, at[0])
                dve.wait_ge(S["lb"], START + NG)
                v = nc.vector
                step(v.tensor_reduce(top[0][:], lg[:], AX.X, ALU.max))
                step(v.tensor_tensor(lg2[:], lg[:], wide(top[0][:]), ALU.subtract))
                dve.wait_ge(s_exp, 1)
                step(v.tensor_reduce(top[0][:], lg2[:], AX.X, ALU.add))
                step(v.reciprocal(top[0][:], top[0][:]))
                step(v.tensor_tensor(lg[:], lg2[:], wide(top[0][:]), ALU.mult))
                for i in range(2):
                    step(v.tensor_reduce(top[i][:], lg[:], AX.X, ALU.max))
                    step(v.tensor_tensor(pick[i][:], lg[:], wide(top[i][:]), ALU.is_equal))
                    step(v.tensor_tensor(pick[i][:], pick[i][:],
                                         rank[:].rearrange("p (o e) -> p o e", o=1).to_broadcast([P, TT, NE]), ALU.mult))
                    step(v.tensor_reduce(top[4][:], pick[i][:], AX.X, ALU.max))
                    step(v.tensor_tensor(pick[i][:], pick[i][:], wide(top[4][:]), ALU.is_equal))
                    if i == 0:
                        step(v.scalar_tensor_tensor(out=lg[:], in0=pick[0][:], scalar=-4.0, in1=lg[:], op0=ALU.mult, op1=ALU.add))
                step(v.tensor_tensor(top[2][:], top[1][:], top[0][:], ALU.subtract))
                assert at[0] == 17, at
                dve.wait_ge(s_exp, 2)
                step(v.tensor_scalar(top[3][:], top[2][:], 1.0, None, ALU.add))
                step(v.reciprocal(top[3][:], top[3][:]))
                step(v.tensor_tensor(top[2][:], top[2][:], top[3][:], ALU.mult))
                for i in range(2):
                    step(v.tensor_tensor(pick[i][:], pick[i][:], wide(top[3 - i][:]), ALU.mult))
                step(v.tensor_tensor(comb[:, :, 0:NE], pick[0][:], pick[1][:], ALU.add))

            @block.tensor
            def _(pe):

                def body(need, g):
                    need("nx", CT)
                    need("xlo", 0)
                    for k in range(KD):
                        for t in range(CT):
                            x = nc.tensor.transpose(b_x[k][:, P * t:P * t + P], xa[:, t, P * k:P * k + P], ident[:])
                        x.then_inc(S["xT"], 1)
                    need("xlo", KD)
                    need("lgc", 0)
                    for n, (a, e) in enumerate(SPLIT3):
                        for k in range(KD):
                            x = nc.tensor.matmul(b_l[:], wr[a][:, k, :], xfT[e][:, k, bass.ds(g * CH, CH)],
                                                 start=(n == 0 and k == 0), stop=(n == 2 and k == KD - 1))
                    x.then_inc(S["lg"], 1)
                    need("lgc", 1)
                    need("lb", 0)
                    for t in range(CT):
                        x = nc.tensor.transpose(b_r[:, P * t:P * t + P], lgT[:, P * t:P * t + P], ident[:])
                    x.then_inc(S["lt"], 1)
                chunks(pe, body)

        raw = sb("raw_w", [P, 3 * KD, FF], F32)
        w13 = [[sb(f"w13_{i}{s}", [P, 2 * KD, FF], F32R) for s in ("hi", "lo")] for i in range(2)]
        w2 = [[sb(f"w2_{i}{s}", [P, KF, D], F32R) for s in ("hi", "lo")] for i in range(2)]
        act_f = sb("act_f", [P, KF, CH], F32)
        hid = sb("hid", [P, KF, CH], F32)
        hT = [[sb(f"hT_{i}{s}", [P, KF, CH], F32R) for s in ("hi", "lo")] for i in range(2)]
        x_res = sb("x_res", [P, 2, CT, D], F32)
        b_g = [ctx.enter_context(nc.psum_tensor(f"ex_b_g{i}", [P, 512], F32)) for i in range(KF)]
        b_u = [ctx.enter_context(nc.psum_tensor(f"ex_b_u{i}", [P, 512], F32)) for i in range(KF)]
        b_y = [ctx.enter_context(nc.psum_tensor(f"ex_b_y{i}", [P, 512], F32)) for i in range(4)]

        STEP = dict(g=KF, u=KF, sil=KF, hm=KF, hhi=KF, hlo=KF, y=CT, acc=CT)
        LOAD = dict(w=16, whi=2, wlo=2)
        LAST = dict(xr=16, fg=CT, fa=1, out=16)
        S = {n: sems.take("ex_" + n) for n in [*STEP, *LOAD, *LAST, "carrier"]}
        begin_counts(nc, [S[n] for n in (*STEP, *LOAD, *LAST)])
        block = ctx.enter_context(nc.Block())

        def run(eng, load, begin, step, last):
            def needs(order, s):
                def need(name, n, apart=False):
                    value = s * STEP[name] + n if name in STEP else order * LOAD[name] + n
                    if isinstance(value, int) and value <= 0:
                        return
                    eng.wait_ge(S[name], START + value)
                    if apart or eng is nc.sync:
                        eng.sem_inc(S["carrier"], 1)
                return need

            def expert(order, w, number, before, following):
                begin(needs(order, order * NG))
                step(needs(order, order * NG), w, number, 0, 0)
                if before is not None:
                    last(needs(order, order * NG), 1 - w, before, NG - 1, 1)
                step(needs(order, order * NG + 1), w, number, 1, 1)
                last(needs(order, order * NG + 1), w, number, 0, 0)
                load(needs(order + 1, order * NG + 2), 1 - w, following)
                with eng.Fori(1, NG // 2) as gg:
                    for par in range(2):
                        g = 2 * gg + par
                        step(needs(order, order * NG + g), w, number, g, par)
                        last(needs(order, order * NG + g), w, number, g - 1, 1 - par)

            load(needs(0, 0), 1, NE)
            expert(0, 1, NE, None, 0)
            expert(1, 0, 0, NE, 1)
            expert(2, 1, 1, 0, 2)
            with eng.Fori(1, NE // 2) as pair:
                expert(1 + 2 * pair, 0, 2 * pair, 2 * pair - 1, 2 * pair + 1)
                expert(2 + 2 * pair, 1, 2 * pair + 1, 2 * pair, 2 * pair + 2)
            last(needs(NX, NX * NG), 1, NE - 1, NG - 1, 1)

        nothing = lambda *a: None

        @block.sync
        def _(sp):
            def load(need, w, which):
                need("whi", 0)
                need("wlo", 0)
                sp.dma_start(raw[:], A["experts"][:, bass.ds(which, 1), :, :].rearrange("p o k n -> p (o k) n")).then_inc(S["w"], 16)
            run(sp, load, nothing, nothing, nothing)

            def load_x(g, par):
                sp.dma_start(x_res[:, par, :, :], x1[:, bass.ds(g * CT, CT), :]).then_inc(S["xr"], 16)
            load_x(0, 0)
            with sp.Fori(0, NG // 2) as gg:
                for par in range(2):
                    g = 2 * gg + par
                    if par == 0:
                        sp.wait_ge(S["out"], START + g * 16)
                        sp.wait_ge(S["xr"], START + (g + 1) * 16)
                        sp.sem_inc(S["carrier"], 1)
                        load_x(g + 1, 1)
                    else:
                        sp.wait_ge(S["out"], START + g * 16)
                        sp.wait_ge(S["xr"], START + (g + 1) * 16)
                        sp.sem_inc(S["carrier"], 1)
                        load_x((g + 1) & (NG - 1), 0)
                    sp.wait_ge(S["fa"], START + g + 1)
                    sp.sem_inc(S["carrier"], 1)
                    sp.dma_start(out[:, bass.ds(g * CT, CT), :], x_res[:, par, :, :]).then_inc(S["out"], 16)
            sp.wait_ge(S["xr"], START + (NG + 1) * 16)
            sp.wait_ge(S["out"], START + NG * 16)
            sp.wait_ge(S["w"], START + 16 * (NX + 1))

        @block.scalar
        def _(act):
            def load(need, w, which):
                need("w", 16)
                need("y", -2 * CT)
                nc.scalar.copy(w13[w][0][:], raw[:, 0:2 * KD, :]).then_inc(S["whi"], 1)
                nc.scalar.copy(w2[w][0][:], raw[:, 2 * KD:3 * KD, :]).then_inc(S["whi"], 1)

            def step(need, w, number, g, par):
                for f in range(KF):
                    need("g", f + 1)
                    need("hm", 0)
                    nc.scalar.activation(act_f[:, f, :], b_g[f][:], ACT.Silu).then_inc(S["sil"], 1)
                need("y", -CT)
                for f in range(KF):
                    need("hm", f + 1)
                    nc.scalar.copy(hT[par][0][:, f, :], hid[:, f, :]).then_inc(S["hhi"], 1)
            run(act, load, nothing, step, nothing)

        @block.gpsimd
        def _(pool):
            def step(need, w, number, g, par):
                for f in range(KF):
                    need("hhi", f + 1, apart=True)
                    nc.gpsimd.tensor_tensor(hT[par][1][:, f, :], hid[:, f, :], hT[par][0][:, f, :].bitcast(F32),
                                            ALU.subtract).then_inc(S["hlo"], 1)
            run(pool, nothing, nothing, step, nothing)

        @block.vector
        def _(dve):
            def load(need, w, which):
                need("whi", 1)
                nc.vector.tensor_tensor(w13[w][1][:], raw[:, 0:2 * KD, :], w13[w][0][:].bitcast(F32), ALU.subtract).then_inc(S["wlo"], 1)
                need("whi", 2)
                nc.vector.tensor_tensor(w2[w][1][:], raw[:, 2 * KD:3 * KD, :], w2[w][0][:].bitcast(F32), ALU.subtract).then_inc(S["wlo"], 1)

            def step(need, w, number, g, par):
                for f in range(KF):
                    need("u", f + 1)
                    need("sil", f + 1)
                    need("hlo", 0)
                    nc.vector.tensor_tensor(hid[:, f, :], b_u[f][:], act_f[:, f, :], ALU.mult).then_inc(S["hm"], 1)

            def last(need, w, number, g, par):
                for t in range(CT):
                    need("y", t + 1 - CT)
                    at = x2[:, bass.ds(g * CT + t, 1), :].rearrange("p o d -> p (o d)")
                    c = comb[:, bass.ds(g * CT + t, 1), bass.ds(number, 1)].rearrange("p o n -> p (o n)")
                    nc.vector.scalar_tensor_tensor(out=at, in0=b_y[t][:, 0:D], scalar=c, in1=at, op0=ALU.mult,
                                                   op1=ALU.add).then_inc(S["acc"], 1)
            run(dve, load, nothing, step, last)
            dve.wait_ge(S["acc"], START + NX * NG * CT)
            with dve.Fori(0, NG // 2) as gg:
                for par in range(2):
                    g = 2 * gg + par
                    b = (g >> (NC.bit_length() - 1)) & (NB - 1)
                    for t in range(CT):
                        at = x2[:, bass.ds(g * CT + t, 1), :].rearrange("p o d -> p (o d)")
                        nc.vector.tensor_tensor(at, at, bc[:, 0, bass.ds(b, 1), :].rearrange("p o d -> p (o d)"),
                                                ALU.mult).then_inc(S["fg"], 1)
                    dve.wait_ge(S["xr"], START + (g + 1) * 16)
                    dve.wait_ge(S["fg"], START + (g + 1) * CT)
                    nc.vector.tensor_tensor(x_res[:, par, :, :], x_res[:, par, :, :], x2[:, bass.ds(g * CT, CT), :],
                                            ALU.add).then_inc(S["fa"], 1)

        @block.tensor
        def _(pe):

            def begin(need):
                need("wlo", 2)

            def step(need, w, number, g, par):
                for f in range(KF):
                    for bank, m, free in ((b_g[f], 0, "sil"), (b_u[f], 1, "hm")):
                        need(free, 0)
                        for n, (a, e) in enumerate(SPLIT3):
                            for k in range(KD):
                                x = nc.tensor.matmul(bank[:], w13[w][a][:, KD * m + k, P * f:P * f + P],
                                                     xfT[e][:, k, bass.ds(g * CH, CH)],
                                                     start=(n == 0 and k == 0), stop=(n == 2 and k == KD - 1))
                        x.then_inc(S["gu"[m]], 1)

            def last(need, w, number, g, par):
                need("hlo", 0)
                for t in range(CT):
                    need("acc", -CT)
                    for n, (a, e) in enumerate(SPLIT3):
                        for k in range(KF):
                            x = nc.tensor.matmul(b_y[t][:, 0:D], hT[par][a][:, k, P * t:P * t + P], w2[w][e][:, k, :],
                                                 start=(n == 0 and k == 0), stop=(n == 2 and k == KF - 1))
                    x.then_inc(S["y"], 1)
            run(pe, nothing, begin, step, last)


def lay_out(I):
    import numpy as np
    a = lambda n: np.asarray(I["L0_" + n])
    kp = lambda w: np.ascontiguousarray(w.reshape(-1, P, w.shape[-1]).transpose(1, 0, 2))
    out = {}
    out["wqkv"] = kp(np.concatenate([a("attn_Wq"), a("attn_Wk"), a("attn_Wv")], axis=1))
    out["wo"] = np.ascontiguousarray(a("attn_Wo").reshape(H1, DH, D).transpose(1, 0, 2))
    out["cT"] = kp(np.ascontiguousarray(a("c").T))
    twice = lambda w, n=2: np.concatenate([w] * n, axis=-1)
    wq2 = np.ascontiguousarray(a("ffn_Wq").T).reshape(D, H2, DH)
    out["wq2"] = kp(np.ascontiguousarray(twice(wq2)).reshape(D, H2 * P)).reshape(P, -1)
    out["wk2"] = kp(twice(np.ascontiguousarray(a("ffn_Wkc").T))).reshape(P, -1)
    out["wv2"] = kp(twice(np.ascontiguousarray(a("ffn_Wvc").T), 4)).reshape(P, -1)
    out["wo2"] = np.ascontiguousarray(a("ffn_Wo").T.reshape(H2, DH, D).transpose(1, 0, 2)).reshape(DH, -1)
    fc = lambda w: kp(np.ascontiguousarray(w.T))
    pack = lambda w1, w3, w2: np.concatenate([fc(w1), fc(w3), fc(w2)], axis=1)
    each = [pack(a("ffn_eW1")[e], a("ffn_eW3")[e], a("ffn_eW2")[e]) for e in range(NE)]
    each.append(pack(a("ffn_sW1"), a("ffn_sW3"), a("ffn_sW2")))
    out["experts"] = np.ascontiguousarray(np.stack(each, axis=1))
    out["wr16"] = kp(twice(np.ascontiguousarray(a("ffn_Wr").T), P // NE)).reshape(P, -1)
    out["bias"] = a("ffn_expert_bias").reshape(1, NE)
    out["g1"] = a("ffn_g1").reshape(1, D)
    out["g2"] = a("ffn_g2").reshape(1, D)
    out["wmod"] = np.ascontiguousarray(kp(a("wmod")).reshape(P, KD, 6, D))
    return out


def program(nc, x, arrays, out):
    A = arrays
    x1 = nc.dram_tensor("x1_scratch", [P, TOK // P, D], F32).ap()
    by_tile = lambda a: a.rearrange("b (t p) d -> p (b t) d", p=P)
    A["x"] = by_tile(x)
    with PhaseSemaphores(nc) as sems:
        windowed_attention(nc, sems, A, x1)
    with nc.sbuf_tensor("x2_resident", [P, TOK // P, D], F32) as x2:
        with PhaseSemaphores(nc) as sems:
            latent_attention(nc, sems, A, x1, x2)
        with PhaseSemaphores(nc) as sems:
            experts(nc, sems, A, x1, x2, by_tile(out))


def kernel(**inputs):
    import numpy as np
    import concourse.bacc as bacc
    from concourse.bass_utils import run_bass_kernel_spmd

    nc = bacc.Bacc("TRN2", target_bir_lowering=False, num_devices=1)
    arrays = {f"in_{k}": v for k, v in lay_out(inputs).items()}
    arrays["in_x"] = np.ascontiguousarray(inputs["L0_attn_x"])
    aps = {k[3:]: nc.dram_tensor(k, a.shape, mybir.dt.from_np(a.dtype), kind="ExternalInput").ap()
           for k, a in arrays.items()}
    out = nc.dram_tensor("out_x", (NB, SEQ, D), F32, kind="ExternalOutput").ap()
    program(nc, aps.pop("x"), aps, out)
    return run_bass_kernel_spmd(nc, [arrays], core_ids=[0]).results[0]["out_x"]
```
